# Optimizing a Trainium2 kernel written in Bass

```python
import numpy as np
import jax
import jax.numpy as jnp

def _softmax(x, axis=-1):
    return jax.nn.softmax(x, axis=axis)

def _gelu(x):
    return jax.nn.gelu(x, approximate=True)

def _silu(x):
    return jax.nn.silu(x)

def _sigmoid(x):
    return jax.nn.sigmoid(x)

def _layernorm(x, axis=-1, eps=1e-05):
    m = jnp.mean(x, axis=axis, keepdims=True)
    v = jnp.var(x, axis=axis, keepdims=True)
    return (x - m) / jnp.sqrt(v + eps)

def _scatter_add(tgt, idx, src, axis=0):
    return tgt.at[idx].add(src)

def _segment_sum(src, seg, n):
    return jax.ops.segment_sum(src, seg, n)
kernel_name = 'mk_flamingo_gated_d2_seqx_r4_1c288c'

def setup_inputs(seed: int=0):
    np.random.seed(seed)
    _w = jnp.asarray

    def _rec_inputs():
        import jax
        import jax.numpy as jnp
        _rk = jax.random.key(seed)
        x = -0.0005146 + 1 * jax.random.normal(jax.random.fold_in(_rk, 1), (2, 512, 256), jnp.float32)
        _lenS = 512 - jax.random.randint(jax.random.fold_in(_rk, 7), (2,), 0, max(1, 512 // 4) + 1, jnp.int32)
        _lenS2 = 1024 - jax.random.randint(jax.random.fold_in(_rk, 8), (2,), 0, max(1, 1024 // 4) + 1, jnp.int32)
        _ctx_768P = jax.random.normal(jax.random.fold_in(_rk, 11), (2, 16, 192), jnp.float32)
        _ctx_768c = jax.random.dirichlet(jax.random.fold_in(_rk, 511), 0.3 * jnp.ones((16,), jnp.float32), (2, 1024))
        _ctx_768t = jnp.einsum('bsk,bkd->bsd', _ctx_768c, _ctx_768P)
        _ctx_768t = _ctx_768t * jax.lax.rsqrt(jnp.mean(jnp.square(_ctx_768t)) + 1e-12) * 0.953939
        ctx_768 = -0.00040386 + 0.999972 * (_ctx_768t + 0.3 * jax.random.normal(jax.random.fold_in(_rk, 611), (2, 1024, 192), jnp.float32))
        _validS = jnp.arange(512)[None, :] < _lenS[:, None]
        _validS2 = jnp.arange(1024)[None, :] < _lenS2[:, None]
        _causal = jnp.tril(jnp.ones((512, 512), dtype=bool))
        mask_BxS2_bk0 = jnp.logical_not(jnp.broadcast_to(_validS2[:, :], (2, 1024)))
        _g = jax.random.normal(jax.random.fold_in(_rk, 9001), (2, 2), jnp.float32)
        _g = jnp.sign(_g) * jnp.maximum(jnp.abs(_g), 1.0) + (_g == 0) * 1.0
        g_xattn = _g[0]
        g_ffn = _g[1]
        return (x, ctx_768, mask_BxS2_bk0, g_xattn, g_ffn)
    x, ctx_768, mask_BxS2_bk0, g_xattn, g_ffn = _rec_inputs()

    def _L0_xattn_setup():
        import jax, jax.numpy as jnp
        import numpy as np
        DIM_IN, DIM_LAT, DIM_HEAD = (192, 256, 64)
        INNER = max(DIM_LAT, DIM_IN)
        HEADS = INNER // DIM_HEAD
        SCALE = DIM_HEAD ** (-0.5)
        RMS_EPS = 1e-08
        LN_EPS = 1e-05

        def layernorm(x, g, b):
            mu = jnp.mean(x, axis=-1, keepdims=True)
            var = jnp.mean((x - mu) ** 2, axis=-1, keepdims=True)
            return (x - mu) * jax.lax.rsqrt(var + LN_EPS) * g + b

        def rmsnorm(x, gamma):
            norm = jnp.sqrt(jnp.sum(x * x, axis=-1, keepdims=True)) * x.shape[-1] ** (-0.5)
            return x / jnp.maximum(norm, RMS_EPS) * gamma
        key = jax.random.key(seed)
        ks = jax.random.split(key, 12)
        b, n, m = (4, 1024, 128)
        x = jax.random.normal(ks[0], (b, n, DIM_IN), jnp.float32)
        latents = jax.random.normal(ks[1], (b, m, DIM_LAT), jnp.float32)
        mask = jax.random.randint(ks[2], (b, n), 0, 2).astype(bool)
        s = lambda k, sh, fan: jax.random.normal(k, sh, jnp.float32) * fan ** (-0.5)
        return {'x': x, 'latents': latents, 'mask': mask, 'ln_x_g': jnp.ones((DIM_IN,), jnp.float32), 'ln_x_b': jnp.zeros((DIM_IN,), jnp.float32), 'ln_l_g': jnp.ones((DIM_LAT,), jnp.float32), 'ln_l_b': jnp.zeros((DIM_LAT,), jnp.float32), 'qn_g': jnp.ones((DIM_HEAD,), jnp.float32), 'kn_g': jnp.ones((DIM_HEAD,), jnp.float32), 'Wq': s(ks[3], (INNER, DIM_LAT), DIM_LAT), 'Wkv': s(ks[4], (2 * INNER, DIM_IN), DIM_IN), 'Wlkv': s(ks[5], (2 * INNER, DIM_LAT), DIM_LAT), 'Wo': s(ks[6], (DIM_LAT, INNER), INNER), 'bo': jnp.zeros((DIM_LAT,), jnp.float32)}
    _L0_xattn_all = _L0_xattn_setup()
    _L0_xattn_in = {k: v for k, v in _L0_xattn_all.items() if k in ('ln_x_g', 'ln_x_b', 'ln_l_g', 'ln_l_b', 'qn_g', 'kn_g', 'Wq', 'Wkv', 'Wlkv', 'Wo', 'bo')}
    del _L0_xattn_all

    def _L0_ffn_setup():
        import jax, jax.numpy as jnp
        import numpy as np
        import math
        D_IN = 256
        FEATURES = (1024, 1024, 256)
        BATCH, SEQ = (8, 512)

        def _conn_dense(kernel_bool, x):
            w = jnp.where(kernel_bool, jnp.float32(1.0), jnp.float32(-1.0))
            return x @ w
        key = jax.random.key(seed)
        kx, kk0, kk1, kk2 = jax.random.split(key, 4)
        x = jax.random.normal(kx, (BATCH, SEQ, D_IN), dtype=jnp.float32)
        k0 = jax.random.randint(kk0, (2 * D_IN, FEATURES[0]), 0, 2).astype(jnp.bool_)
        k1 = jax.random.randint(kk1, (FEATURES[0], FEATURES[1]), 0, 2).astype(jnp.bool_)
        k2 = jax.random.randint(kk2, (FEATURES[1], FEATURES[2]), 0, 2).astype(jnp.bool_)
        s0 = jnp.asarray(1.0 / math.sqrt(2 * D_IN), dtype=jnp.float32)
        s1 = jnp.asarray(1.0 / math.sqrt(FEATURES[0]), dtype=jnp.float32)
        s2 = jnp.asarray(1.0 / math.sqrt(FEATURES[1]), dtype=jnp.float32)
        return {'x': x, 'k0': k0, 'k1': k1, 'k2': k2, 's0': s0, 's1': s1, 's2': s2}
    _L0_ffn_all = _L0_ffn_setup()
    _L0_ffn_in = {k: v for k, v in _L0_ffn_all.items() if k in ('k0', 'k1', 'k2', 's0', 's1', 's2')}
    del _L0_ffn_all

    def _L1_xattn_setup():
        import jax, jax.numpy as jnp
        import numpy as np
        HEADS = 16
        DIM_HEAD = 64
        key = jax.random.key(seed)
        ks = jax.random.split(key, 8)
        B, S, D = (16, 1024, 256)
        K, DE = (77, 192)
        inner = HEADS * DIM_HEAD
        hidden_states = jax.random.normal(ks[0], (B, S, D), dtype=jnp.float32)
        encoder_hidden_states = jax.random.normal(ks[1], (B, K, DE), dtype=jnp.float32)
        sc_q = 1.0 / np.sqrt(D)
        sc_kv = 1.0 / np.sqrt(DE)
        sc_o = 1.0 / np.sqrt(inner)
        Wq = jax.random.normal(ks[2], (D, inner), dtype=jnp.float32) * sc_q
        Wk = jax.random.normal(ks[3], (DE, inner), dtype=jnp.float32) * sc_kv
        Wv = jax.random.normal(ks[4], (DE, inner), dtype=jnp.float32) * sc_kv
        Wo = jax.random.normal(ks[5], (inner, D), dtype=jnp.float32) * sc_o
        bo = jax.random.normal(ks[6], (D,), dtype=jnp.float32) * 0.01
        return {'hidden_states': hidden_states, 'encoder_hidden_states': encoder_hidden_states, 'Wq': Wq, 'Wk': Wk, 'Wv': Wv, 'Wo': Wo, 'bo': bo}
    _L1_xattn_all = _L1_xattn_setup()
    _L1_xattn_in = {k: v for k, v in _L1_xattn_all.items() if k in ('Wq', 'Wk', 'Wv', 'Wo', 'bo')}
    del _L1_xattn_all

    def _L1_ffn_setup():
        import jax, jax.numpy as jnp
        import numpy as np
        B, S, H = (1, 512, 256)
        E = 16
        I = 192
        TOPK = 4
        G = 4
        TOPK_G = 2
        SCALE = 2.5
        N_SHARED = 1

        def _route(x, gate_w, gate_bias):
            n = x.shape[0]
            logits = jnp.einsum('nh,eh->ne', x.astype(jnp.float32), gate_w)
            scores = jax.nn.sigmoid(logits)
            sb = scores + gate_bias
            gs = sb.reshape(n, G, E // G)
            group_scores = jnp.sum(jax.lax.top_k(gs, 2)[0], axis=-1)
            _, gidx = jax.lax.top_k(group_scores, TOPK_G)
            gmask = jnp.sum(jax.nn.one_hot(gidx, G, dtype=sb.dtype), axis=1)
            emask = jnp.repeat(gmask, E // G, axis=-1)
            masked = jnp.where(emask > 0, sb, -jnp.inf)
            _, tidx = jax.lax.top_k(masked, TOPK)
            w = jnp.take_along_axis(scores, tidx, axis=1)
            w = w / (jnp.sum(w, axis=-1, keepdims=True) + 1e-20)
            return (tidx, w * SCALE)
        key = jax.random.key(seed)
        ks = jax.random.split(key, 9)

        def rn(k, shape, scale=0.02):
            return jax.random.normal(k, shape, dtype=jnp.float32) * scale
        return dict(hidden_states=jax.random.normal(ks[0], (B, S, H), dtype=jnp.float32), gate_w=rn(ks[1], (E, H)), gate_bias=jax.random.normal(ks[2], (E,), dtype=jnp.float32) * 0.1, w1=rn(ks[3], (E, I, H)), w2=rn(ks[4], (E, H, I)), w3=rn(ks[5], (E, I, H)), ws1=rn(ks[6], (I * N_SHARED, H)), ws2=rn(ks[7], (H, I * N_SHARED)), ws3=rn(ks[8], (I * N_SHARED, H)))
    _L1_ffn_all = _L1_ffn_setup()
    _L1_ffn_in = {k: v for k, v in _L1_ffn_all.items() if k in ('gate_w', 'gate_bias', 'w1', 'w2', 'w3', 'ws1', 'ws2', 'ws3')}
    del _L1_ffn_all
    return {'x': x, 'ctx_768': ctx_768, 'mask_BxS2_bk0': mask_BxS2_bk0, 'g_xattn': g_xattn, 'g_ffn': g_ffn, 'L0_xattn_ln_x_g': _L0_xattn_in['ln_x_g'], 'L0_xattn_ln_x_b': _L0_xattn_in['ln_x_b'], 'L0_xattn_ln_l_g': _L0_xattn_in['ln_l_g'], 'L0_xattn_ln_l_b': _L0_xattn_in['ln_l_b'], 'L0_xattn_qn_g': _L0_xattn_in['qn_g'], 'L0_xattn_kn_g': _L0_xattn_in['kn_g'], 'L0_xattn_Wq': _L0_xattn_in['Wq'], 'L0_xattn_Wkv': _L0_xattn_in['Wkv'], 'L0_xattn_Wlkv': _L0_xattn_in['Wlkv'], 'L0_xattn_Wo': _L0_xattn_in['Wo'], 'L0_xattn_bo': _L0_xattn_in['bo'], 'L0_ffn_k0': _L0_ffn_in['k0'], 'L0_ffn_k1': _L0_ffn_in['k1'], 'L0_ffn_k2': _L0_ffn_in['k2'], 'L0_ffn_s0': _L0_ffn_in['s0'], 'L0_ffn_s1': _L0_ffn_in['s1'], 'L0_ffn_s2': _L0_ffn_in['s2'], 'L1_xattn_Wq': _L1_xattn_in['Wq'], 'L1_xattn_Wk': _L1_xattn_in['Wk'], 'L1_xattn_Wv': _L1_xattn_in['Wv'], 'L1_xattn_Wo': _L1_xattn_in['Wo'], 'L1_xattn_bo': _L1_xattn_in['bo'], 'L1_ffn_gate_w': _L1_ffn_in['gate_w'], 'L1_ffn_gate_bias': _L1_ffn_in['gate_bias'], 'L1_ffn_w1': _L1_ffn_in['w1'], 'L1_ffn_w2': _L1_ffn_in['w2'], 'L1_ffn_w3': _L1_ffn_in['w3'], 'L1_ffn_ws1': _L1_ffn_in['ws1'], 'L1_ffn_ws2': _L1_ffn_in['ws2'], 'L1_ffn_ws3': _L1_ffn_in['ws3']}

def reference(x, ctx_768, mask_BxS2_bk0, g_xattn, g_ffn, L0_xattn_ln_x_g, L0_xattn_ln_x_b, L0_xattn_ln_l_g, L0_xattn_ln_l_b, L0_xattn_qn_g, L0_xattn_kn_g, L0_xattn_Wq, L0_xattn_Wkv, L0_xattn_Wlkv, L0_xattn_Wo, L0_xattn_bo, L0_ffn_k0, L0_ffn_k1, L0_ffn_k2, L0_ffn_s0, L0_ffn_s1, L0_ffn_s2, L1_xattn_Wq, L1_xattn_Wk, L1_xattn_Wv, L1_xattn_Wo, L1_xattn_bo, L1_ffn_gate_w, L1_ffn_gate_bias, L1_ffn_w1, L1_ffn_w2, L1_ffn_w3, L1_ffn_ws1, L1_ffn_ws2, L1_ffn_ws3):
    import jax
    import jax.numpy as jnp

    def _L0_xattn_ref(x, latents, mask, ln_x_g, ln_x_b, ln_l_g, ln_l_b, qn_g, kn_g, Wq, Wkv, Wlkv, Wo, bo):
        import jax, jax.numpy as jnp
        import numpy as np
        DIM_IN, DIM_LAT, DIM_HEAD = (192, 256, 64)
        INNER = max(DIM_LAT, DIM_IN)
        HEADS = INNER // DIM_HEAD
        SCALE = DIM_HEAD ** (-0.5)
        RMS_EPS = 1e-08
        LN_EPS = 1e-05

        def layernorm(x, g, b):
            mu = jnp.mean(x, axis=-1, keepdims=True)
            var = jnp.mean((x - mu) ** 2, axis=-1, keepdims=True)
            return (x - mu) * jax.lax.rsqrt(var + LN_EPS) * g + b

        def rmsnorm(x, gamma):
            norm = jnp.sqrt(jnp.sum(x * x, axis=-1, keepdims=True)) * x.shape[-1] ** (-0.5)
            return x / jnp.maximum(norm, RMS_EPS) * gamma
        b, n, _ = x.shape
        m = latents.shape[1]
        xn = layernorm(x, ln_x_g, ln_x_b)
        ln = layernorm(latents, ln_l_g, ln_l_b)
        q = ln @ Wq.T
        kv = jnp.concatenate([xn @ Wkv.T, ln @ Wlkv.T], axis=1)
        k, v = (kv[..., :INNER], kv[..., INNER:])
        split_heads = lambda t: t.reshape(t.shape[0], t.shape[1], HEADS, DIM_HEAD).transpose(0, 2, 1, 3)
        q, k, v = (split_heads(q), split_heads(k), split_heads(v))
        qn = rmsnorm(q, qn_g) * SCALE
        kn = rmsnorm(k, kn_g)
        attn = jnp.einsum('bhid,bhjd->bhij', qn, kn)
        full_mask = jnp.pad(mask, ((0, 0), (0, m)), constant_values=True)
        attn = jnp.where(full_mask[:, None, None, :], attn, -jnp.finfo(attn.dtype).max)
        attn = jax.nn.softmax(attn, axis=-1)
        out = jnp.einsum('bhij,bhjd->bhid', attn, v)
        out = out.transpose(0, 2, 1, 3).reshape(b, m, INNER)
        return out @ Wo.T + bo

    def _L0_ffn_ref(x, k0, k1, k2, s0, s1, s2):
        import jax, jax.numpy as jnp
        import numpy as np
        import math
        D_IN = 256
        FEATURES = (1024, 1024, 256)
        BATCH, SEQ = (8, 512)

        def _conn_dense(kernel_bool, x):
            w = jnp.where(kernel_bool, jnp.float32(1.0), jnp.float32(-1.0))
            return x @ w
        h = jnp.concatenate([x, -x], axis=-1)
        h = s0 * _conn_dense(k0, h)
        h = jax.nn.relu(h) * 2
        h = s1 * _conn_dense(k1, h)
        h = jax.nn.relu(h) * 2
        h = s2 * _conn_dense(k2, h)
        return h

    def _L1_xattn_ref(hidden_states, encoder_hidden_states, Wq, Wk, Wv, Wo, bo):
        import jax, jax.numpy as jnp
        import numpy as np
        HEADS = 16
        DIM_HEAD = 64
        B, S, D = hidden_states.shape
        K = encoder_hidden_states.shape[1]
        H, Dh = (HEADS, DIM_HEAD)
        scale = 1.0 / np.sqrt(Dh)
        q = hidden_states @ Wq
        k = encoder_hidden_states @ Wk
        v = encoder_hidden_states @ Wv
        q = q.reshape(B, S, H, Dh).transpose(0, 2, 1, 3)
        k = k.reshape(B, K, H, Dh).transpose(0, 2, 1, 3)
        v = v.reshape(B, K, H, Dh).transpose(0, 2, 1, 3)
        scores = jnp.einsum('bhsd,bhkd->bhsk', q, k) * scale
        probs = jax.nn.softmax(scores, axis=-1)
        out = jnp.einsum('bhsk,bhkd->bhsd', probs, v)
        out = out.transpose(0, 2, 1, 3).reshape(B, S, H * Dh)
        out = out @ Wo + bo
        return out

    def _L1_ffn_ref(hidden_states, gate_w, gate_bias, w1, w2, w3, ws1, ws2, ws3):
        import jax, jax.numpy as jnp
        import numpy as np
        B, S, H = (1, 512, 256)
        E = 16
        I = 192
        TOPK = 4
        G = 4
        TOPK_G = 2
        SCALE = 2.5
        N_SHARED = 1

        def _route(x, gate_w, gate_bias):
            n = x.shape[0]
            logits = jnp.einsum('nh,eh->ne', x.astype(jnp.float32), gate_w)
            scores = jax.nn.sigmoid(logits)
            sb = scores + gate_bias
            gs = sb.reshape(n, G, E // G)
            group_scores = jnp.sum(jax.lax.top_k(gs, 2)[0], axis=-1)
            _, gidx = jax.lax.top_k(group_scores, TOPK_G)
            gmask = jnp.sum(jax.nn.one_hot(gidx, G, dtype=sb.dtype), axis=1)
            emask = jnp.repeat(gmask, E // G, axis=-1)
            masked = jnp.where(emask > 0, sb, -jnp.inf)
            _, tidx = jax.lax.top_k(masked, TOPK)
            w = jnp.take_along_axis(scores, tidx, axis=1)
            w = w / (jnp.sum(w, axis=-1, keepdims=True) + 1e-20)
            return (tidx, w * SCALE)
        b, s, h = hidden_states.shape
        x = hidden_states.reshape(-1, h)
        tidx, tw = _route(x, gate_w, gate_bias)
        n = x.shape[0]
        combine = jnp.zeros((n, E), x.dtype).at[jnp.arange(n)[:, None], tidx].add(tw)
        g = jnp.einsum('nh,eih->nei', x, w1)
        u = jnp.einsum('nh,eih->nei', x, w3)
        hact = jax.nn.silu(g) * u * combine[:, :, None]
        y = jnp.einsum('nei,ehi->nh', hact, w2)
        shared = jnp.einsum('ni,hi->nh', jax.nn.silu(x @ ws1.T) * (x @ ws3.T), ws2)
        return (y + shared).reshape(b, s, h)
    x = x + jnp.tanh(g_xattn[0]) * _L0_xattn_ref(ctx_768, _layernorm(x, axis=-1), mask_BxS2_bk0, L0_xattn_ln_x_g, L0_xattn_ln_x_b, L0_xattn_ln_l_g, L0_xattn_ln_l_b, L0_xattn_qn_g, L0_xattn_kn_g, L0_xattn_Wq, L0_xattn_Wkv, L0_xattn_Wlkv, L0_xattn_Wo, L0_xattn_bo)
    x = x + jnp.tanh(g_ffn[0]) * _L0_ffn_ref(_layernorm(x, axis=-1), L0_ffn_k0, L0_ffn_k1, L0_ffn_k2, L0_ffn_s0, L0_ffn_s1, L0_ffn_s2)
    x = x + jnp.tanh(g_xattn[1]) * _L1_xattn_ref(_layernorm(x, axis=-1), ctx_768, L1_xattn_Wq, L1_xattn_Wk, L1_xattn_Wv, L1_xattn_Wo, L1_xattn_bo)
    x = x + jnp.tanh(g_ffn[1]) * _L1_ffn_ref(_layernorm(x, axis=-1), L1_ffn_gate_w, L1_ffn_gate_bias, L1_ffn_w1, L1_ffn_w2, L1_ffn_w3, L1_ffn_ws1, L1_ffn_ws2, L1_ffn_ws3)
    return x

_drawn_inputs = setup_inputs


def setup_inputs(seed=0):
    import zlib

    import numpy as np

    out = dict(_drawn_inputs(seed))
    spreads = {'g_ffn': (-1.0, 0.6),
     'L0_xattn_ln_x_g': (1.0, 0.6),
     'L0_xattn_ln_x_b': (0.0, 0.362),
     'L0_xattn_ln_l_g': (1.0, 0.6),
     'L0_xattn_ln_l_b': (0.0, 0.1),
     'L0_xattn_qn_g': (1.0, 0.6),
     'L0_xattn_kn_g': (1.0, 0.6),
     'L0_xattn_bo': (0.0, 0.1)}
    factors = {'L1_xattn_bo': 8.0,
     'L1_ffn_gate_w': 8.0,
     'L1_ffn_gate_bias': 8.0,
     'L1_ffn_w1': 7.112,
     'L1_ffn_w2': 7.184,
     'L1_ffn_w3': 7.064,
     'L1_ffn_ws1': 8.0,
     'L1_ffn_ws2': 8.0,
     'L1_ffn_ws3': 8.0}
    for name, (base, spread) in spreads.items():
        noise = np.random.default_rng([zlib.crc32(name.encode()), seed]).standard_normal(out[name].shape)
        drawn = base * np.exp(spread * noise) if base else spread * noise
        out[name] = jnp.asarray(drawn.astype(out[name].dtype))
    for name, factor in factors.items():
        out[name] = (out[name] * factor).astype(out[name].dtype)
    return out
```

```python
from contextlib import ExitStack

import concourse.bass as bass
from concourse import mybir
from concourse.alu_op_type import AluOpType as ALU

F32 = mybir.dt.float32
F32R = mybir.dt.float32r
U8 = mybir.dt.uint8
U32 = mybir.dt.uint32
ACT = mybir.ActivationFunctionType
AX = mybir.AxisListType

P = 128
NB, S, D = 2, 512, 256
KT = D // P
TT = S // P
NCTX, DC = 1024, 192
DC1 = DC - P
CT = NCTX // P
DH = 64
NK0 = NCTX + S
NK1 = NCTX
HG = 4
NG1 = 1024 // DH // HG
UNITS = 16
BLOCKS = UNITS // 2
FF = 1024
MT = FF // P
E, EI = 16, 192
ET = 26
LN_EPS = 1e-5
SCALE = DH ** -0.5
BIG = 3.0e38

AHEAD_F3, AHEAD_Y, AHEAD_FULL = 2, 4, 1

W0 = {"q": 0, "lkv": 512, "kv": 1536, "wo": 2560}
W0_COLS = 3072
W1 = {"q": 0, "k": 512, "v": 1024, "wo": 1536}
W1_COLS = 2048
WE_COLS = 768
CHUNK = 1024

R_LN, R_W, R_XC = 0, 4096, 10240
R_AT = 2048
R_ATT0 = 14336
R_ATT1 = 18432
R_COLS = 40960

CONST = ["ln_x_g0", "ln_x_g1", "ln_x_b0", "ln_x_b1", "ln_l_g0", "ln_l_g1", "ln_l_b0", "ln_l_b1",
         "qn", "kn", "s0", "s1", "s2", "gx0", "gx1", "gf0", "gf1"]
NC_ = len(CONST)


def build(nc, x_d, ctx_d, ctxT_d, mask_d, cst_d, bo_d, gbias_d, w0_d, k0_d, k1_d, k2_d, w1_d, gw_d, we_d,
          eye_d, ones_d, iota_d, out_d, comb_d):
    with ExitStack() as stack:
        program(nc, stack, x_d, ctx_d, ctxT_d, mask_d, cst_d, bo_d, gbias_d, w0_d, k0_d, k1_d, k2_d, w1_d,
                gw_d, we_d, eye_d, ones_d, iota_d, out_d, comb_d)


def program(nc, stack, x_d, ctx_d, ctxT_d, mask_d, cst_d, bo_d, gbias_d, w0_d, k0_d, k1_d, k2_d, w1_d,
            gw_d, we_d, eye_d, ones_d, iota_d, out_d, comb_d):
    def sb(name, shape, dt=F32):
        return stack.enter_context(nc.sbuf_tensor(name, shape, dt))

    def sem(name):
        return stack.enter_context(nc.semaphore(name))

    R = sb("R", [P, R_COLS], F32R)
    zero = sb("zero", [P, P], F32R)
    x = sb("x", [P, NB * TT, D])
    eye = sb("eye", [P, P])
    cst = sb("cst", [P, 52])
    half_ones = sb("half_ones", [P, 2])
    tg = sb("tg", [P, 8])
    bo = sb("bo", [P, D])
    st6 = sb("st6", [P, 8, 6])
    mv = sb("mv", [P, 8, 2])
    rstd = sb("rstd", [P, 16])
    nmax = sb("nmax", [P, 8])
    sums = sb("sums", [P, 32])
    rr = sb("rr", [P, 128])
    FA = sb("FA", [P, 4096])
    FB = sb("FB", [P, 2816])
    wst = sb("wst", [P, 2048])

    LNH0 = R[:, R_LN:R_LN + 1024].rearrange("p (k n) -> p k n", k=KT)
    LNL0 = R[:, R_LN + 1024:R_LN + 2048].rearrange("p (k n) -> p k n", k=KT)
    LNH = R[:, R_LN:R_LN + 2048].rearrange("p (k n) -> p k n", k=KT)
    LNL = R[:, R_LN + 2048:R_LN + 4096].rearrange("p (k n) -> p k n", k=KT)
    XC0 = [R[:, R_XC + 2048 * j:R_XC + 2048 * (j + 1)].rearrange("p (k n) -> p k n", k=2) for j in range(2)]
    XC1 = [R[:, R_XC + 4096 * j:R_XC + 4096 * (j + 1)].rearrange("p (k n) -> p k n", k=2) for j in range(2)]
    WH = R[:, R_W:R_W + W0_COLS]
    WL = R[:, R_W + W0_COLS:R_W + 2 * W0_COLS]
    xn = FA[:, 1536:2560].rearrange("p (t n) -> p t n", t=TT)

    PS = stack.enter_context(nc.psum_tensor("PS", [P, 8, 512], F32))

    class Attention:

        def __init__(self, layer):
            self.layer = layer
            nk = NK0 if layer == 0 else NK1
            self.nk, self.kt, self.ng, self.nb = nk, nk // P, nk // 512, nk // 512
            at = R_ATT0 if layer == 0 else R_ATT1

            def take(cols):
                nonlocal at
                at += cols
                return R[:, at - cols:at]

            self.q = [take(1024).rearrange("p (j n) -> p j n", j=2) for _ in range(2)]
            self.k = [take(2 * nk).rearrange("p (j n) -> p j n", j=2) for _ in range(2)]
            self.v = take(self.kt * 512).rearrange("p (t h c) -> p t h c", h=HG, c=P)
            self.pt = [take(2 * self.kt * 256).rearrange("p (r t n) -> p r t n", r=2, t=self.kt) for _ in range(2)]
            if layer == 1:
                self.at = [take(1024).rearrange("p (j n) -> p j n", j=2) for _ in range(2)]
            else:
                self.at = [R[:, R_AT + 1024 * j:R_AT + 1024 * (j + 1)].rearrange("p (j n) -> p j n", j=2)
                           for j in range(2)]
            self.probs = FA[:, 0:2 * nk].rearrange("p (r n) -> p r n", r=2)
            self.tmp = FA[:, 3072:3584].rearrange("p (r n) -> p r n", r=2)
            self.wo = (W0 if layer == 0 else W1)["wo"]
            self.score = [PS[:, 3 * r:3 * r + self.nb, :].rearrange("p b n -> p (b n)") for r in range(2)]
            self.turn = [PS[:, 6, :]] if layer == 0 else [PS[:, 6, :], PS[:, 2, :]]

    L0, L1 = Attention(0), Attention(1)

    def qk_dst(i, j):
        if i < 2:
            return L0.q[j][:, i, :]
        return L0.k[j][:, (i - 2) // 3, (i - 2) % 3 * 512:(i - 2) % 3 * 512 + 512]

    maskbias = FB[:, 0:NK0]
    mask8 = FB[:, NK0:NK0 + 256].bitcast(U8)
    at32 = FB[:, 1792:2816].rearrange("p (j n) -> p j n", j=2)

    h1 = [R[:, 18432 + 8192 * j:18432 + 8192 * (j + 1)].rearrange("p (k n) -> p k n", k=MT) for j in range(2)]
    fw0 = R[:, 34816:36864].rearrange("p (k n) -> p k n", k=KT)
    fw1 = R[:, 36864:38912].rearrange("p (r k n) -> p r k n", r=2, k=MT)
    fh2 = R[:, 38912:40960].rearrange("p (r j n) -> p r j n", r=2, j=2)
    fw2 = R[:, 9216:9728].rearrange("p (r n) -> p r n", r=2)
    hf = FA[:, 0:1024].rearrange("p (r n) -> p r n", r=2)
    k0b = FA[:, 2560:3584].bitcast(U8).rearrange("p (k n) -> p k n", k=4)
    k12b = FB[:, 2048:2688].bitcast(U8).rearrange("p (r n) -> p r n", r=2)
    k0t = FA[:, 3584:4096]

    ew = [[R[:, R_W + 1536 * r + 768 * j:R_W + 1536 * r + 768 * (j + 1)] for j in range(2)] for r in range(2)]
    eh = R[:, 18432:20480].rearrange("p (r j n) -> p r j n", r=2, j=2)
    gw = [R[:, 20480 + 32 * j:20512 + 32 * j].rearrange("p (k n) -> p k n", k=KT) for j in range(2)]
    est = wst[:, 0:1536].rearrange("p (r n) -> p r n", r=2)
    silu = FA[:, 0:1024].rearrange("p (r n) -> p r n", r=2)
    hcomb = FA[:, 1024:2048].rearrange("p (r n) -> p r n", r=2)
    hful = FA[:, 2560:3584].rearrange("p (r n) -> p r n", r=2)
    comb = FB[:, 0:2048].rearrange("p (r n) -> p r n", r=2)
    gst = wst[:, 1536:1568]

    names = (
        "x_in0 x_in1 ctx_in mask_in cst_in bo_in w0_in0 w0_in1 w1_in k0_in k1_in0 k1_in1 ctxT_in0 ctxT_in1 gw_in we_in0 we_in1 comb_in0 comb_in1 "
        "comb_out stores zeroed gates bo_gated bo_added w0_split maskbias_ready "
        "ln_var ln_std ln_xn ln_turned ln_aff ln_hi ln_lo cx_var cx_std cx_xn cx_turned cx_aff cx_hi cx_lo "
        "qk0_done qk0_raw qk0_sq qk0_ss qk0_norm qk0_rr qk0_spread qk0_rb qk0_scaled qk0_hi qk0_lo v0_done v0_hi v0_lo "
        "scored maxed expd turned p_hi p_lo pv_done o_tmp o_sum rsum rspread rbc at_norm at_hi at_lo wo_done x_att "
        "pj_done pj_hi pj_lo w1_split xc_hi xc_lo "
        "fw0_ready fw1_ready f1_done f2_done f_act f_hi f_lo f3_done x_ffn "
        "gw_split gate_done gate_sig rt_comb rt_turned rt_copied e_split gu_done e_comb e_silu e_full e_hi e_lo e_y "
        "out_ready dve_step act_step pool_step pool_free").split()
    s = {n: sem(n) for n in names}

    def first(eng, name, value):
        if not isinstance(value, int) or value > 0:
            eng.wait_ge(s[name], value)

    class Steps:

        def __init__(self, eng, name):
            self.eng, self.sem, self.base, self.n = eng, s[name], 0, 0

        def __call__(self, ins):
            self.n += 1
            ins.then_inc(self.sem, 1)

        def wait(self):
            self.eng.wait_ge(self.sem, self.base + self.n)

    mm = nc.tensor.matmul
    eye_ap = eye[:, :]

    def three(pairs):
        out = []
        for (ah, al), (bh, bl) in pairs:
            out += [(ah, bh), (al, bh), (ah, bl)]
        return out

    def group(out, passes, skip=False):
        for n, (a, b) in enumerate(passes):
            last = mm(out, a, b, start=(n == 0), stop=(n == len(passes) - 1), skip_group_check=skip)
        return last

    def wcol(layer, name, kt, width, a, b):
        off = (W0 if layer == 0 else W1)[name] + kt * width
        return off + a, off + b

    def wpair(layer, name, kt, width, a, b, rows=P):
        lo, hi = wcol(layer, name, kt, width, a, b)
        return WH[0:rows, lo:hi], WL[0:rows, lo:hi]

    block = stack.enter_context(nc.Block())

    @block.sync
    def _(sp):
        sp.sem_inc(s["f3_done"], AHEAD_F3)
        sp.sem_inc(s["e_y"], AHEAD_Y)
        sp.sem_inc(s["e_full"], AHEAD_FULL)
        sp.dma_start(x[:, 0:TT, :], x_d[0].rearrange("(t p) n -> p t n", p=P)).then_inc(s["x_in0"], 16)
        sp.dma_start(cst[:, 0:NC_], cst_d).then_inc(s["cst_in"], 16)
        sp.dma_start(eye[:, :], eye_d).then_inc(s["cst_in"], 16)
        sp.dma_start(cst[:, 20:36], gbias_d.partition_broadcast(P)).then_inc(s["cst_in"], 16)
        sp.dma_start(cst[:, 36:52], iota_d.partition_broadcast(P)).then_inc(s["cst_in"], 16)
        sp.dma_start(half_ones[:, :], ones_d).then_inc(s["cst_in"], 16)
        ctx_v = FA[:, 0:CT * DC].rearrange("p (t n) -> p t n", t=CT)
        sp.dma_start(ctx_v, ctx_d[0].rearrange("(t p) n -> p t n", p=P)).then_inc(s["ctx_in"], 16)
        sp.dma_start(wst[:, 0:CHUNK], w0_d[:, 0:CHUNK]).then_inc(s["w0_in0"], 16)
        sp.dma_start(wst[:, CHUNK:2 * CHUNK], w0_d[:, CHUNK:2 * CHUNK]).then_inc(s["w0_in1"], 16)
        sp.dma_start(mask8, mask_d[0:1, :].partition_broadcast(P)).then_inc(s["mask_in"], 16)
        sp.dma_start(x[:, TT:2 * TT, :], x_d[1].rearrange("(t p) n -> p t n", p=P)).then_inc(s["x_in1"], 16)
        sp.dma_start(bo[:, :], bo_d[0:1, :].partition_broadcast(P)).then_inc(s["bo_in"], 16)
        sp.wait_ge(s["w0_split"], 1)
        sp.dma_start(wst[:, 0:CHUNK], w0_d[:, 2 * CHUNK:3 * CHUNK]).then_inc(s["w0_in0"], 16)
        sp.wait_ge(s["maskbias_ready"], 1)
        sp.dma_start(mask8, mask_d[1:2, :].partition_broadcast(P)).then_inc(s["mask_in"], 16)
        sp.wait_ge(s["o_sum"], BLOCKS)
        sp.wait_ge(s["rbc"], 2)
        sp.dma_start(ctx_v, ctx_d[1].rearrange("(t p) n -> p t n", p=P)).then_inc(s["ctx_in"], 16)
        sp.wait_ge(s["bo_added"], NB)
        sp.dma_start(bo[:, :], bo_d[1:2, :].partition_broadcast(P)).then_inc(s["bo_in"], 16)
        sp.wait_ge(s["w0_split"], 3)
        sp.dma_start(wst[:, 0:W1_COLS], w1_d[0]).then_inc(s["w1_in"], 16)
        sp.wait_ge(s["rbc"], 4)
        sp.wait_ge(s["o_sum"], 2 * BLOCKS)
        sp.dma_start(k0b, k0_d.rearrange("(k p) n -> p k n", p=P)).then_inc(s["k0_in"], 16)
        sp.wait_ge(s["x_att"], 4)
        sp.wait_ge(s["maxed"], 2 * UNITS)

        def context_load(c):
            kt, h = c // 2, c % 2
            rows = P if kt == 0 else DC1
            sp.dma_start(FB[0:rows, 1024 * h:1024 * h + 1024],
                         ctxT_d[kt * P:kt * P + rows, h * 1024:h * 1024 + 1024]).then_inc(s[f"ctxT_in{h}"], 16)

        def ffn_load(m):
            sp.dma_start(k12b[:, m % 2, 0:FF], k1_d[m]).then_inc(s[f"k1_in{m % 2}"], 16)
            sp.dma_start(k12b[:, m % 2, FF:FF + D], k2_d[m]).then_inc(s[f"k1_in{m % 2}"], 16)

        for c in range(2):
            context_load(c)
            ffn_load(c)
        for c in range(2):
            sp.wait_ge(s["xc_lo"], c + 1)
            context_load(c + 2)
        for m in range(2, MT):
            sp.wait_ge(s["fw1_ready"], m - 1)
            ffn_load(m)
        sp.wait_ge(s["w1_split"], 1)
        sp.dma_start(wst[:, 0:W1_COLS], w1_d[1]).then_inc(s["w1_in"], 16)
        with sp.Fori(0, NG1 - 2) as g:
            sp.wait_ge(s["w1_split"], g + 2)
            sp.dma_start(wst[:, 0:W1_COLS], w1_d[bass.ds(g + 2, 1)].rearrange("g p n -> (g p) n")).then_inc(s["w1_in"], 16)
        sp.wait_ge(s["w1_split"], NG1)
        sp.dma_start(gst, gw_d).then_inc(s["gw_in"], 16)
        sp.dma_start(est[:, 0, :], we_d[0]).then_inc(s["we_in0"], 16)
        sp.dma_start(est[:, 1, :], we_d[1]).then_inc(s["we_in1"], 16)
        sp.wait_ge(s["rt_copied"], 3)
        sp.dma_start(comb_d[3 * E:2 * ET, :], FA[0:2 * ET - 3 * E, 2560:3584]).then_inc(s["comb_out"], 16)
        routed = comb_d[0:3 * E, :].rearrange("(e r) n -> e r n", r=3)
        for r in range(3):
            sp.dma_start(routed[:, r, :], FA[0:E, 1024:2048]).then_inc(s["comb_out"], 16)
        sp.wait_ge(s["comb_out"], 64)

        def comb_load(row, r, name):
            for half in range(2):
                sp.dma_start(comb[64 * half:64 * half + 64, r, :],
                             comb_d[bass.ds(row + half, 1), :].partition_broadcast(64).rearrange("q o n -> q (o n)")
                             ).then_inc(s[name], 16)

        comb_load(0, 0, "comb_in0")
        comb_load(2, 1, "comb_in1")
        with sp.Fori(0, ET // 2 - 1) as i:
            for r in range(2):
                sp.wait_ge(s["e_split"], 2 * i + r + 1)
                sp.dma_start(est[:, r, :], we_d[bass.ds(2 * i + 2 + r, 1)].rearrange("g p n -> (g p) n")
                             ).then_inc(s[f"we_in{r}"], 16)
                sp.wait_ge(s["e_full"], AHEAD_FULL + 4 * i + 2 * r + 2)
                comb_load(4 * i + 4 + 2 * r, r, f"comb_in{r}")
        for t in range(NB * TT):
            sp.wait_ge(s["out_ready"], t + 1)
            sp.dma_start(out_d[t // TT, (t % TT) * P:(t % TT) * P + P, :], x[:, t, :]).then_inc(s["stores"], 16)
        sp.wait_ge(s["stores"], 16 * NB * TT)

    @block.gpsimd
    def _(pool):
        step = Steps(pool, "pool_step")
        g = nc.gpsimd

        def split(hi, lo, src):
            step(g.tensor_scalar(hi, src, 1.0, None, ALU.mult))
            step.wait()
            return g.tensor_tensor(lo, src, hi.bitcast(F32), ALU.subtract)

        g.memset(zero[:, :].bitcast(F32), 0.0).then_inc(s["zeroed"], 1)
        for c in range(W0_COLS // CHUNK):
            pool.wait_ge(s[f"w0_in{c % 2}"], 16 * (c // 2 + 1))
            src = wst[:, (c % 2) * CHUNK:(c % 2) * CHUNK + CHUNK]
            split(WH[:, c * CHUNK:(c + 1) * CHUNK], WL[:, c * CHUNK:(c + 1) * CHUNK], src).then_inc(s["w0_split"], 1)
        for b in range(NB):
            pool.wait_ge(s["ln_xn"], 2 * b + 1)
            pool.wait_ge(s["bo_gated"], 1)
            for t in range(TT):
                last = g.tensor_tensor(x[:, b * TT + t, :], x[:, b * TT + t, :], bo[:, :], ALU.add)
            last.then_inc(s["bo_added"], 1)
        pool.wait_ge(s["k0_in"], 16)
        pool.wait_ge(s["at_lo"], 4)
        pool.wait_ge(s["wo_done"], 4)
        for kt in range(KT):
            for h in range(2):
                cols = slice(512 * h, 512 * h + 512)
                step(g.tensor_scalar(k0t, k0b[:, KT + kt, cols], -2.0, None, ALU.mult))
                step.wait()
                step(g.tensor_scalar(fw0[:, kt, cols], k0b[:, kt, cols], 2.0, None, ALU.mult))
                step.wait()
                last = g.tensor_tensor(fw0[:, kt, cols], fw0[:, kt, cols].bitcast(F32), k0t, ALU.add)
                step(last)
                step.wait()
        g.tensor_scalar(fw0[:, 0, 0:1], fw0[:, 0, 0:1].bitcast(F32), 1.0, None, ALU.mult).then_inc(s["fw0_ready"], 1)
        for m in range(MT):
            pool.wait_ge(s[f"k1_in{m % 2}"], 32 * (m // 2 + 1))
            if m >= 2:
                pool.wait_ge(s["f3_done"], AHEAD_F3 + 2 * m - 2)
            step(g.tensor_scalar(fw1[:, m % 2].rearrange("p k n -> p (k n)"), k12b[:, m % 2, 0:FF], 2.0, -1.0, ALU.mult, ALU.add))
            step.wait()
            g.tensor_scalar(fw2[:, m % 2], k12b[:, m % 2, FF:FF + D], 2.0, -1.0, ALU.mult, ALU.add).then_inc(s["fw1_ready"], 1)
            if m == 1:
                for c in range(4):
                    kt, h = c // 2, c % 2
                    rows = P if kt == 0 else DC1
                    pool.wait_ge(s[f"ctxT_in{h}"], 16 * (c // 2 + 1))
                    cols = slice(1024 * h, 1024 * h + 1024)
                    split(XC1[0][0:rows, kt, cols], XC1[1][0:rows, kt, cols],
                          FB[0:rows, cols]).then_inc(s["xc_lo"], 1)
                pool.wait_ge(s["w1_in"], 16)
                split(WH[:, 0:W1_COLS], WL[:, 0:W1_COLS], wst[:, 0:W1_COLS]).then_inc(s["w1_split"], 1)
        for b in range(NB):
            pool.wait_ge(s["ln_xn"], 2 * NB + NB + b + 1)
            pool.wait_ge(s["bo_gated"], 2)
            for t in range(TT):
                last = g.tensor_tensor(x[:, b * TT + t, :], x[:, b * TT + t, :], bo[:, :], ALU.add)
            last.then_inc(s["bo_added"], 1)
        with pool.Fori(1, NG1) as i:
            pool.wait_ge(s["w1_in"], 16 * i + 16)
            pool.wait_ge(s["pj_done"], 28 * i)
            n = W1["wo"]
            pool.sem_inc(s["pool_free"], 1)
            g.tensor_scalar(WH[:, 0:n], wst[:, 0:n], 1.0, None, ALU.mult).then_inc(s["pool_step"], 1)
            pool.wait_ge(s["pool_step"], step.n + 2 * (i - 1) + 1)
            g.tensor_tensor(WL[:, 0:n], wst[:, 0:n], WH[:, 0:n].bitcast(F32), ALU.subtract)
            pool.wait_ge(s["wo_done"], 4 + 4 * i)
            pool.sem_inc(s["pool_free"], 1)
            g.tensor_scalar(WH[:, n:W1_COLS], wst[:, n:W1_COLS], 1.0, None, ALU.mult).then_inc(s["pool_step"], 1)
            pool.wait_ge(s["pool_step"], step.n + 2 * (i - 1) + 2)
            g.tensor_tensor(WL[:, n:W1_COLS], wst[:, n:W1_COLS], WH[:, n:W1_COLS].bitcast(F32),
                            ALU.subtract).then_inc(s["w1_split"], 1)
        step.n += 2 * (NG1 - 1)
        pool.wait_ge(s["gw_in"], 16)
        pool.wait_ge(s["wo_done"], 4 + 4 * NG1)
        split(gw[0].rearrange("p k n -> p (k n)"), gw[1].rearrange("p k n -> p (k n)"), gst).then_inc(s["gw_split"], 1)
        base = step.n
        with pool.Fori(0, ET // 2) as i:
            for r in range(2):
                pool.wait_ge(s[f"we_in{r}"], 16 * i + 16)
                pool.wait_ge(s["e_y"], AHEAD_Y + 4 * i + 2 * r - 2)
                pool.sem_inc(s["pool_free"], 1)
                g.tensor_scalar(ew[r][0], est[:, r, :], 1.0, None, ALU.mult).then_inc(s["pool_step"], 1)
                pool.wait_ge(s["pool_step"], base + 2 * i + r + 1)
                g.tensor_tensor(ew[r][1], est[:, r, :], ew[r][0].bitcast(F32), ALU.subtract).then_inc(s["e_split"], 1)

    @block.tensor
    def _(pe):
        def ln_turn(n, double):
            pe.wait_ge(s["ln_xn"], n)
            for kt in range(KT):
                for t in range(TT):
                    last = nc.tensor.transpose(PS[:, kt, t * P:t * P + P], xn[:, t, kt * P:kt * P + P], eye_ap)
            last.then_inc(s["ln_turned"], 1)

        def attention(L, b, C):
            U0, K0 = UNITS * C, BLOCKS * C
            G0 = L.ng * UNITS * C if L.layer == 0 else 32 * C + 32

            def scores(u, n):
                p, h, qt = u // 8, (u // 2) % 2, ((u // 4) % 2) * 2 + u % 2
                rows = slice(DH * h, DH * h + DH)
                if n == 0:
                    first(pe, "expd", U0 + u - 1)
                q = [L.q[j][rows, p, qt * P:qt * P + P] for j in range(2)]
                k = [L.k[j][rows, p, n * 512:n * 512 + 512] for j in range(2)]
                last = group(L.score[u % 2][:, n * 512:n * 512 + 512], three([(q, k)]))
                if n == L.nb - 1:
                    last.then_inc(s["scored"], 1)

            def turn(u, g_):
                G = G0 + L.ng * u + g_
                nt = len(L.turn)
                if g_ == 0:
                    pe.wait_ge(s["expd"], U0 + u + 1)
                first(pe, "p_lo", G - nt + 1)
                out = L.turn[g_ % nt]
                for i in range(4):
                    c = (4 * g_ + i) * P
                    last = nc.tensor.transpose(out[:, i * P:i * P + P], L.probs[:, u % 2, c:c + P], eye_ap)
                last.then_inc(s["turned"], 1)

            def values(k, half):
                hd = 2 * (k // 4) + k % 2
                if half == 0:
                    pe.wait_ge(s["p_lo"], G0 + L.ng * (2 * k + 2))
                    first(pe, "o_sum", K0 + k)
                n = L.kt // 2
                for kt in range(half * n, half * n + n):
                    for j in range(2):
                        last = mm(PS[:, 7, 0:256], L.v[:, kt, hd, :], L.pt[j][:, k % 2, kt, :],
                                  start=(kt == 0 and j == 0), stop=(kt == L.kt - 1 and j == 1))
                if half == 1:
                    last.then_inc(s["pv_done"], 1)

            for u in (0, 1):
                for n in range(L.nb):
                    scores(u, n)
            for u in range(UNITS + 2):
                for g_ in range(L.ng):
                    if u < UNITS:
                        turn(u, g_)
                    if u + 2 < UNITS:
                        scores(u + 2, g_)
                if u >= 2:
                    values(u // 2 - 1, u % 2)
            pe.wait_ge(s["rspread"], 2 * C + 2)
            for p in range(2):
                for qt in range(TT):
                    c = 512 * p + P * qt
                    last = mm(PS[:, p, qt * P:qt * P + P], FA[:, c:c + P], eye_ap, start=True, stop=True)
                last.then_inc(s["rbc"], 1)
            pe.wait_ge(s["at_lo"], 2 * C + 2)
            for w in range(2):
                for e in range(2):
                    tt = 2 * w + e
                    pairs = [(tuple(L.at[j][:, p, tt * P:tt * P + P] for j in range(2)),
                              (WH[:, L.wo + p * D:L.wo + p * D + D], WL[:, L.wo + p * D:L.wo + p * D + D]))
                             for p in range(2)]
                    last = group(PS[:, 3 + w, e * D:e * D + D], three(pairs))
                last.then_inc(s["wo_done"], 1)

        pe.wait_ge(s["cst_in"], 80)
        for b in range(NB):
            ln_turn(2 * b + 2, True)
            pe.wait_ge(s["cx_xn"], b + 1)
            ctx_v = FA[:, 0:CT * DC].rearrange("p (t n) -> p t n", t=CT)
            for gg in range(2):
                for kt in range(2):
                    rows = P if kt == 0 else DC1
                    for t in range(4):
                        last = nc.tensor.transpose(PS[0:rows, 2 + 2 * gg + kt, t * P:t * P + P],
                                                   ctx_v[:, 4 * gg + t, kt * P:kt * P + rows], eye_ap)
                    last.then_inc(s["cx_turned"], 1)
            pe.wait_ge(s["ln_lo"], 2 * b + 2)
            pe.wait_ge(s["cx_lo"], 4 * b + 4)
            pe.wait_ge(s["w0_split"], 3)

            def square_sums(i):
                pe.wait_ge(s["qk0_sq"], 8 * b + i + 1)
                for tt in range(TT):
                    last = mm(PS[:, 4, i * 8 + tt * 2:i * 8 + tt * 2 + 2],
                              FB[:, 1792 + 512 * (i % 2) + tt * P:1792 + 512 * (i % 2) + tt * P + P],
                              half_ones[:, :], start=True, stop=True)
                last.then_inc(s["qk0_ss"], 1)

            lat = [(LNH0[:, kt, :], LNL0[:, kt, :]) for kt in range(KT)]
            for i in range(8):
                if i >= 4:
                    pe.wait_ge(s["qk0_sq"], 8 * b + i - 3)
                if i < 2:
                    pairs = [(wpair(0, "q", kt, 256, i * P, i * P + P), lat[kt]) for kt in range(KT)]
                else:
                    p, n = (i - 2) // 3, (i - 2) % 3
                    if n < 2:
                        pairs = [(wpair(0, "kv", kt, 512, p * P, p * P + P, P if kt == 0 else DC1),
                                  tuple(XC0[j][0:P if kt == 0 else DC1, kt, n * 512:n * 512 + 512] for j in range(2)))
                                 for kt in range(2)]
                    else:
                        pairs = [(wpair(0, "lkv", kt, 512, p * P, p * P + P), lat[kt]) for kt in range(KT)]
                group(PS[:, i % 4, :], three(pairs)).then_inc(s["qk0_done"], 1)
                if i >= 1:
                    square_sums(i - 1)
            square_sums(7)
            for t in range(L0.kt):
                if t >= 3:
                    pe.wait_ge(s["v0_lo"], 12 * b + t - 2)
                if t < CT:
                    pairs = [(tuple(XC0[j][0:P if kt == 0 else DC1, kt, t * P:t * P + P] for j in range(2)),
                              wpair(0, "kv", kt, 512, 256, 512, P if kt == 0 else DC1)) for kt in range(2)]
                else:
                    c = (t - CT) * P
                    pairs = [((LNH0[:, kt, c:c + P], LNL0[:, kt, c:c + P]), wpair(0, "lkv", kt, 512, 256, 512))
                             for kt in range(KT)]
                group(PS[:, 5 + t % 3, 0:256], three(pairs)).then_inc(s["v0_done"], 1)
            for i in range(8):
                if i >= 4:
                    pe.wait_ge(s["qk0_scaled"], 8 * b + i - 3)
                pe.wait_ge(s["qk0_spread"], 8 * b + i + 1)
                for tt in range(TT):
                    c = 1792 + 512 * (i % 2) + tt * P
                    last = mm(PS[:, i % 4, tt * P:tt * P + P], FB[:, c:c + P], eye_ap, start=True, stop=True)
                last.then_inc(s["qk0_rb"], 1)
            pe.wait_ge(s["qk0_lo"], 8 * b + 8)
            pe.wait_ge(s["v0_lo"], 12 * b + 12)
            attention(L0, b, b)
            pe.wait_ge(s["x_att"], 2 * b + 2)

        for b in range(NB):
            ln_turn(2 * NB + b + 1, False)
            pe.wait_ge(s["ln_lo"], 2 * NB + 2 * (b + 1))
        pe.wait_ge(s["fw0_ready"], 1)
        for j in range(2 * MT):
            m, h = j // 2, j % 2
            if j >= 4:
                pe.wait_ge(s["f_act"], j - 3)
            passes = [(fw0[:, kt, m * P:m * P + P], X[:, kt, h * 512:h * 512 + 512])
                      for kt in range(KT) for X in (LNH, LNL)]
            group(PS[:, j % 4, :], passes).then_inc(s["f1_done"], 1)
        pe.wait_ge(s["zeroed"], 1)
        for w in range(4):
            last = mm(PS[:, 4 + w, :], zero[:, :], LNH[:, 0, 0:512], start=True, stop=False, skip_group_check=True)
        pe.wait_ge(s["f_lo"], 2 * MT)

        def ffn2(j, m, r, h):
            if h == 0:
                pe.wait_ge(s["fw1_ready"], m + 1)
            pe.wait_ge(s["f_act"], 2 * MT + j - 3)
            passes = [(fw1[:, r, kt, :], X[:, kt, h * 512:h * 512 + 512]) for kt in range(MT) for X in h1]
            group(PS[:, (2 * r + h) % 4, :], passes).then_inc(s["f2_done"], 1)

        def ffn3(j, r, h):
            pe.wait_ge(s["f_lo"], 2 * MT + j + 1)
            for tt in range(TT):
                T = TT * h + tt
                for part in range(2):
                    last = mm(PS[:, 4 + T // 2, (T % 2) * D:(T % 2) * D + D], fh2[:, h, part, tt * P:tt * P + P],
                              fw2[:, r, :], start=False, stop=False, skip_group_check=True)
            last.then_inc(s["f3_done"], 1)

        ffn2(0, 0, 0, 0)
        with pe.Fori(0, MT // 2 - 1) as i:
            for c in range(4):
                ffn2(4 * i + c + 1, 2 * i + (c + 1) // 2, ((c + 1) // 2) % 2, (c + 1) % 2)
                ffn3(4 * i + c, c // 2, c % 2)
        base = 2 * MT - 4
        for c in range(4):
            if c < 3:
                ffn2(base + c + 1, MT - 2 + (c + 1) // 2, (c + 1) // 2, (c + 1) % 2)
            ffn3(base + c, c // 2, c % 2)
        pe.wait_ge(s["x_ffn"], 1)

        for b in range(NB):
            ln_turn(3 * NB + b + 1, False)
            pe.wait_ge(s["ln_lo"], 4 * NB + 2 * (b + 1))
        pe.wait_ge(s["xc_lo"], 4)
        with pe.Fori(0, NG1) as g_:
            pe.wait_ge(s["w1_split"], g_ + 1)
            for b in range(NB):
                C = 2 * g_ + b + 2
                J0 = 28 * g_ + 14 * b

                def context(kt, a, z):
                    rows = P if kt == 0 else DC1
                    return tuple(XC1[j][0:rows, kt, NCTX * b + a:NCTX * b + z] for j in range(2))

                for j in range(14):
                    if j >= 8:
                        pe.wait_ge(s["pj_lo"], J0 + j - 7)
                    if j < 2:
                        pairs = [(wpair(1, "q", kt, 256, j * P, j * P + P),
                                  (LNH[:, kt, b * S:b * S + S], LNL[:, kt, b * S:b * S + S])) for kt in range(KT)]
                        out = PS[:, j % 8, :]
                    elif j < 6:
                        p, n = (j - 2) // 2, (j - 2) % 2
                        pairs = [(wpair(1, "k", kt, 256, p * P, p * P + P, P if kt == 0 else DC1),
                                  context(kt, n * 512, n * 512 + 512)) for kt in range(2)]
                        out = PS[:, j % 8, :]
                    else:
                        t = j - 6
                        pairs = [(context(kt, t * P, t * P + P),
                                  wpair(1, "v", kt, 256, 0, 256, P if kt == 0 else DC1)) for kt in range(2)]
                        out = PS[:, j % 8, 0:256]
                    group(out, three(pairs)).then_inc(s["pj_done"], 1)
                pe.wait_ge(s["pj_lo"], J0 + 14)
                attention(L1, b, C)
                pe.wait_ge(s["x_att"], 2 * C + 2)

        for b in range(NB):
            ln_turn(4 * NB + b + 1, False)
            pe.wait_ge(s["ln_lo"], 6 * NB + 2 * (b + 1))
        pe.wait_ge(s["gw_split"], 1)
        for t in range(NB * TT):
            c = t * P
            passes = three([((LNH[:, kt, c:c + P], LNL[:, kt, c:c + P]), (gw[0][:, kt, :], gw[1][:, kt, :]))
                            for kt in range(KT)])
            last = group(PS[:, 2, t * E:t * E + E], passes)
        last.then_inc(s["gate_done"], 1)
        for w in range(4):
            last = mm(PS[:, 4 + w, :], zero[:, :], LNH[:, 0, 0:512], start=True, stop=False, skip_group_check=True)
        pe.wait_ge(s["rt_comb"], 1)
        for t in range(NB * TT):
            last = nc.tensor.transpose(PS[0:E, t // TT, (t % TT) * P:(t % TT) * P + P], wst[:, 1600 + t * E:1600 + t * E + E],
                                       eye_ap)
        last.then_inc(s["rt_turned"], 1)
        pe.wait_ge(s["rt_copied"], 2)

        def gate_up(j, tile, r, h):
            if h == 0:
                pe.wait_ge(s["e_split"], tile + 1)
            first(pe, "e_full", AHEAD_FULL + j - 1)
            for part in range(2):
                c = part * 256
                pairs = [((ew[r][0][:, c + kt * P:c + kt * P + P], ew[r][1][:, c + kt * P:c + kt * P + P]),
                          (LNH[:, kt, h * 512:h * 512 + 512], LNL[:, kt, h * 512:h * 512 + 512]))
                         for kt in range(KT)]
                last = group(PS[:, 2 * h + part, :], three(pairs))
            last.then_inc(s["gu_done"], 1)

        def down(j, r, h):
            pe.wait_ge(s["e_lo"], j + 1)
            for tt in range(TT):
                T = TT * h + tt
                for a, w in three([((eh[:, h, 0, tt * P:tt * P + P], eh[:, h, 1, tt * P:tt * P + P]),
                                    (ew[r][0][:, 512:768], ew[r][1][:, 512:768]))]):
                    last = mm(PS[:, 4 + T // 2, (T % 2) * D:(T % 2) * D + D], a, w,
                              start=False, stop=False, skip_group_check=True)
            last.then_inc(s["e_y"], 1)

        gate_up(0, 0, 0, 0)
        with pe.Fori(0, ET // 2 - 1) as i:
            for c in range(4):
                gate_up(4 * i + c + 1, 2 * i + (c + 1) // 2, ((c + 1) // 2) % 2, (c + 1) % 2)
                down(4 * i + c, c // 2, c % 2)
        base = 2 * ET - 4
        for c in range(4):
            if c < 3:
                gate_up(base + c + 1, ET - 2 + (c + 1) // 2, (c + 1) // 2, (c + 1) % 2)
            down(base + c, c // 2, c % 2)

    @block.scalar
    def _(act):
        a_ = nc.scalar.activation
        col = {n: cst[:, i:i + 1] for i, n in enumerate(CONST)}

        def ln_root(n, cols=TT):
            act.wait_ge(s["ln_var"], n)
            a_(rstd[:, 8:8 + cols], rstd[:, 0:cols], ACT.Sqrt).then_inc(s["ln_std"], 1)

        def ln_split(n, b, dst):
            act.wait_ge(s["ln_turned"], n)
            for kt in range(KT):
                a_(dst[:, kt, b * S:b * S + S], PS[:, kt, :], ACT.Copy).then_inc(s["ln_hi"], 1)

        def attention(L, b, C):
            U0, K0 = UNITS * C, BLOCKS * C
            G0 = L.ng * UNITS * C if L.layer == 0 else 32 * C + 32

            def exp(u):
                act.wait_ge(s["maxed"], U0 + u + 1)
                first(act, "turned", G0 + L.ng * (u - 1))
                a_(L.probs[:, u % 2, :], L.score[u % 2], ACT.Exp, bias=nmax[:, u % 2:u % 2 + 1], scale=1.0,
                   accum_out=sums[:, u:u + 1]).then_inc(s["expd"], 1)

            def out_copy(k):
                h = k % 2
                act.wait_ge(s["pv_done"], K0 + k + 1)
                first(act, "o_sum", K0 + k - 1)
                a_(L.tmp[DH * h:DH * h + DH, k % 2, :], PS[0:DH, 7, 0:256], ACT.Copy).then_inc(s["o_tmp"], 1)

            first(act, "rsum", C)
            exp(0)
            for u in range(UNITS + 3):
                if u >= 4 and u % 2 == 0:
                    out_copy(u // 2 - 2)
                if u < UNITS:
                    for g_ in range(L.ng):
                        G = G0 + L.ng * u + g_
                        act.wait_ge(s["turned"], G + 1)
                        if g_ == 0:
                            first(act, "pv_done", K0 + u // 2 - 1)
                        a_(L.pt[0][:, (u // 2) % 2, 4 * g_:4 * g_ + 4, (u % 2) * P:(u % 2) * P + P],
                           L.turn[g_ % len(L.turn)].rearrange("p (t n) -> p t n", t=4), ACT.Copy).then_inc(s["p_hi"], 1)
                if u + 1 < UNITS:
                    exp(u + 1)
            for p in range(2):
                act.wait_ge(s["at_norm"], 2 * C + p + 1)
                a_(L.at[0][:, p, :], at32[:, p, :], ACT.Copy).then_inc(s["at_hi"], 1)

        act.wait_ge(s["cst_in"], 80)
        a_(tg[:, 0:4], cst[:, CONST.index("gx0"):CONST.index("gx0") + 4], ACT.Tanh).then_inc(s["gates"], 1)
        for b in range(NB):
            ln_root(2 * b + 1)
            act.wait_ge(s["cx_var"], b + 1)
            a_(rr[:, CT:2 * CT], rr[:, 0:CT], ACT.Sqrt).then_inc(s["cx_std"], 1)
            ln_root(2 * b + 2)
            act.wait_ge(s["ln_turned"], b + 1)
            for kt in range(KT):
                first(act, "qk0_lo", 8 * b)
                a_(FA[:, 2560 + 512 * kt:3072 + 512 * kt], PS[:, kt, :], ACT.Identity,
                   bias=col[f"ln_l_b{kt}"], scale=col[f"ln_l_g{kt}"]).then_inc(s["ln_aff"], 1)
                a_(LNH0[:, kt, :], PS[:, kt, :], ACT.Identity,
                   bias=col[f"ln_l_b{kt}"], scale=col[f"ln_l_g{kt}"]).then_inc(s["ln_hi"], 1)
            for i in range(4):
                gg, kt = i // 2, i % 2
                rows = P if kt == 0 else DC1
                act.wait_ge(s["cx_turned"], 4 * b + i + 1)
                first(act, "cx_lo", 4 * b + i - 1)
                src = PS[0:rows, 2 + 2 * gg + kt, :]
                gain = dict(bias=col[f"ln_x_b{kt}"][0:rows], scale=col[f"ln_x_g{kt}"][0:rows])
                a_(FB[0:rows, 1792 + 512 * kt:2304 + 512 * kt], src, ACT.Identity, **gain).then_inc(s["cx_aff"], 1)
                a_(XC0[0][0:rows, kt, gg * 512:gg * 512 + 512], src, ACT.Identity, **gain).then_inc(s["cx_hi"], 1)
            for i in range(8):
                act.wait_ge(s["qk0_done"], 8 * b + i + 1)
                a_(FA[:, 512 * i:512 * i + 512], PS[:, i % 4, :], ACT.Copy).then_inc(s["qk0_raw"], 1)
                first(act, "qk0_ss", 8 * b + i - 1)
                a_(FB[:, 1792 + 512 * (i % 2):2304 + 512 * (i % 2)], PS[:, i % 4, :], ACT.Square).then_inc(s["qk0_sq"], 1)
            act.wait_ge(s["qk0_ss"], 8 * b + 8)
            a_(rr[:, 64:128], PS[:, 4, 0:64], ACT.Sqrt).then_inc(s["qk0_norm"], 1)
            for t in range(L0.kt):
                act.wait_ge(s["v0_done"], 12 * b + t + 1)
                a_(L0.v[:, t, :, 0:DH], PS[:, 5 + t % 3, 0:256].rearrange("p (h c) -> p h c", h=HG),
                   ACT.Copy).then_inc(s["v0_hi"], 1)
            for i in range(8):
                act.wait_ge(s["qk0_scaled"], 8 * b + i + 1)
                a_(qk_dst(i, 0), FA[:, 512 * i:512 * i + 512], ACT.Copy).then_inc(s["qk0_hi"], 1)
            act.wait_ge(s["qk0_lo"], 8 * b + 8)
            attention(L0, b, b)

        for b in range(NB):
            ln_root(2 * NB + b + 1)
            ln_split(NB + b + 1, b, LNH)
        for j in range(2 * MT):
            act.wait_ge(s["f1_done"], j + 1)
            if j >= 2:
                act.wait_ge(s["f_lo"], j - 1)
            a_(hf[:, j % 2, :], PS[:, j % 4, :], ACT.Relu, scale=tg[:, 4:5]).then_inc(s["f_act"], 1)
        with act.Fori(0, MT // 2) as i:
            for c in range(4):
                act.wait_ge(s["f2_done"], 4 * i + c + 1)
                act.wait_ge(s["f_lo"], 2 * MT + 4 * i + c - 1)
                a_(hf[:, c % 2, :], PS[:, c, :], ACT.Relu, scale=tg[:, 5:6]).then_inc(s["f_act"], 1)

        for b in range(NB):
            ln_root(3 * NB + b + 1)
            ln_split(2 * NB + b + 1, b, LNH)
        with act.Fori(0, NG1) as g_:
            for b in range(NB):
                C = 2 * g_ + b + 2
                J0 = 28 * g_ + 14 * b
                for j in range(14):
                    act.wait_ge(s["pj_done"], J0 + j + 1)
                    if j < 2:
                        a_(L1.q[0][:, j, :], PS[:, j, :], ACT.Copy, scale=SCALE).then_inc(s["pj_hi"], 1)
                    elif j < 6:
                        p, n = (j - 2) // 2, (j - 2) % 2
                        a_(L1.k[0][:, p, n * 512:n * 512 + 512], PS[:, j, :], ACT.Copy).then_inc(s["pj_hi"], 1)
                    else:
                        a_(L1.v[:, j - 6, :, 0:DH], PS[:, j % 8, 0:256].rearrange("p (h c) -> p h c", h=HG),
                           ACT.Copy).then_inc(s["pj_hi"], 1)
                attention(L1, b, C)
        for b in range(NB):
            ln_root(4 * NB + b + 1)
            ln_split(3 * NB + b + 1, b, LNH)
        act.wait_ge(s["gate_done"], 1)
        a_(wst[:, 1728:1856], PS[:, 2, 0:P], ACT.Sigmoid).then_inc(s["gate_sig"], 1)
        with act.Fori(0, ET // 2) as i:
            for c in range(4):
                act.wait_ge(s["gu_done"], 4 * i + c + 1)
                a_(silu[:, c % 2, :], PS[:, 2 * (c % 2), :], ACT.Silu).then_inc(s["e_silu"], 1)
                act.wait_ge(s["e_full"], AHEAD_FULL + 4 * i + c + 1)
                act.wait_ge(s["e_y"], AHEAD_Y + 4 * i + c - 1)
                a_(eh[:, c % 2, 0, :], hful[:, c % 2, :], ACT.Copy).then_inc(s["e_hi"], 1)

    @block.vector
    def _(dve):
        step = Steps(dve, "dve_step")
        v = nc.vector

        def inc(ins, name):
            ins.then_inc(s[name], 1)

        def norm(n, b, src):
            for t in range(TT):
                last = v.bn_stats(st6[:, t, :], src(t))
            step(last)
            step.wait()
            for t in range(TT):
                last = v.bn_aggr(mv[:, t, :], st6[:, t, :])
            step(last)
            step.wait()
            step(v.tensor_scalar(rstd[:, 4:8], mv[:, 0:TT, 1], LN_EPS, None, ALU.add))
            step.wait()
            inc(v.reciprocal(rstd[:, 0:TT], rstd[:, 4:8]), "ln_var")
            dve.wait_ge(s["ln_std"], n)
            for t in range(TT):
                last = v.tensor_scalar(xn[:, t, :], src(t), mv[:, t, 0:1], rstd[:, 8 + t:9 + t], ALU.subtract, ALU.mult)
            inc(last, "ln_xn")

        def x_tiles(b):
            return lambda t: x[:, b * TT + t, :]

        def split_norm(n, b):
            for kt in range(KT):
                dve.wait_ge(s["ln_hi"], 2 * (n - 1) + kt + 1)
                cols = slice(b * S, b * S + S)
                inc(v.tensor_tensor(LNL[:, kt, cols], PS[:, kt, :], LNH[:, kt, cols].bitcast(F32), ALU.subtract), "ln_lo")

        def attention(L, b, C):
            U0, K0 = UNITS * C, BLOCKS * C
            G0 = L.ng * UNITS * C if L.layer == 0 else 32 * C + 32

            def maximum(u):
                r = u % 2
                dve.wait_ge(s["scored"], U0 + u + 1)
                first(dve, "expd", U0 + u - 1)
                if L.layer == 0:
                    step(v.tensor_tensor_reduce(L.score[r], L.score[r], maskbias, 1.0, -BIG, ALU.add, ALU.max,
                                                accum_out=nmax[:, 2 + r:3 + r]))
                    step.wait()
                    inc(v.tensor_scalar(nmax[:, r:r + 1], nmax[:, 2 + r:3 + r], -1.0, None, ALU.mult), "maxed")
                else:
                    inc(v.tensor_reduce(nmax[:, r:r + 1], L.score[r], AX.X, ALU.max, negate=True), "maxed")

            def split(u):
                for g_ in range(L.ng):
                    dve.wait_ge(s["p_hi"], G0 + L.ng * u + g_ + 1)
                    hi, lo = (L.pt[j][:, (u // 2) % 2, 4 * g_:4 * g_ + 4, (u % 2) * P:(u % 2) * P + P] for j in range(2))
                    turned = L.turn[g_ % len(L.turn)].rearrange("p (t n) -> p t n", t=4)
                    inc(v.tensor_tensor(lo, turned, hi.bitcast(F32), ALU.subtract), "p_lo")

            def out_sum(k):
                p, qh, h = k // 4, (k // 2) % 2, k % 2
                dve.wait_ge(s["o_tmp"], K0 + k + 1)
                if k == 0:
                    first(dve, "at_hi", 2 * C)
                rows = slice(DH * h, DH * h + DH)
                inc(v.tensor_tensor(at32[rows, p, qh * 256:qh * 256 + 256], PS[DH:P, 7, 0:256], L.tmp[rows, k % 2, :],
                                    ALU.add), "o_sum")

            maximum(0)
            for u in range(UNITS + 3):
                if u + 1 < UNITS:
                    maximum(u + 1)
                if u >= 4 and u % 2 == 0:
                    out_sum(u // 2 - 2)
                if u < UNITS:
                    split(u)
            dve.wait_ge(s["expd"], U0 + UNITS)
            inc(v.reciprocal(rr[:, 0:UNITS], sums[:, 0:UNITS]), "rsum")
            dve.wait_ge(s["rsum"], C + 1)
            dve.wait_ge(s["turned"], G0 + L.ng * UNITS)
            for p in range(2):
                for qh in range(2):
                    src = rr[:, 8 * p + 4 * qh:8 * p + 4 * qh + 4].rearrange("p (h q) -> p q h", h=2)
                    dst = FA[:, 512 * p + 256 * qh:512 * p + 256 * qh + 256].rearrange("p (q h c) -> p q h c", q=2, h=2)
                    last = v.tensor_copy(dst, src.unsqueeze(3).to_broadcast([P, 2, 2, DH]))
                inc(last, "rspread")
            dve.wait_ge(s["o_sum"], K0 + BLOCKS)
            for p in range(2):
                dve.wait_ge(s["rbc"], 2 * C + p + 1)
                inc(v.tensor_tensor(at32[:, p, :], PS[:, p, :], at32[:, p, :], ALU.mult), "at_norm")
            for p in range(2):
                dve.wait_ge(s["at_hi"], 2 * C + p + 1)
                inc(v.tensor_tensor(L.at[1][:, p, :], at32[:, p, :], L.at[0][:, p, :].bitcast(F32), ALU.subtract), "at_lo")
            first(dve, "x_att", 2 * C)
            for w in range(2):
                dve.wait_ge(s["wo_done"], 2 * C + w + 1)
                xt = x[:, b * TT + 2 * w:b * TT + 2 * w + 2, :].rearrange("p t n -> p (t n)")
                inc(v.scalar_tensor_tensor(xt, PS[:, 3 + w, :], tg[:, L.layer:L.layer + 1], xt, ALU.mult, ALU.add), "x_att")

        dve.wait_ge(s["cst_in"], 80)
        dve.wait_ge(s["gates"], 1)
        s0 = CONST.index("s0")
        step(v.tensor_scalar(tg[:, 4:6], cst[:, s0:s0 + 2], 2.0, None, ALU.mult))
        step(v.tensor_tensor(tg[:, 6:7], cst[:, s0 + 2:s0 + 3], tg[:, 2:3], ALU.mult))
        q_ = CONST.index("qn")
        step(v.tensor_scalar(tg[:, 7:8], cst[:, q_:q_ + 1], SCALE, None, ALU.mult))
        dve.wait_ge(s["bo_in"], 16)
        inc(v.tensor_scalar(bo[:, :], bo[:, :], tg[:, 0:1], None, ALU.mult), "bo_gated")
        ctx_v = FA[:, 0:CT * DC].rearrange("p (t n) -> p t n", t=CT)
        for b in range(NB):
            dve.wait_ge(s[f"x_in{b}"], 16)
            norm(2 * b + 1, b, x_tiles(b))
            dve.wait_ge(s["ctx_in"], 16 * (b + 1))
            for t in range(CT):
                last = v.bn_stats(st6[:, t, :], ctx_v[:, t, :])
            step(last)
            dve.wait_ge(s["ln_xn"], 2 * b + 1)
            step.wait()
            for t in range(CT):
                last = v.bn_aggr(mv[:, t, :], st6[:, t, :])
            step(last)
            step.wait()
            step(v.tensor_scalar(rr[:, 2 * CT:3 * CT], mv[:, :, 1], LN_EPS, None, ALU.add))
            step.wait()
            inc(v.reciprocal(rr[:, 0:CT], rr[:, 2 * CT:3 * CT]), "cx_var")
            dve.wait_ge(s["cx_std"], b + 1)
            for t in range(CT):
                last = v.tensor_scalar(ctx_v[:, t, :], ctx_v[:, t, :], mv[:, t, 0:1], rr[:, CT + t:CT + t + 1],
                                       ALU.subtract, ALU.mult)
            inc(last, "cx_xn")
            dve.wait_ge(s["cx_xn"], b + 1)
            norm(2 * b + 2, b, lambda t: xn[:, t, :])
            dve.wait_ge(s["mask_in"], 16 * (b + 1))
            step(v.tensor_scalar(maskbias[:, 0:NCTX], mask8, BIG, -BIG, ALU.mult, ALU.add))
            step(v.memset(maskbias[:, NCTX:NK0], 0.0))
            step.wait()
            inc(v.tensor_copy(nmax[:, 4:5], maskbias[:, 0:1]), "maskbias_ready")
            for kt in range(KT):
                dve.wait_ge(s["ln_hi"], 2 * b + kt + 1)
                inc(v.tensor_tensor(LNL0[:, kt, :], FA[:, 2560 + 512 * kt:3072 + 512 * kt],
                                    LNH0[:, kt, :].bitcast(F32), ALU.subtract), "ln_lo")
            for i in range(4):
                gg, kt = i // 2, i % 2
                rows = P if kt == 0 else DC1
                cols = slice(gg * 512, gg * 512 + 512)
                dve.wait_ge(s["cx_hi"], 4 * b + i + 1)
                inc(v.tensor_tensor(XC0[1][0:rows, kt, cols], FB[0:rows, 1792 + 512 * kt:2304 + 512 * kt],
                                    XC0[0][0:rows, kt, cols].bitcast(F32), ALU.subtract), "cx_lo")
            dve.wait_ge(s["qk0_norm"], b + 1)
            step(v.tensor_scalar(rr[:, 64:128], rr[:, 64:128], 1e-8, None, ALU.max))
            step.wait()
            inc(v.reciprocal(rr[:, 0:64], rr[:, 64:128]), "qk0_rr")
            for t in range(L0.kt):
                dve.wait_ge(s["v0_hi"], 12 * b + t + 1)
                inc(v.tensor_tensor(L0.v[:, t, :, DH:P], PS[:, 5 + t % 3, 0:256].rearrange("p (h c) -> p h c", h=HG),
                                    L0.v[:, t, :, 0:DH].bitcast(F32), ALU.subtract), "v0_lo")
            dve.wait_ge(s["qk0_rr"], b + 1)

            def spread(i):
                if i >= 2:
                    dve.wait_ge(s["qk0_rb"], 8 * b + i - 1)
                c = 1792 + 512 * (i % 2)
                inc(v.tensor_copy(FB[:, c:c + 512].rearrange("p (n c) -> p n c", c=DH),
                                  rr[:, 8 * i:8 * i + 8].unsqueeze(2).to_broadcast([P, 8, DH])), "qk0_spread")

            spread(0)
            for i in range(8 + 1):
                if i + 1 < 8:
                    spread(i + 1)
                if i < 8:
                    dve.wait_ge(s["qk0_rb"], 8 * b + i + 1)
                    gain = tg[:, 7:8] if i < 2 else cst[:, q_ + 1:q_ + 2]
                    raw = FA[:, 512 * i:512 * i + 512]
                    inc(v.scalar_tensor_tensor(raw, raw, gain, PS[:, i % 4, :], ALU.mult, ALU.mult), "qk0_scaled")
                if i >= 1:
                    dve.wait_ge(s["qk0_hi"], 8 * b + i)
                    inc(v.tensor_tensor(qk_dst(i - 1, 1), FA[:, 512 * (i - 1):512 * i], qk_dst(i - 1, 0).bitcast(F32),
                                        ALU.subtract), "qk0_lo")
            dve.wait_ge(s["bo_added"], b + 1)
            attention(L0, b, b)

        dve.wait_ge(s["x_att"], 4)
        for b in range(NB):
            if b:
                dve.wait_ge(s["ln_turned"], NB + b)
            norm(2 * NB + b + 1, b, x_tiles(b))
            split_norm(NB + b + 1, b)

        def ffn_split(j, r, hi, lo):
            dve.wait_ge(s["f_act"], j + 1)
            inc(v.tensor_copy(hi, hf[:, r, :]), "f_hi")
            dve.wait_ge(s["f_hi"], j + 1)
            inc(v.tensor_tensor(lo, hf[:, r, :], hi.bitcast(F32), ALU.subtract), "f_lo")

        for j in range(2 * MT):
            m, h = j // 2, j % 2
            ffn_split(j, h, h1[0][:, m, h * 512:h * 512 + 512], h1[1][:, m, h * 512:h * 512 + 512])
        with dve.Fori(0, MT // 2) as i:
            for c in range(4):
                dve.wait_ge(s["f3_done"], AHEAD_F3 + 4 * i + c - 1)
                ffn_split(2 * MT + 4 * i + c, c % 2, fh2[:, c % 2, 0, :], fh2[:, c % 2, 1, :])
        dve.wait_ge(s["f3_done"], AHEAD_F3 + 2 * MT)

        def x_update(gate, name):
            for w in range(4):
                xt = x[:, 2 * w:2 * w + 2, :].rearrange("p t n -> p (t n)")
                last = v.scalar_tensor_tensor(xt, PS[:, 4 + w, :], tg[:, gate:gate + 1], xt, ALU.mult, ALU.add)
                if name == "out_ready":
                    last.then_inc(s[name], 2)
            return last

        inc(x_update(6, "x_ffn"), "x_ffn")
        dve.wait_ge(s["bo_in"], 32)
        inc(v.tensor_scalar(bo[:, :], bo[:, :], tg[:, 1:2], None, ALU.mult), "bo_gated")
        dve.wait_ge(s["x_ffn"], 1)
        for b in range(NB):
            dve.wait_ge(s["ln_turned"], 2 * NB + b)
            norm(3 * NB + b + 1, b, x_tiles(b))
            split_norm(2 * NB + b + 1, b)
        dve.wait_ge(s["bo_added"], 2 * NB)
        with dve.Fori(0, NG1) as g_:
            for b in range(NB):
                C = 2 * g_ + b + 2
                J0 = 28 * g_ + 14 * b
                for j in range(14):
                    dve.wait_ge(s["pj_hi"], J0 + j + 1)
                    if j < 2:
                        ins = v.scalar_tensor_tensor(L1.q[1][:, j, :], PS[:, j, :], SCALE, L1.q[0][:, j, :].bitcast(F32),
                                                     ALU.mult, ALU.subtract)
                    elif j < 6:
                        p, n = (j - 2) // 2, (j - 2) % 2
                        cols = slice(n * 512, n * 512 + 512)
                        ins = v.tensor_tensor(L1.k[1][:, p, cols], PS[:, j, :], L1.k[0][:, p, cols].bitcast(F32),
                                              ALU.subtract)
                    else:
                        ins = v.tensor_tensor(L1.v[:, j - 6, :, DH:P],
                                              PS[:, j % 8, 0:256].rearrange("p (h c) -> p h c", h=HG),
                                              L1.v[:, j - 6, :, 0:DH].bitcast(F32), ALU.subtract)
                    inc(ins, "pj_lo")
                attention(L1, b, C)

        dve.wait_ge(s["x_att"], 4 + 4 * NG1)
        for b in range(NB):
            dve.wait_ge(s["ln_turned"], 3 * NB + b)
            norm(4 * NB + b + 1, b, x_tiles(b))
            split_norm(3 * NB + b + 1, b)

        NT = NB * TT
        dve.wait_ge(s["ln_turned"], 4 * NB)
        dve.wait_ge(s["gate_sig"], 1)
        sig = wst[:, 1728:1856].rearrange("p (t e) -> p t e", t=NT)
        biased = FA[:, 0:128].rearrange("p (t e) -> p t e", t=NT)
        expert_bias = cst[:, 20:36].unsqueeze(1).to_broadcast([P, NT, E])
        ids = cst[:, 36:52]

        def do(ins):
            step(ins)
            step.wait()

        do(v.tensor_tensor(biased, sig, expert_bias, ALU.add))
        quad = FA[:, 0:128].rearrange("p (a b c) -> p a b c", b=2, c=2)
        hi2 = FA[:, 128:192].rearrange("p (a b) -> p a b", b=2)
        lo2 = FA[:, 192:256].rearrange("p (a b) -> p a b", b=2)
        do(v.tensor_tensor(hi2, quad[:, :, :, 0], quad[:, :, :, 1], ALU.max))
        do(v.tensor_tensor(lo2, quad[:, :, :, 0], quad[:, :, :, 1], ALU.min))
        top, mid, low, grp = (FA[:, 256 + 32 * k:288 + 32 * k] for k in range(4))
        do(v.tensor_tensor(top, hi2[:, :, 0], hi2[:, :, 1], ALU.max))
        do(v.tensor_tensor(mid, hi2[:, :, 0], hi2[:, :, 1], ALU.min))
        do(v.tensor_tensor(low, lo2[:, :, 0], lo2[:, :, 1], ALU.max))
        do(v.tensor_tensor(mid, mid, low, ALU.max))
        do(v.tensor_tensor(grp, top, mid, ALU.add))
        better = FA[:, 384:512].rearrange("p (k t g) -> p k t g", k=4, t=NT)
        do(v.memset(FA[:, 384:512], 0.0))
        g4 = grp.rearrange("p (t g) -> p t g", t=NT)
        for k in range(4):
            if k:
                do(v.tensor_tensor(better[:, k, :, 0:k], g4[:, :, k:k + 1].to_broadcast([P, NT, k]), g4[:, :, 0:k],
                                   ALU.is_gt))
            if k < 3:
                do(v.tensor_tensor(better[:, k, :, k + 1:4], g4[:, :, k:k + 1].to_broadcast([P, NT, 3 - k]),
                                   g4[:, :, k + 1:4], ALU.is_ge))
        rank = FA[:, 512:544]
        do(v.tensor_reduce(rank, FA[:, 384:512].rearrange("p (k n) -> p n k", k=4), AX.X, ALU.add))
        do(v.tensor_scalar(rank, rank, 2.0, None, ALU.is_lt))
        do(v.tensor_scalar(rank, rank, BIG, -BIG, ALU.mult, ALU.add))
        masked = FA[:, 640:768]
        do(v.tensor_tensor(masked.rearrange("p (n j) -> p n j", j=4), FA[:, 0:128].rearrange("p (n j) -> p n j", j=4),
                           rank.unsqueeze(2).to_broadcast([P, 32, 4]), ALU.add))
        best = FA[:, 768:832]
        index = FA[:, 832:896]
        for t in range(NT):
            last = v.max(best[:, 8 * t:8 * t + 8], masked[:, E * t:E * t + E])
        do(last)
        for t in range(NT):
            last = v.max_index(index[:, 8 * t:8 * t + 8].bitcast(U32), best[:, 8 * t:8 * t + 8], masked[:, E * t:E * t + E])
        do(last)
        do(v.tensor_copy(best, index.bitcast(U32)))
        chosen = FA[:, 3584:4096].rearrange("p (t k e) -> p t k e", t=NT, k=4)
        for t in range(NT):
            last = v.tensor_tensor(chosen[:, t], best[:, 8 * t:8 * t + 4].unsqueeze(2).to_broadcast([P, 4, E]),
                                   ids.unsqueeze(1).to_broadcast([P, 4, E]), ALU.is_equal)
        do(last)
        pick = FA[:, 896:1024].rearrange("p (t e) -> p t e", t=NT)
        do(v.tensor_reduce(pick, chosen.rearrange("p t k e -> p t e k"), AX.X, ALU.add))
        do(v.tensor_tensor(pick, pick, sig, ALU.mult))
        den = FA[:, 544:552]
        do(v.tensor_reduce(den, pick, AX.X, ALU.add))
        do(v.tensor_scalar(den, den, 1e-20, None, ALU.add))
        do(v.reciprocal(FA[:, 552:560], den))
        do(v.tensor_scalar(FA[:, 552:560], FA[:, 552:560], 2.5, None, ALU.mult))
        inc(v.tensor_tensor(wst[:, 1600:1728].rearrange("p (t e) -> p t e", t=NT), pick,
                            FA[:, 552:560].unsqueeze(2).to_broadcast([P, NT, E]), ALU.mult), "rt_comb")
        dve.wait_ge(s["rt_turned"], 1)
        for w in range(2):
            inc(v.tensor_copy(FA[0:E, 1024 + 512 * w:1536 + 512 * w], PS[0:E, w, :]), "rt_copied")
        inc(v.memset(FA[0:2 * ET - 3 * E, 2560:3584], 1.0), "rt_copied")

        with dve.Fori(0, ET // 2) as i:
            for c in range(4):
                r, h = c // 2, c % 2
                dve.wait_ge(s["e_silu"], 4 * i + c + 1)
                dve.wait_ge(s[f"comb_in{r}"], 32 * i + 32)
                inc(v.tensor_tensor(hcomb[:, h, :], silu[:, h, :], comb[:, r, h * 512:h * 512 + 512], ALU.mult), "e_comb")
                dve.wait_ge(s["e_comb"], 4 * i + c + 1)
                inc(v.tensor_tensor(hful[:, h, :], hcomb[:, h, :], PS[:, 2 * h + 1, :], ALU.mult), "e_full")
                dve.wait_ge(s["e_hi"], 4 * i + c + 1)
                inc(v.tensor_tensor(eh[:, h, 1, :], hful[:, h, :], eh[:, h, 0, :].bitcast(F32), ALU.subtract), "e_lo")
        dve.wait_ge(s["e_y"], AHEAD_Y + 2 * ET)
        x_update(3, "out_ready")


def kernel(**inputs):
    import numpy as np
    import concourse.bacc as bacc
    from concourse.bass_utils import run_bass_kernel_spmd

    a = {k: np.asarray(v) for k, v in inputs.items()}

    def pack(*parts):
        out = []
        for w in parts:
            rows, cols = w.shape
            tiles = -(-rows // 128)
            full = np.zeros((tiles * 128, cols), w.dtype)
            full[:rows] = w
            out.append(full.reshape(tiles, 128, cols).transpose(1, 0, 2).reshape(128, tiles * cols))
        return np.concatenate(out, axis=1)

    w0 = pack(a["L0_xattn_Wq"].T, a["L0_xattn_Wlkv"].T, a["L0_xattn_Wkv"].T, a["L0_xattn_Wo"].T)
    w1 = np.stack([pack(*[a[f"L1_xattn_{n}"][:, 256 * g:256 * g + 256] for n in ("Wq", "Wk", "Wv")],
                        a["L1_xattn_Wo"][256 * g:256 * g + 256]) for g in range(4)])

    def experts(routed, shared):
        w = np.concatenate([routed.reshape(E * EI, D), shared])
        return np.concatenate([w, np.zeros((ET * 128 - len(w), D), w.dtype)]).T

    g_in, u_in = experts(a["L1_ffn_w1"], a["L1_ffn_ws1"]), experts(a["L1_ffn_w3"], a["L1_ffn_ws3"])
    y_out = experts(a["L1_ffn_w2"].transpose(0, 2, 1), a["L1_ffn_ws2"].T).T
    we = np.stack([pack(g_in[:, 128 * j:128 * j + 128], u_in[:, 128 * j:128 * j + 128], y_out[128 * j:128 * j + 128])
                   for j in range(ET)])
    k1 = np.stack([pack(a["L0_ffn_k1"][:, 128 * m:128 * m + 128]) for m in range(MT)])
    k2 = a["L0_ffn_k2"].reshape(MT, 128, D)

    def column(v):
        full = np.zeros(128, np.float32)
        full[:len(v)] = v
        return full

    def same(v):
        return np.broadcast_to(v, 128)

    cst = np.stack([column(a["L0_xattn_ln_x_g"][:128]), column(a["L0_xattn_ln_x_g"][128:]),
                    column(a["L0_xattn_ln_x_b"][:128]), column(a["L0_xattn_ln_x_b"][128:]),
                    a["L0_xattn_ln_l_g"][:128], a["L0_xattn_ln_l_g"][128:],
                    a["L0_xattn_ln_l_b"][:128], a["L0_xattn_ln_l_b"][128:],
                    np.tile(a["L0_xattn_qn_g"], 2), np.tile(a["L0_xattn_kn_g"], 2),
                    same(a["L0_ffn_s0"]), same(a["L0_ffn_s1"]), same(a["L0_ffn_s2"]),
                    same(a["g_xattn"][0]), same(a["g_xattn"][1]), same(a["g_ffn"][0]), same(a["g_ffn"][1])], axis=1)
    half_ones = np.zeros((128, 2), np.float32)
    half_ones[:DH, 0] = half_ones[DH:, 1] = 1 / DH
    arrays = {
        "x": a["x"], "ctx": a["ctx_768"], "ctxT": a["ctx_768"].reshape(NB * NCTX, DC).T,
        "mask": a["mask_BxS2_bk0"],
        "cst": cst, "bo": np.stack([a["L0_xattn_bo"], a["L1_xattn_bo"]]), "gbias": a["L1_ffn_gate_bias"],
        "w0": w0, "k0": a["L0_ffn_k0"], "k1": k1, "k2": k2,
        "w1": w1, "gw": pack(a["L1_ffn_gate_w"].T), "we": we, "eye": np.eye(128, dtype=np.float32),
        "ones": half_ones, "iota": np.arange(E, dtype=np.float32),
    }
    arrays = {f"{k}_in": np.ascontiguousarray(v) for k, v in arrays.items()}
    nc = bacc.Bacc("TRN2", target_bir_lowering=False, num_devices=1)
    args = [nc.dram_tensor(k, v.shape, mybir.dt.from_np(v.dtype), kind="ExternalInput").ap() for k, v in arrays.items()]
    out = nc.dram_tensor("out", (NB, S, D), F32, kind="ExternalOutput").ap()
    comb = nc.dram_tensor("comb", (2 * ET, NB * S), F32, kind="Internal").ap()
    build(nc, *args, out, comb)
    result = run_bass_kernel_spmd(nc, [arrays], core_ids=[0])
    return result.results[0]["out"]
```

```python
from contextlib import ExitStack

import concourse.bass as bass
from concourse import mybir
from concourse.alu_op_type import AluOpType as ALU

F32 = mybir.dt.float32
F32R = mybir.dt.float32r
U8 = mybir.dt.uint8
U32 = mybir.dt.uint32
ACT = mybir.ActivationFunctionType
AX = mybir.AxisListType

P = 128
NB, S, D = 2, 512, 256
KT = D // P
TT = S // P
NCTX, DC = 1024, 192
DC1 = DC - P
CT = NCTX // P
DH = 64
NK0 = NCTX + S
NK1 = NCTX
HG = 4
NG1 = 1024 // DH // HG
UNITS = 16
BLOCKS = UNITS // 2
FF = 1024
MT = FF // P
E, EI = 16, 192
ET = 26
LN_EPS = 1e-5
SCALE = DH ** -0.5
BIG = 3.0e38

PROJ_BANKS = [0, 1, 3, 4]
OUT_AT = 9
AHEAD_F3, AHEAD_Y, AHEAD_G = 2, 4, 4

W0 = {"q": 0, "lkv": 512, "kv": 1536, "wo": 2560}
W0_COLS = 3072
W1 = {"q": 0, "k": 512, "v": 1024, "wo": 1536}
W1_COLS = 2048
WE_COLS = 768
CHUNK = 1024

R_LN, R_W, R_XC = 0, 4096, 10240
R_AT = 2048
R_ATT0 = 14336
R_ATT1 = 18432
R_COLS = 40960

CONST = ["ln_x_g0", "ln_x_g1", "ln_x_b0", "ln_x_b1", "ln_l_g0", "ln_l_g1", "ln_l_b0", "ln_l_b1",
         "qn", "kn", "s0", "s1", "s2", "gx0", "gx1", "gf0", "gf1"]
NC_ = len(CONST)


def build(nc, x_d, ctx_d, ctxT_d, mask_d, cst_d, bo_d, gbias_d, w0_d, k0_d, k1_d, k2_d, w1_d, gw_d, we_d,
          eye_d, ones_d, iota_d, out_d, comb_d):
    with ExitStack() as stack:
        program(nc, stack, x_d, ctx_d, ctxT_d, mask_d, cst_d, bo_d, gbias_d, w0_d, k0_d, k1_d, k2_d, w1_d,
                gw_d, we_d, eye_d, ones_d, iota_d, out_d, comb_d)


def program(nc, stack, x_d, ctx_d, ctxT_d, mask_d, cst_d, bo_d, gbias_d, w0_d, k0_d, k1_d, k2_d, w1_d,
            gw_d, we_d, eye_d, ones_d, iota_d, out_d, comb_d):
    def sb(name, shape, dt=F32):
        return stack.enter_context(nc.sbuf_tensor(name, shape, dt))

    def sem(name):
        return stack.enter_context(nc.semaphore(name))

    R = sb("R", [P, R_COLS], F32R)
    zero = sb("zero", [P, P], F32R)
    x = sb("x", [P, NB * TT, D])
    eye = sb("eye", [P, P])
    cst = sb("cst", [P, 52])
    half_ones = sb("half_ones", [P, 2])
    tg = sb("tg", [P, 8])
    bo = sb("bo", [P, D])
    st6 = sb("st6", [P, 8, 6])
    mv = sb("mv", [P, 8, 2])
    rstd = sb("rstd", [P, 16])
    nmax = sb("nmax", [P, 8])
    sums = sb("sums", [P, 32])
    rr = sb("rr", [P, 128])
    FA = sb("FA", [P, 4096])
    FB = sb("FB", [P, 2816])
    wst = sb("wst", [P, 2048])

    LNH0 = R[:, R_LN:R_LN + 1024].rearrange("p (k n) -> p k n", k=KT)
    LNL0 = R[:, R_LN + 1024:R_LN + 2048].rearrange("p (k n) -> p k n", k=KT)
    LNH = R[:, R_LN:R_LN + 2048].rearrange("p (k n) -> p k n", k=KT)
    LNL = R[:, R_LN + 2048:R_LN + 4096].rearrange("p (k n) -> p k n", k=KT)
    XC0 = [R[:, R_XC + 2048 * j:R_XC + 2048 * (j + 1)].rearrange("p (k n) -> p k n", k=2) for j in range(2)]
    XC1 = [R[:, R_XC + 4096 * j:R_XC + 4096 * (j + 1)].rearrange("p (k n) -> p k n", k=2) for j in range(2)]
    WH = R[:, R_W:R_W + W0_COLS]
    WL = R[:, R_W + W0_COLS:R_W + 2 * W0_COLS]
    xn = FA[:, 1536:2560].rearrange("p (t n) -> p t n", t=TT)

    PS = stack.enter_context(nc.psum_tensor("PS", [P, 8, 512], F32))

    class Attention:

        def __init__(self, layer):
            self.layer = layer
            nk = NK0 if layer == 0 else NK1
            self.nk, self.kt, self.ng, self.nb = nk, nk // P, nk // 512, nk // 512
            at = R_ATT0 if layer == 0 else R_ATT1

            def take(cols):
                nonlocal at
                at += cols
                return R[:, at - cols:at]

            self.q = take(HG * 512).rearrange("p (j n) -> p j n", j=HG)
            self.k = take(HG * nk).rearrange("p (j n) -> p j n", j=HG)
            self.q_lo = (take(1024) if layer == 1 else R[:, R_LN:R_LN + 1024]).rearrange("p (j n) -> p j n", j=2)
            self.v = take(self.kt * 512).rearrange("p (t h c) -> p t h c", h=HG, c=P)
            self.pt = [take(2 * self.kt * 256).rearrange("p (r t n) -> p r t n", r=2, t=self.kt) for _ in range(2)]
            if layer == 1:
                self.at = [take(1024).rearrange("p (j n) -> p j n", j=2) for _ in range(2)]
            else:
                self.at = [R[:, R_AT + 1024 * j:R_AT + 1024 * (j + 1)].rearrange("p (j n) -> p j n", j=2)
                           for j in range(2)]
            self.probs = FA[:, 0:2 * nk].rearrange("p (r n) -> p r n", r=2)
            self.tmp = FA[:, 3072:3584].rearrange("p (r n) -> p r n", r=2)
            self.wo = (W0 if layer == 0 else W1)["wo"]
            self.score = [PS[:, 3 * r:3 * r + self.nb, :].rearrange("p b n -> p (b n)") for r in range(2)]

        def turn(self, u, g_):
            if g_ == 0:
                return PS[:, 6, :]
            return PS[:, 2, :] if self.layer == 1 else PS[:, 3 * (u % 2) + g_, :]

    L0, L1 = Attention(0), Attention(1)

    def key_block(i):
        return (i, slice(0, 512)) if i < 2 else ((i - 2) // 3, slice((i - 2) % 3 * 512, (i - 2) % 3 * 512 + 512))

    maskbias = FB[:, 0:NK0]
    mask8 = FB[:, NK0:NK0 + 256].bitcast(U8)
    at32 = FB[:, 1792:2816].rearrange("p (j n) -> p j n", j=2)

    h1 = [R[:, 18432 + 8192 * j:18432 + 8192 * (j + 1)].rearrange("p (k n) -> p k n", k=MT) for j in range(2)]
    fw0 = R[:, 34816:36864].rearrange("p (k n) -> p k n", k=KT)
    fw1 = R[:, 36864:38912].rearrange("p (r k n) -> p r k n", r=2, k=MT)
    fh2 = R[:, 38912:40960].rearrange("p (r j n) -> p r j n", r=2, j=2)
    fw2 = R[:, 9216:9728].rearrange("p (r n) -> p r n", r=2)
    hf = FA[:, 0:1024].rearrange("p (r n) -> p r n", r=2)
    k0b = FA[:, 2560:3584].bitcast(U8).rearrange("p (k n) -> p k n", k=4)
    k12b = FB[:, 2048:2688].bitcast(U8).rearrange("p (r n) -> p r n", r=2)
    k0t = FA[:, 3584:4096]

    ew = [[R[:, R_W + 1536 * r + 768 * j:R_W + 1536 * r + 768 * (j + 1)] for j in range(2)] for r in range(2)]
    eh = R[:, 18432:20480].rearrange("p (r j n) -> p r j n", r=2, j=2)
    gw = [R[:, 20480 + 32 * j:20512 + 32 * j].rearrange("p (k n) -> p k n", k=KT) for j in range(2)]
    est = wst[:, 0:1536].rearrange("p (r n) -> p r n", r=2)
    silu = FA[:, 0:1024].rearrange("p (r n) -> p r n", r=2)
    hcomb = FA[:, 1024:2048].rearrange("p (r n) -> p r n", r=2)
    hful = FA[:, 2560:3584].rearrange("p (r n) -> p r n", r=2)
    comb = FB[:, 0:2048].rearrange("p (r n) -> p r n", r=2)
    gst = wst[:, 1536:1568]

    names = (
        "x_in0 x_in1 ctx_in mask_in cst_in bo_in w0_in0 w0_in1 w1_in k0_in k1_in0 k1_in1 ctxT_in0 ctxT_in1 gw_in we_in0 we_in1 comb_in0 comb_in1 "
        "comb_out stores zeroed gates bo_gated bo_added w0_split maskbias_ready "
        "ln_var ln_std ln_xn ln_turned ln_aff ln_hi ln_lo cx_var cx_std cx_xn cx_turned cx_aff cx_hi cx_lo "
        "qk0_done qk0_raw qk0_sq qk0_ss qk0_norm qk0_rr qk0_spread qk0_rb qk0_scaled qk0_hi qk0_lo v0_done v0_hi v0_lo "
        "scored maxed expd turned p_hi p_lo pv_done o_tmp o_sum rsum rspread rbc at_norm at_hi at_lo wo_done x_att "
        "q_twice cx_twice pj_done pj_hi pj_lo w1q_split w1o_split xc_hi xc_lo "
        "fw0_ready fw1_ready f1_done f2_done f_act f_hi f_lo f3_done x_ffn "
        "gw_split gate_done gate_sig rt_comb rt_turned rt_copied e_split_in e_split_out g_done u_done e_comb e_silu e_full e_hi e_lo e_y "
        "out_ready dve_step act_step pool_step pool_free").split()
    s = {n: sem(n) for n in names}

    def first(eng, name, value):
        if not isinstance(value, int) or value > 0:
            eng.wait_ge(s[name], value)

    class Steps:

        def __init__(self, eng, name):
            self.eng, self.sem, self.base, self.n = eng, s[name], 0, 0

        def __call__(self, ins):
            self.n += 1
            ins.then_inc(self.sem, 1)

        def wait(self):
            self.eng.wait_ge(self.sem, self.base + self.n)

    mm = nc.tensor.matmul
    eye_ap = eye[:, :]

    def three(pairs):
        out = []
        for (ah, al), (bh, bl) in pairs:
            out += [(ah, bh), (al, bh), (ah, bl)]
        return out

    def group(out, passes, skip=False):
        for n, (a, b) in enumerate(passes):
            last = mm(out, a, b, start=(n == 0), stop=(n == len(passes) - 1), skip_group_check=skip)
        return last

    def wcol(layer, name, kt, width, a, b):
        off = (W0 if layer == 0 else W1)[name] + kt * width
        return off + a, off + b

    def wpair(layer, name, kt, width, a, b, rows=P):
        lo, hi = wcol(layer, name, kt, width, a, b)
        return WH[0:rows, lo:hi], WL[0:rows, lo:hi]

    def context_passes(layer, name, width, a, b, xc, c, z, weights_first):
        w0, w1 = wpair(layer, name, 0, width, a, b), wpair(layer, name, 1, width, a, b)
        x0 = tuple(xc[j][:, 0, c:z] for j in range(2))
        pairs = [(w0[0], x0[0]), (w0[1], x0[0]), (w0[0], x0[1]),
                 (w1[0], xc[0][:, 1, c:z]), (w1[0][0:DC1], xc[1][0:DC1, 1, c:z])]
        return pairs if weights_first else [(x_, w) for w, x_ in pairs]

    halves = [(slice(0, DH), slice(DH, P)), (slice(DH, P), slice(0, DH))]

    block = stack.enter_context(nc.Block())

    @block.sync
    def _(sp):
        sp.sem_inc(s["f3_done"], AHEAD_F3)
        sp.sem_inc(s["e_y"], AHEAD_Y)
        sp.sem_inc(s["g_done"], AHEAD_G)
        sp.dma_start(x[:, 0:TT, :], x_d[0].rearrange("(t p) n -> p t n", p=P)).then_inc(s["x_in0"], 16)
        sp.dma_start(cst[:, 0:NC_], cst_d).then_inc(s["cst_in"], 16)
        sp.dma_start(eye[:, :], eye_d).then_inc(s["cst_in"], 16)
        sp.dma_start(cst[:, 20:36], gbias_d.partition_broadcast(P)).then_inc(s["cst_in"], 16)
        sp.dma_start(cst[:, 36:52], iota_d.partition_broadcast(P)).then_inc(s["cst_in"], 16)
        sp.dma_start(half_ones[:, :], ones_d).then_inc(s["cst_in"], 16)
        ctx_v = FA[:, 0:CT * DC].rearrange("p (t n) -> p t n", t=CT)
        sp.dma_start(ctx_v, ctx_d[0].rearrange("(t p) n -> p t n", p=P)).then_inc(s["ctx_in"], 16)
        sp.dma_start(wst[:, 0:CHUNK], w0_d[:, 0:CHUNK]).then_inc(s["w0_in0"], 16)
        sp.dma_start(wst[:, CHUNK:2 * CHUNK], w0_d[:, CHUNK:2 * CHUNK]).then_inc(s["w0_in1"], 16)
        sp.dma_start(mask8, mask_d[0:1, :].partition_broadcast(P)).then_inc(s["mask_in"], 16)
        sp.dma_start(x[:, TT:2 * TT, :], x_d[1].rearrange("(t p) n -> p t n", p=P)).then_inc(s["x_in1"], 16)
        sp.dma_start(bo[:, :], bo_d[0:1, :].partition_broadcast(P)).then_inc(s["bo_in"], 16)
        sp.wait_ge(s["w0_split"], 1)
        sp.dma_start(wst[:, 0:CHUNK], w0_d[:, 2 * CHUNK:3 * CHUNK]).then_inc(s["w0_in0"], 16)
        sp.wait_ge(s["maskbias_ready"], 1)
        sp.dma_start(mask8, mask_d[1:2, :].partition_broadcast(P)).then_inc(s["mask_in"], 16)
        sp.wait_ge(s["o_sum"], BLOCKS)
        sp.wait_ge(s["rbc"], 2)
        sp.dma_start(ctx_v, ctx_d[1].rearrange("(t p) n -> p t n", p=P)).then_inc(s["ctx_in"], 16)
        sp.wait_ge(s["bo_added"], NB)
        sp.dma_start(bo[:, :], bo_d[1:2, :].partition_broadcast(P)).then_inc(s["bo_in"], 16)
        sp.wait_ge(s["w0_split"], 3)
        sp.dma_start(wst[:, 0:W1_COLS], w1_d[0]).then_inc(s["w1_in"], 16)
        sp.wait_ge(s["rbc"], 4)
        sp.wait_ge(s["o_sum"], 2 * BLOCKS)
        sp.dma_start(k0b, k0_d.rearrange("(k p) n -> p k n", p=P)).then_inc(s["k0_in"], 16)
        sp.wait_ge(s["x_att"], 4)
        sp.wait_ge(s["maxed"], 2 * UNITS)

        def context_load(c):
            kt, h = c // 2, c % 2
            for to in ((0,) if kt == 0 else (0, DC1)):
                rows = P if kt == 0 else DC1
                sp.dma_start(FB[to:to + rows, 1024 * h:1024 * h + 1024],
                             ctxT_d[kt * P:kt * P + rows, h * 1024:h * 1024 + 1024]).then_inc(s[f"ctxT_in{h}"], 16)

        def ffn_load(m):
            sp.dma_start(k12b[:, m % 2, 0:FF], k1_d[m]).then_inc(s[f"k1_in{m % 2}"], 16)
            sp.dma_start(k12b[:, m % 2, FF:FF + D], k2_d[m]).then_inc(s[f"k1_in{m % 2}"], 16)

        for c in range(2):
            context_load(c)
            ffn_load(c)
        for c in range(2):
            sp.wait_ge(s["xc_lo"], c + 1)
            context_load(c + 2)
        for m in range(2, MT):
            sp.wait_ge(s["fw1_ready"], m - 1)
            ffn_load(m)
        sp.wait_ge(s["w1o_split"], 1)
        sp.dma_start(wst[:, 0:W1_COLS], w1_d[1]).then_inc(s["w1_in"], 16)
        with sp.Fori(0, NG1 - 2) as g:
            sp.wait_ge(s["w1o_split"], g + 2)
            sp.dma_start(wst[:, 0:W1_COLS], w1_d[bass.ds(g + 2, 1)].rearrange("g p n -> (g p) n")).then_inc(s["w1_in"], 16)
        sp.wait_ge(s["w1o_split"], NG1)
        sp.dma_start(gst, gw_d).then_inc(s["gw_in"], 16)
        sp.dma_start(est[:, 0, :], we_d[0]).then_inc(s["we_in0"], 16)
        sp.dma_start(est[:, 1, :], we_d[1]).then_inc(s["we_in1"], 16)
        sp.wait_ge(s["rt_copied"], 3)
        sp.dma_start(comb_d[3 * E:2 * ET, :], FA[0:2 * ET - 3 * E, 2560:3584]).then_inc(s["comb_out"], 16)
        routed = comb_d[0:3 * E, :].rearrange("(e r) n -> e r n", r=3)
        for r in range(3):
            sp.dma_start(routed[:, r, :], FA[0:E, 1024:2048]).then_inc(s["comb_out"], 16)
        sp.wait_ge(s["comb_out"], 64)

        def comb_load(row, r, name):
            for half in range(2):
                sp.dma_start(comb[64 * half:64 * half + 64, r, :],
                             comb_d[bass.ds(row + half, 1), :].partition_broadcast(64).rearrange("q o n -> q (o n)")
                             ).then_inc(s[name], 16)

        comb_load(0, 0, "comb_in0")
        comb_load(2, 1, "comb_in1")
        with sp.Fori(0, ET // 2 - 1) as i:
            for r in range(2):
                sp.wait_ge(s["e_split_out"], 2 * i + r + 1)
                sp.dma_start(est[:, r, :], we_d[bass.ds(2 * i + 2 + r, 1)].rearrange("g p n -> (g p) n")
                             ).then_inc(s[f"we_in{r}"], 16)
                sp.wait_ge(s["e_full"], 4 * i + 2 * r + 2)
                comb_load(4 * i + 4 + 2 * r, r, f"comb_in{r}")
        for t in range(NB * TT):
            sp.wait_ge(s["out_ready"], t + 1)
            sp.dma_start(out_d[t // TT, (t % TT) * P:(t % TT) * P + P, :], x[:, t, :]).then_inc(s["stores"], 16)
        sp.wait_ge(s["stores"], 16 * NB * TT)

    @block.gpsimd
    def _(pool):
        step = Steps(pool, "pool_step")
        g = nc.gpsimd

        def split(hi, lo, src):
            step(g.tensor_scalar(hi, src, 1.0, 0.0, ALU.mult, ALU.add))
            step.wait()
            return g.tensor_tensor(lo, src, hi.bitcast(F32), ALU.subtract)

        def stack_low(c, n):
            return g.tensor_scalar(WH[DC1:P, c:c + n], WL[DC1:P, c:c + n].bitcast(F32), 1.0, 0.0, ALU.mult, ALU.add)

        def copy_queries(L, C, count):
            name = "qk0_hi" if L.layer == 0 else "pj_hi"
            pool.wait_ge(s[name], count)
            for slot in range(HG):
                rows, other = halves[slot % 2]
                pool.sem_inc(s["pool_free"], 1)
                g.tensor_scalar(L.q[other, slot, :], L.q[rows, slot, :].bitcast(F32), 1.0, 0.0, ALU.mult,
                                ALU.add).then_inc(s["q_twice"], 1)
                pool.wait_ge(s["q_twice"], HG * C + slot + 1)
            pool.sem_inc(s["pool_free"], 1)

        g.memset(zero[:, :].bitcast(F32), 0.0).then_inc(s["zeroed"], 1)
        for c in range(W0_COLS // CHUNK):
            pool.wait_ge(s[f"w0_in{c % 2}"], 16 * (c // 2 + 1))
            src = wst[:, (c % 2) * CHUNK:(c % 2) * CHUNK + CHUNK]
            last = split(WH[:, c * CHUNK:(c + 1) * CHUNK], WL[:, c * CHUNK:(c + 1) * CHUNK], src)
            if c == W0["kv"] // CHUNK + 1:
                step(last)
                step.wait()
                last = stack_low(W0["kv"] + 512, 512)
            last.then_inc(s["w0_split"], 1)
            if c == W0["kv"] // CHUNK + 1:
                pool.wait_ge(s["w0_split"], c + 1)
        for b in range(NB):
            pool.wait_ge(s["ln_xn"], 2 * b + 1)
            pool.wait_ge(s["bo_gated"], 1)
            for t in range(TT):
                last = g.tensor_tensor(x[:, b * TT + t, :], x[:, b * TT + t, :], bo[:, :], ALU.add)
            last.then_inc(s["bo_added"], 1)
            pool.wait_ge(s["cx_hi"], 4 * b + 4)
            pool.wait_ge(s["bo_added"], b + 1)
            g.tensor_scalar(XC0[0][DC1:P, 1, :], XC0[0][0:DC1, 1, :].bitcast(F32), 1.0, 0.0, ALU.mult,
                            ALU.add).then_inc(s["cx_twice"], 1)
            pool.wait_ge(s["cx_twice"], b + 1)
            copy_queries(L0, b, 8 * b + 2)
        pool.wait_ge(s["k0_in"], 16)
        pool.wait_ge(s["at_lo"], 4)
        pool.wait_ge(s["wo_done"], 4)
        for kt in range(KT):
            for h in range(2):
                cols = slice(512 * h, 512 * h + 512)
                step(g.tensor_scalar(k0t, k0b[:, KT + kt, cols], -2.0, None, ALU.mult))
                step.wait()
                step(g.tensor_scalar(fw0[:, kt, cols], k0b[:, kt, cols], 2.0, None, ALU.mult))
                step.wait()
                last = g.tensor_tensor(fw0[:, kt, cols], fw0[:, kt, cols].bitcast(F32), k0t, ALU.add)
                step(last)
                step.wait()
        g.tensor_scalar(fw0[:, 0, 0:1], fw0[:, 0, 0:1].bitcast(F32), 1.0, None, ALU.mult).then_inc(s["fw0_ready"], 1)
        for m in range(MT):
            pool.wait_ge(s[f"k1_in{m % 2}"], 32 * (m // 2 + 1))
            if m >= 2:
                pool.wait_ge(s["f3_done"], AHEAD_F3 + 2 * m - 2)
            step(g.tensor_scalar(fw1[:, m % 2].rearrange("p k n -> p (k n)"), k12b[:, m % 2, 0:FF], 2.0, -1.0, ALU.mult, ALU.add))
            step.wait()
            g.tensor_scalar(fw2[:, m % 2], k12b[:, m % 2, FF:FF + D], 2.0, -1.0, ALU.mult, ALU.add).then_inc(s["fw1_ready"], 1)
            if m == 1:
                for c in range(4):
                    kt, h = c // 2, c % 2
                    pool.wait_ge(s[f"ctxT_in{h}"], 16 if kt == 0 else 48)
                    cols = slice(1024 * h, 1024 * h + 1024)
                    split(XC1[0][:, kt, cols], XC1[1][:, kt, cols], FB[:, cols]).then_inc(s["xc_lo"], 1)
                pool.wait_ge(s["w1_in"], 16)
                n = W1["wo"]
                step(split(WH[:, 0:n], WL[:, 0:n], wst[:, 0:n]))
                step.wait()
                stack_low(W1["k"] + 256, 256)
                stack_low(W1["v"] + 256, 256).then_inc(s["w1q_split"], 1)
                pool.wait_ge(s["w1q_split"], 1)
                split(WH[:, n:W1_COLS], WL[:, n:W1_COLS], wst[:, n:W1_COLS]).then_inc(s["w1o_split"], 1)
        for b in range(NB):
            pool.wait_ge(s["ln_xn"], 2 * NB + NB + b + 1)
            pool.wait_ge(s["bo_gated"], 2)
            for t in range(TT):
                last = g.tensor_tensor(x[:, b * TT + t, :], x[:, b * TT + t, :], bo[:, :], ALU.add)
            last.then_inc(s["bo_added"], 1)

        pool.wait_ge(s["bo_added"], 2 * NB)
        copy_queries(L1, 2, 2)
        with pool.Fori(1, NG1) as i:
            copy_queries(L1, 2 * i + 1, 28 * i - 14 + 2)
            pool.wait_ge(s["w1_in"], 16 * i + 16)
            pool.wait_ge(s["pj_done"], 28 * i)
            n = W1["wo"]
            pool.sem_inc(s["pool_free"], 1)
            g.tensor_scalar(WH[:, 0:n], wst[:, 0:n], 1.0, 0.0, ALU.mult, ALU.add).then_inc(s["pool_step"], 1)
            pool.wait_ge(s["pool_step"], step.n + 3 * (i - 1) + 1)
            g.tensor_tensor(WL[:, 0:n], wst[:, 0:n], WH[:, 0:n].bitcast(F32), ALU.subtract).then_inc(s["pool_step"], 1)
            pool.wait_ge(s["pool_step"], step.n + 3 * (i - 1) + 2)
            pool.sem_inc(s["pool_free"], 1)
            stack_low(W1["k"] + 256, 256)
            stack_low(W1["v"] + 256, 256).then_inc(s["w1q_split"], 1)
            pool.wait_ge(s["w1q_split"], i + 1)
            copy_queries(L1, 2 * i + 2, 28 * i + 2)
            pool.wait_ge(s["wo_done"], 4 + 4 * i)
            pool.sem_inc(s["pool_free"], 1)
            g.tensor_scalar(WH[:, n:W1_COLS], wst[:, n:W1_COLS], 1.0, 0.0, ALU.mult, ALU.add).then_inc(s["pool_step"], 1)
            pool.wait_ge(s["pool_step"], step.n + 3 * (i - 1) + 3)
            g.tensor_tensor(WL[:, n:W1_COLS], wst[:, n:W1_COLS], WH[:, n:W1_COLS].bitcast(F32),
                            ALU.subtract).then_inc(s["w1o_split"], 1)
            pool.wait_ge(s["w1o_split"], i + 1)
        step.n += 3 * (NG1 - 1)
        copy_queries(L1, 2 * NG1 + 1, 28 * NG1 - 14 + 2)
        pool.wait_ge(s["gw_in"], 16)
        pool.wait_ge(s["wo_done"], 4 + 4 * NG1)
        split(gw[0].rearrange("p k n -> p (k n)"), gw[1].rearrange("p k n -> p (k n)"), gst).then_inc(s["gw_split"], 1)
        base = step.n
        with pool.Fori(0, ET // 2) as i:
            for r in range(2):
                pool.wait_ge(s[f"we_in{r}"], 16 * i + 16)
                pool.wait_ge(s["g_done"], AHEAD_G + 4 * i + 2 * r - 2)
                pool.sem_inc(s["pool_free"], 1)
                g.tensor_scalar(ew[r][0][:, 0:512], est[:, r, 0:512], 1.0, 0.0, ALU.mult, ALU.add).then_inc(s["pool_step"], 1)
                pool.wait_ge(s["pool_step"], base + 4 * i + 2 * r + 1)
                g.tensor_tensor(ew[r][1][:, 0:512], est[:, r, 0:512], ew[r][0][:, 0:512].bitcast(F32),
                                ALU.subtract).then_inc(s["e_split_in"], 1)
                pool.wait_ge(s["e_y"], AHEAD_Y + 4 * i + 2 * r - 2)
                pool.sem_inc(s["pool_free"], 1)
                g.tensor_scalar(ew[r][0][:, 512:768], est[:, r, 512:768], 1.0, 0.0, ALU.mult, ALU.add).then_inc(s["pool_step"], 1)
                pool.wait_ge(s["pool_step"], base + 4 * i + 2 * r + 2)
                g.tensor_tensor(ew[r][1][:, 512:768], est[:, r, 512:768], ew[r][0][:, 512:768].bitcast(F32),
                                ALU.subtract).then_inc(s["e_split_out"], 1)

    @block.tensor
    def _(pe):
        def ln_turn(n, double):
            pe.wait_ge(s["ln_xn"], n)
            for kt in range(KT):
                for t in range(TT):
                    last = nc.tensor.transpose(PS[:, kt, t * P:t * P + P], xn[:, t, kt * P:kt * P + P], eye_ap)
            last.then_inc(s["ln_turned"], 1)

        def attention(L, b, C):
            U0, K0 = UNITS * C, BLOCKS * C
            G0 = L.ng * UNITS * C if L.layer == 0 else 32 * C + 32

            def scores(u, n):
                p, h, qt = u // 8, (u // 2) % 2, ((u // 4) % 2) * 2 + u % 2
                rows = slice(DH * h, DH * h + DH)
                if n == 0:
                    first(pe, "expd", U0 + u - 1)
                elif L.layer == 0 and u >= 2:
                    pe.wait_ge(s["p_lo"], G0 + L.ng * (u - 2) + n + 1)
                tok, keys = slice(qt * P, qt * P + P), slice(n * 512, n * 512 + 512)
                last = group(L.score[u % 2][:, keys],
                             [(L.q[:, 2 * p + h, tok], L.k[:, 2 * p + h, keys]),
                              (L.q_lo[rows, p, tok], L.k[rows, 2 * p + h, keys])])
                if n == L.nb - 1:
                    last.then_inc(s["scored"], 1)

            def turn(u, g_):
                G = G0 + L.ng * u + g_
                if g_ == 0:
                    pe.wait_ge(s["expd"], U0 + u + 1)
                if L.layer == 1 or g_ == 0:
                    first(pe, "p_lo", G - L.ng + 1)
                out = L.turn(u, g_)
                for i in range(4):
                    c = (4 * g_ + i) * P
                    last = nc.tensor.transpose(out[:, i * P:i * P + P], L.probs[:, u % 2, c:c + P], eye_ap)
                last.then_inc(s["turned"], 1)

            def values(k, half):
                hd = 2 * (k // 4) + k % 2
                if half == 0:
                    pe.wait_ge(s["p_lo"], G0 + L.ng * (2 * k + 2))
                    first(pe, "o_sum", K0 + k)
                n = L.kt // 2
                for kt in range(half * n, half * n + n):
                    for j in range(2):
                        last = mm(PS[:, 7, 0:256], L.v[:, kt, hd, :], L.pt[j][:, k % 2, kt, :],
                                  start=(kt == 0 and j == 0), stop=(kt == L.kt - 1 and j == 1))
                if half == 1:
                    last.then_inc(s["pv_done"], 1)

            pe.wait_ge(s["q_twice"], HG * C + HG)
            for u in (0, 1):
                for n in range(L.nb):
                    scores(u, n)
            first(pe, "x_att", 2 * C)
            for u in range(UNITS + 2):
                if u < UNITS:
                    for g_ in range(L.ng):
                        turn(u, g_)
                if u + 2 < UNITS:
                    scores(u + 2, 0)
                    if L.layer == 1:
                        scores(u + 2, 1)
                if u >= 2:
                    values(u // 2 - 1, u % 2)
                if u + 2 < UNITS and L.layer == 0:
                    scores(u + 2, 1)
                    scores(u + 2, 2)

        def out_rows(C):
            pe.wait_ge(s["rspread"], 2 * C + 2)
            for p in range(2):
                for qt in range(TT):
                    c = 512 * p + P * qt
                    last = mm(PS[:, 2 + 3 * p, qt * P:qt * P + P], FA[:, c:c + P], eye_ap, start=True, stop=True)
                last.then_inc(s["rbc"], 1)

        def out_project(L, C):
            pe.wait_ge(s["at_lo"], 2 * C + 2)
            for w in range(2):
                for e in range(2):
                    tt = 2 * w + e
                    pairs = [(tuple(L.at[j][:, p, tt * P:tt * P + P] for j in range(2)),
                              (WH[:, L.wo + p * D:L.wo + p * D + D], WL[:, L.wo + p * D:L.wo + p * D + D]))
                             for p in range(2)]
                    last = group(PS[:, 6 + w, e * D:e * D + D], three(pairs))
                last.then_inc(s["wo_done"], 1)

        pe.wait_ge(s["cst_in"], 80)
        for b in range(NB):
            ln_turn(2 * b + 2, True)
            pe.wait_ge(s["cx_xn"], b + 1)
            ctx_v = FA[:, 0:CT * DC].rearrange("p (t n) -> p t n", t=CT)
            for gg in range(2):
                for kt in range(2):
                    rows = P if kt == 0 else DC1
                    for t in range(4):
                        last = nc.tensor.transpose(PS[0:rows, 2 + 2 * gg + kt, t * P:t * P + P],
                                                   ctx_v[:, 4 * gg + t, kt * P:kt * P + rows], eye_ap)
                    last.then_inc(s["cx_turned"], 1)
            pe.wait_ge(s["ln_lo"], 2 * b + 2)
            pe.wait_ge(s["cx_lo"], 4 * b + 4)
            pe.wait_ge(s["cx_twice"], b + 1)
            pe.wait_ge(s["w0_split"], 3)

            def square_sums(i):
                pe.wait_ge(s["qk0_sq"], 8 * b + i + 1)
                for tt in range(TT):
                    last = mm(PS[:, 4, i * 8 + tt * 2:i * 8 + tt * 2 + 2],
                              FB[:, 1792 + 512 * (i % 2) + tt * P:1792 + 512 * (i % 2) + tt * P + P],
                              half_ones[:, :], start=True, stop=True)
                last.then_inc(s["qk0_ss"], 1)

            lat = [(LNH0[:, kt, :], LNL0[:, kt, :]) for kt in range(KT)]
            for i in range(8):
                if i >= 4:
                    pe.wait_ge(s["qk0_sq"], 8 * b + i - 3)
                if i < 2:
                    passes = three([(wpair(0, "q", kt, 256, i * P, i * P + P), lat[kt]) for kt in range(KT)])
                else:
                    p, n = (i - 2) // 3, (i - 2) % 3
                    if n < 2:
                        passes = context_passes(0, "kv", 512, p * P, p * P + P, XC0, n * 512, n * 512 + 512, True)
                    else:
                        passes = three([(wpair(0, "lkv", kt, 512, p * P, p * P + P), lat[kt]) for kt in range(KT)])
                group(PS[:, i % 4, :], passes).then_inc(s["qk0_done"], 1)
                if i >= 1:
                    square_sums(i - 1)
            square_sums(7)
            for t in range(L0.kt):
                if t >= 3:
                    pe.wait_ge(s["v0_lo"], 12 * b + t - 2)
                if t < CT:
                    passes = context_passes(0, "kv", 512, 256, 512, XC0, t * P, t * P + P, False)
                else:
                    c = (t - CT) * P
                    passes = three([((LNH0[:, kt, c:c + P], LNL0[:, kt, c:c + P]), wpair(0, "lkv", kt, 512, 256, 512))
                                    for kt in range(KT)])
                group(PS[:, 5 + t % 3, 0:256], passes).then_inc(s["v0_done"], 1)
            for i in range(8):
                if i >= 4:
                    pe.wait_ge(s["qk0_scaled"], 8 * b + i - 3)
                pe.wait_ge(s["qk0_spread"], 8 * b + i + 1)
                for tt in range(TT):
                    c = 1792 + 512 * (i % 2) + tt * P
                    last = mm(PS[:, i % 4, tt * P:tt * P + P], FB[:, c:c + P], eye_ap, start=True, stop=True)
                last.then_inc(s["qk0_rb"], 1)
            pe.wait_ge(s["qk0_lo"], 8 * b + 8)
            pe.wait_ge(s["v0_lo"], 12 * b + 12)
            attention(L0, b, b)
            out_rows(b)
            out_project(L0, b)

        pe.wait_ge(s["x_att"], 4)
        for b in range(NB):
            ln_turn(2 * NB + b + 1, False)
            pe.wait_ge(s["ln_lo"], 2 * NB + 2 * (b + 1))
        pe.wait_ge(s["fw0_ready"], 1)
        for j in range(2 * MT):
            m, h = j // 2, j % 2
            if j >= 4:
                pe.wait_ge(s["f_act"], j - 3)
            passes = [(fw0[:, kt, m * P:m * P + P], X[:, kt, h * 512:h * 512 + 512])
                      for kt in range(KT) for X in (LNH, LNL)]
            group(PS[:, j % 4, :], passes).then_inc(s["f1_done"], 1)
        pe.wait_ge(s["zeroed"], 1)
        for w in range(4):
            last = mm(PS[:, 4 + w, :], zero[:, :], LNH[:, 0, 0:512], start=True, stop=False, skip_group_check=True)
        pe.wait_ge(s["f_lo"], 2 * MT)

        def ffn2(j, m, r, h):
            if h == 0:
                pe.wait_ge(s["fw1_ready"], m + 1)
            pe.wait_ge(s["f_act"], 2 * MT + j - 3)
            passes = [(fw1[:, r, kt, :], X[:, kt, h * 512:h * 512 + 512]) for kt in range(MT) for X in h1]
            group(PS[:, (2 * r + h) % 4, :], passes).then_inc(s["f2_done"], 1)

        def ffn3(j, r, h):
            pe.wait_ge(s["f_lo"], 2 * MT + j + 1)
            for tt in range(TT):
                T = TT * h + tt
                for part in range(2):
                    last = mm(PS[:, 4 + T // 2, (T % 2) * D:(T % 2) * D + D], fh2[:, h, part, tt * P:tt * P + P],
                              fw2[:, r, :], start=False, stop=False, skip_group_check=True)
            last.then_inc(s["f3_done"], 1)

        ffn2(0, 0, 0, 0)
        with pe.Fori(0, MT // 2 - 1) as i:
            for c in range(4):
                ffn2(4 * i + c + 1, 2 * i + (c + 1) // 2, ((c + 1) // 2) % 2, (c + 1) % 2)
                ffn3(4 * i + c, c // 2, c % 2)
        base = 2 * MT - 4
        for c in range(4):
            if c < 3:
                ffn2(base + c + 1, MT - 2 + (c + 1) // 2, (c + 1) // 2, (c + 1) % 2)
            ffn3(base + c, c // 2, c % 2)
        pe.wait_ge(s["x_ffn"], 1)

        for b in range(NB):
            ln_turn(3 * NB + b + 1, False)
            pe.wait_ge(s["ln_lo"], 4 * NB + 2 * (b + 1))
        pe.wait_ge(s["xc_lo"], 4)

        def project(b, J0, jobs):
            for j in jobs:
                if j >= 4:
                    pe.wait_ge(s["pj_lo"], J0 + j - 3)
                out = PS[:, PROJ_BANKS[j % 4], :]
                if j < 2:
                    passes = three([(wpair(1, "q", kt, 256, j * P, j * P + P),
                                     (LNH[:, kt, b * S:b * S + S], LNL[:, kt, b * S:b * S + S])) for kt in range(KT)])
                elif j < 6:
                    p, c = (j - 2) // 2, NCTX * b + (j - 2) % 2 * 512
                    passes = context_passes(1, "k", 256, p * P, p * P + P, XC1, c, c + 512, True)
                else:
                    c = NCTX * b + (j - 6) * P
                    passes = context_passes(1, "v", 256, 0, 256, XC1, c, c + P, False)
                    out = out[:, 0:256]
                group(out, passes).then_inc(s["pj_done"], 1)

        def heads(g_, more):
            for b in range(NB):
                C = 2 * g_ + b + 2
                nxt = b == 0 or more
                J1 = 28 * g_ + 14 * (b + 1)
                pe.wait_ge(s["pj_lo"], J1)
                attention(L1, b, C)
                if nxt:
                    if b == 1:
                        pe.wait_ge(s["w1q_split"], g_ + 2)
                    pe.wait_ge(s["expd"], UNITS * C + UNITS)
                    project(1 - b, J1, range(6))
                out_rows(C)
                if nxt:
                    project(1 - b, J1, range(6, 14))
                if b == 0:
                    pe.wait_ge(s["w1o_split"], g_ + 1)
                out_project(L1, C)

        pe.wait_ge(s["w1q_split"], 1)
        project(0, 0, range(14))
        with pe.Fori(0, NG1 - 1) as g_:
            heads(g_, True)
        heads(NG1 - 1, False)
        pe.wait_ge(s["x_att"], 4 + 4 * NG1)

        for b in range(NB):
            ln_turn(4 * NB + b + 1, False)
            pe.wait_ge(s["ln_lo"], 6 * NB + 2 * (b + 1))
        pe.wait_ge(s["gw_split"], 1)
        for t in range(NB * TT):
            c = t * P
            passes = three([((LNH[:, kt, c:c + P], LNL[:, kt, c:c + P]), (gw[0][:, kt, :], gw[1][:, kt, :]))
                            for kt in range(KT)])
            last = group(PS[:, 2, t * E:t * E + E], passes)
        last.then_inc(s["gate_done"], 1)
        for w in range(4):
            last = mm(PS[:, 4 + w, :], zero[:, :], LNH[:, 0, 0:512], start=True, stop=False, skip_group_check=True)
        pe.wait_ge(s["rt_comb"], 1)
        for t in range(NB * TT):
            last = nc.tensor.transpose(PS[0:E, t // TT, (t % TT) * P:(t % TT) * P + P], wst[:, 1600 + t * E:1600 + t * E + E],
                                       eye_ap)
        last.then_inc(s["rt_turned"], 1)
        pe.wait_ge(s["rt_copied"], 2)

        def gate_up(j, tile, r, h):
            if h == 0:
                pe.wait_ge(s["e_split_in"], tile + 1)
            first(pe, "e_full", j - 1)
            for part in (1, 0):
                c = part * 256
                pairs = [((ew[r][0][:, c + kt * P:c + kt * P + P], ew[r][1][:, c + kt * P:c + kt * P + P]),
                          (LNH[:, kt, h * 512:h * 512 + 512], LNL[:, kt, h * 512:h * 512 + 512]))
                         for kt in range(KT)]
                group(PS[:, 2 * h + part, :], three(pairs)).then_inc(s["g_done" if part == 0 else "u_done"], 1)

        def down(j, tile, r, h):
            if h == 0:
                pe.wait_ge(s["e_split_out"], tile + 1)
            pe.wait_ge(s["e_lo"], j + 1)
            for tt in range(TT):
                T = TT * h + tt
                for a, w in three([((eh[:, h, 0, tt * P:tt * P + P], eh[:, h, 1, tt * P:tt * P + P]),
                                    (ew[r][0][:, 512:768], ew[r][1][:, 512:768]))]):
                    last = mm(PS[:, 4 + T // 2, (T % 2) * D:(T % 2) * D + D], a, w,
                              start=False, stop=False, skip_group_check=True)
            last.then_inc(s["e_y"], 1)

        gate_up(0, 0, 0, 0)
        gate_up(1, 0, 0, 1)
        with pe.Fori(0, ET // 2 - 1) as i:
            for c in range(4):
                gate_up(4 * i + c + 2, 2 * i + c // 2 + 1, (c // 2 + 1) % 2, c % 2)
                down(4 * i + c, 2 * i + c // 2, c // 2, c % 2)
        base = 2 * ET - 4
        for c in range(4):
            if c < 2:
                gate_up(base + c + 2, ET - 1, 1, c)
            down(base + c, ET - 2 + c // 2, c // 2, c % 2)

    @block.scalar
    def _(act):
        a_ = nc.scalar.activation
        col = {n: cst[:, i:i + 1] for i, n in enumerate(CONST)}

        def ln_root(n, cols=TT):
            act.wait_ge(s["ln_var"], n)
            a_(rstd[:, 8:8 + cols], rstd[:, 0:cols], ACT.Sqrt).then_inc(s["ln_std"], 1)

        def ln_split(n, b, dst):
            act.wait_ge(s["ln_turned"], n)
            for kt in range(KT):
                a_(dst[:, kt, b * S:b * S + S], PS[:, kt, :], ACT.Copy).then_inc(s["ln_hi"], 1)

        def attention(L, b, C):
            U0, K0 = UNITS * C, BLOCKS * C
            G0 = L.ng * UNITS * C if L.layer == 0 else 32 * C + 32

            def exp(u):
                act.wait_ge(s["maxed"], U0 + u + 1)
                first(act, "turned", G0 + L.ng * (u - 1))
                a_(L.probs[:, u % 2, :], L.score[u % 2], ACT.Exp, bias=nmax[:, u % 2:u % 2 + 1], scale=1.0,
                   accum_out=sums[:, u:u + 1]).then_inc(s["expd"], 1)

            def out_copy(k):
                h = k % 2
                act.wait_ge(s["pv_done"], K0 + k + 1)
                first(act, "o_sum", K0 + k - 1)
                a_(L.tmp[DH * h:DH * h + DH, k % 2, :], PS[0:DH, 7, 0:256], ACT.Copy).then_inc(s["o_tmp"], 1)

            first(act, "rsum", C)
            exp(0)
            for u in range(UNITS + 3):
                if u >= 4 and u % 2 == 0:
                    out_copy(u // 2 - 2)
                if u < UNITS:
                    for g_ in range(L.ng):
                        G = G0 + L.ng * u + g_
                        act.wait_ge(s["turned"], G + 1)
                        if g_ == 0:
                            first(act, "pv_done", K0 + u // 2 - 1)
                        a_(L.pt[0][:, (u // 2) % 2, 4 * g_:4 * g_ + 4, (u % 2) * P:(u % 2) * P + P],
                           L.turn(u, g_).rearrange("p (t n) -> p t n", t=4), ACT.Copy).then_inc(s["p_hi"], 1)
                if u + 1 < UNITS:
                    exp(u + 1)

        def out_hi(L, C):
            for p in range(2):
                act.wait_ge(s["at_norm"], 2 * C + p + 1)
                a_(L.at[0][:, p, :], at32[:, p, :], ACT.Copy).then_inc(s["at_hi"], 1)

        act.wait_ge(s["cst_in"], 80)
        a_(tg[:, 0:4], cst[:, CONST.index("gx0"):CONST.index("gx0") + 4], ACT.Tanh).then_inc(s["gates"], 1)
        for b in range(NB):
            ln_root(2 * b + 1)
            act.wait_ge(s["cx_var"], b + 1)
            a_(rr[:, CT:2 * CT], rr[:, 0:CT], ACT.Sqrt).then_inc(s["cx_std"], 1)
            ln_root(2 * b + 2)
            act.wait_ge(s["ln_turned"], b + 1)
            for kt in range(KT):
                first(act, "qk0_lo", 8 * b)
                a_(FA[:, 2560 + 512 * kt:3072 + 512 * kt], PS[:, kt, :], ACT.Identity,
                   bias=col[f"ln_l_b{kt}"], scale=col[f"ln_l_g{kt}"]).then_inc(s["ln_aff"], 1)
                a_(LNH0[:, kt, :], PS[:, kt, :], ACT.Identity,
                   bias=col[f"ln_l_b{kt}"], scale=col[f"ln_l_g{kt}"]).then_inc(s["ln_hi"], 1)
            for i in range(4):
                gg, kt = i // 2, i % 2
                rows = P if kt == 0 else DC1
                act.wait_ge(s["cx_turned"], 4 * b + i + 1)
                first(act, "cx_lo", 4 * b + i - 1)
                src = PS[0:rows, 2 + 2 * gg + kt, :]
                gain = dict(bias=col[f"ln_x_b{kt}"][0:rows], scale=col[f"ln_x_g{kt}"][0:rows])
                a_(FB[0:rows, 1792 + 512 * kt:2304 + 512 * kt], src, ACT.Identity, **gain).then_inc(s["cx_aff"], 1)
                a_(XC0[0][0:rows, kt, gg * 512:gg * 512 + 512], src, ACT.Identity, **gain).then_inc(s["cx_hi"], 1)
            for i in range(8):
                act.wait_ge(s["qk0_done"], 8 * b + i + 1)
                a_(FA[:, 512 * i:512 * i + 512], PS[:, i % 4, :], ACT.Copy).then_inc(s["qk0_raw"], 1)
                first(act, "qk0_ss", 8 * b + i - 1)
                a_(FB[:, 1792 + 512 * (i % 2):2304 + 512 * (i % 2)], PS[:, i % 4, :], ACT.Square).then_inc(s["qk0_sq"], 1)
            act.wait_ge(s["qk0_ss"], 8 * b + 8)
            a_(rr[:, 64:128], PS[:, 4, 0:64], ACT.Sqrt).then_inc(s["qk0_norm"], 1)
            for t in range(L0.kt):
                act.wait_ge(s["v0_done"], 12 * b + t + 1)
                a_(L0.v[:, t, :, 0:DH], PS[:, 5 + t % 3, 0:256].rearrange("p (h c) -> p h c", h=HG),
                   ACT.Copy).then_inc(s["v0_hi"], 1)
            for i in range(8):
                act.wait_ge(s["qk0_scaled"], 8 * b + i + 1)
                p, cols = key_block(i)
                for h, (rows, other) in enumerate(halves):
                    last = a_((L0.q if i < 2 else L0.k)[rows, 2 * p + h, cols], FA[rows, 512 * i:512 * i + 512], ACT.Copy)
                last.then_inc(s["qk0_hi"], 1)
            act.wait_ge(s["qk0_lo"], 8 * b + 8)
            attention(L0, b, b)
            out_hi(L0, b)

        for b in range(NB):
            ln_root(2 * NB + b + 1)
            ln_split(NB + b + 1, b, LNH)
        for j in range(2 * MT):
            act.wait_ge(s["f1_done"], j + 1)
            if j >= 2:
                act.wait_ge(s["f_lo"], j - 1)
            a_(hf[:, j % 2, :], PS[:, j % 4, :], ACT.Relu, scale=tg[:, 4:5]).then_inc(s["f_act"], 1)
        with act.Fori(0, MT // 2) as i:
            for c in range(4):
                act.wait_ge(s["f2_done"], 4 * i + c + 1)
                act.wait_ge(s["f_lo"], 2 * MT + 4 * i + c - 1)
                a_(hf[:, c % 2, :], PS[:, c, :], ACT.Relu, scale=tg[:, 5:6]).then_inc(s["f_act"], 1)

        for b in range(NB):
            ln_root(3 * NB + b + 1)
            ln_split(2 * NB + b + 1, b, LNH)

        def project_hi(J0, jobs):
            for j in jobs:
                act.wait_ge(s["pj_done"], J0 + j + 1)
                src = PS[:, PROJ_BANKS[j % 4], :]
                if j < 6:
                    for h, (rows, other) in enumerate(halves):
                        if j < 2:
                            ins = a_(L1.q[rows, 2 * j + h, :], src[rows, :], ACT.Copy, scale=SCALE)
                        else:
                            p, n = (j - 2) // 2, (j - 2) % 2
                            ins = a_(L1.k[rows, 2 * p + h, n * 512:n * 512 + 512], src[rows, :], ACT.Copy)
                else:
                    ins = a_(L1.v[:, j - 6, :, 0:DH], src[:, 0:256].rearrange("p (h c) -> p h c", h=HG), ACT.Copy)
                ins.then_inc(s["pj_hi"], 1)

        def heads(g_, more):
            for b in range(NB):
                C = 2 * g_ + b + 2
                nxt = b == 0 or more
                J1 = 28 * g_ + 14 * (b + 1)
                attention(L1, b, C)
                if nxt:
                    project_hi(J1, range(OUT_AT))
                out_hi(L1, C)
                if nxt:
                    project_hi(J1, range(OUT_AT, 14))

        project_hi(0, range(14))
        with act.Fori(0, NG1 - 1) as g_:
            heads(g_, True)
        heads(NG1 - 1, False)
        for b in range(NB):
            ln_root(4 * NB + b + 1)
            ln_split(3 * NB + b + 1, b, LNH)
        act.wait_ge(s["gate_done"], 1)
        a_(wst[:, 1728:1856], PS[:, 2, 0:P], ACT.Sigmoid).then_inc(s["gate_sig"], 1)
        with act.Fori(0, ET // 2) as i:
            for c in range(4):
                act.wait_ge(s["g_done"], AHEAD_G + 4 * i + c + 1)
                a_(silu[:, c % 2, :], PS[:, 2 * (c % 2), :], ACT.Silu).then_inc(s["e_silu"], 1)
                act.wait_ge(s["e_full"], 4 * i + c + 1)
                act.wait_ge(s["e_y"], AHEAD_Y + 4 * i + c - 1)
                a_(eh[:, c % 2, 0, :], hful[:, c % 2, :], ACT.Copy).then_inc(s["e_hi"], 1)

    @block.vector
    def _(dve):
        step = Steps(dve, "dve_step")
        v = nc.vector

        def inc(ins, name):
            ins.then_inc(s[name], 1)

        def norm(n, b, src):
            for t in range(TT):
                last = v.bn_stats(st6[:, t, :], src(t))
            step(last)
            step.wait()
            for t in range(TT):
                last = v.bn_aggr(mv[:, t, :], st6[:, t, :])
            step(last)
            step.wait()
            step(v.tensor_scalar(rstd[:, 4:8], mv[:, 0:TT, 1], LN_EPS, None, ALU.add))
            step.wait()
            inc(v.reciprocal(rstd[:, 0:TT], rstd[:, 4:8]), "ln_var")
            dve.wait_ge(s["ln_std"], n)
            for t in range(TT):
                last = v.tensor_scalar(xn[:, t, :], src(t), mv[:, t, 0:1], rstd[:, 8 + t:9 + t], ALU.subtract, ALU.mult)
            inc(last, "ln_xn")

        def x_tiles(b):
            return lambda t: x[:, b * TT + t, :]

        def split_norm(n, b):
            for kt in range(KT):
                dve.wait_ge(s["ln_hi"], 2 * (n - 1) + kt + 1)
                cols = slice(b * S, b * S + S)
                inc(v.tensor_tensor(LNL[:, kt, cols], PS[:, kt, :], LNH[:, kt, cols].bitcast(F32), ALU.subtract), "ln_lo")

        def attention(L, b, C):
            U0, K0 = UNITS * C, BLOCKS * C
            G0 = L.ng * UNITS * C if L.layer == 0 else 32 * C + 32

            def maximum(u):
                r = u % 2
                dve.wait_ge(s["scored"], U0 + u + 1)
                first(dve, "expd", U0 + u - 1)
                if L.layer == 0:
                    step(v.tensor_tensor_reduce(L.score[r], L.score[r], maskbias, 1.0, -BIG, ALU.add, ALU.max,
                                                accum_out=nmax[:, 2 + r:3 + r]))
                    step.wait()
                    inc(v.tensor_scalar(nmax[:, r:r + 1], nmax[:, 2 + r:3 + r], -1.0, None, ALU.mult), "maxed")
                else:
                    inc(v.tensor_reduce(nmax[:, r:r + 1], L.score[r], AX.X, ALU.max, negate=True), "maxed")

            def split(u):
                for g_ in range(L.ng):
                    dve.wait_ge(s["p_hi"], G0 + L.ng * u + g_ + 1)
                    hi, lo = (L.pt[j][:, (u // 2) % 2, 4 * g_:4 * g_ + 4, (u % 2) * P:(u % 2) * P + P] for j in range(2))
                    turned = L.turn(u, g_).rearrange("p (t n) -> p t n", t=4)
                    inc(v.tensor_tensor(lo, turned, hi.bitcast(F32), ALU.subtract), "p_lo")

            def out_sum(k):
                p, qh, h = k // 4, (k // 2) % 2, k % 2
                dve.wait_ge(s["o_tmp"], K0 + k + 1)
                if k == 0:
                    first(dve, "at_hi", 2 * C)
                rows = slice(DH * h, DH * h + DH)
                inc(v.tensor_tensor(at32[rows, p, qh * 256:qh * 256 + 256], PS[DH:P, 7, 0:256], L.tmp[rows, k % 2, :],
                                    ALU.add), "o_sum")

            maximum(0)
            for u in range(UNITS + 3):
                if u + 1 < UNITS:
                    maximum(u + 1)
                if u >= 4 and u % 2 == 0:
                    out_sum(u // 2 - 2)
                if u < UNITS:
                    split(u)
            dve.wait_ge(s["expd"], U0 + UNITS)
            inc(v.reciprocal(rr[:, 0:UNITS], sums[:, 0:UNITS]), "rsum")
            dve.wait_ge(s["rsum"], C + 1)
            dve.wait_ge(s["turned"], G0 + L.ng * UNITS)
            for p in range(2):
                for qh in range(2):
                    src = rr[:, 8 * p + 4 * qh:8 * p + 4 * qh + 4].rearrange("p (h q) -> p q h", h=2)
                    dst = FA[:, 512 * p + 256 * qh:512 * p + 256 * qh + 256].rearrange("p (q h c) -> p q h c", q=2, h=2)
                    last = v.tensor_copy(dst, src.unsqueeze(3).to_broadcast([P, 2, 2, DH]))
                inc(last, "rspread")

        def out_norm(L, C):
            dve.wait_ge(s["o_sum"], BLOCKS * C + BLOCKS)
            for p in range(2):
                dve.wait_ge(s["rbc"], 2 * C + p + 1)
                inc(v.tensor_tensor(at32[:, p, :], PS[:, 2 + 3 * p, :], at32[:, p, :], ALU.mult), "at_norm")

        def out_lo(L, C):
            for p in range(2):
                dve.wait_ge(s["at_hi"], 2 * C + p + 1)
                inc(v.tensor_tensor(L.at[1][:, p, :], at32[:, p, :], L.at[0][:, p, :].bitcast(F32), ALU.subtract), "at_lo")

        def out_add(L, b, C):
            first(dve, "x_att", 2 * C)
            for w in range(2):
                dve.wait_ge(s["wo_done"], 2 * C + w + 1)
                xt = x[:, b * TT + 2 * w:b * TT + 2 * w + 2, :].rearrange("p t n -> p (t n)")
                inc(v.scalar_tensor_tensor(xt, PS[:, 6 + w, :], tg[:, L.layer:L.layer + 1], xt, ALU.mult, ALU.add), "x_att")

        dve.wait_ge(s["cst_in"], 80)
        dve.wait_ge(s["gates"], 1)
        s0 = CONST.index("s0")
        step(v.tensor_scalar(tg[:, 4:6], cst[:, s0:s0 + 2], 2.0, None, ALU.mult))
        step(v.tensor_tensor(tg[:, 6:7], cst[:, s0 + 2:s0 + 3], tg[:, 2:3], ALU.mult))
        q_ = CONST.index("qn")
        step(v.tensor_scalar(tg[:, 7:8], cst[:, q_:q_ + 1], SCALE, None, ALU.mult))
        dve.wait_ge(s["bo_in"], 16)
        inc(v.tensor_scalar(bo[:, :], bo[:, :], tg[:, 0:1], None, ALU.mult), "bo_gated")
        ctx_v = FA[:, 0:CT * DC].rearrange("p (t n) -> p t n", t=CT)
        for b in range(NB):
            dve.wait_ge(s[f"x_in{b}"], 16)
            norm(2 * b + 1, b, x_tiles(b))
            dve.wait_ge(s["ctx_in"], 16 * (b + 1))
            for t in range(CT):
                last = v.bn_stats(st6[:, t, :], ctx_v[:, t, :])
            step(last)
            dve.wait_ge(s["ln_xn"], 2 * b + 1)
            step.wait()
            for t in range(CT):
                last = v.bn_aggr(mv[:, t, :], st6[:, t, :])
            step(last)
            step.wait()
            step(v.tensor_scalar(rr[:, 2 * CT:3 * CT], mv[:, :, 1], LN_EPS, None, ALU.add))
            step.wait()
            inc(v.reciprocal(rr[:, 0:CT], rr[:, 2 * CT:3 * CT]), "cx_var")
            dve.wait_ge(s["cx_std"], b + 1)
            for t in range(CT):
                last = v.tensor_scalar(ctx_v[:, t, :], ctx_v[:, t, :], mv[:, t, 0:1], rr[:, CT + t:CT + t + 1],
                                       ALU.subtract, ALU.mult)
            inc(last, "cx_xn")
            dve.wait_ge(s["cx_xn"], b + 1)
            norm(2 * b + 2, b, lambda t: xn[:, t, :])
            dve.wait_ge(s["mask_in"], 16 * (b + 1))
            step(v.tensor_scalar(maskbias[:, 0:NCTX], mask8, BIG, -BIG, ALU.mult, ALU.add))
            step(v.memset(maskbias[:, NCTX:NK0], 0.0))
            step.wait()
            inc(v.tensor_copy(nmax[:, 4:5], maskbias[:, 0:1]), "maskbias_ready")
            for kt in range(KT):
                dve.wait_ge(s["ln_hi"], 2 * b + kt + 1)
                inc(v.tensor_tensor(LNL0[:, kt, :], FA[:, 2560 + 512 * kt:3072 + 512 * kt],
                                    LNH0[:, kt, :].bitcast(F32), ALU.subtract), "ln_lo")
            for i in range(4):
                gg, kt = i // 2, i % 2
                rows = P if kt == 0 else DC1
                cols = slice(gg * 512, gg * 512 + 512)
                dve.wait_ge(s["cx_hi"], 4 * b + i + 1)
                inc(v.tensor_tensor(XC0[1][0:rows, kt, cols], FB[0:rows, 1792 + 512 * kt:2304 + 512 * kt],
                                    XC0[0][0:rows, kt, cols].bitcast(F32), ALU.subtract), "cx_lo")
            dve.wait_ge(s["qk0_norm"], b + 1)
            step(v.tensor_scalar(rr[:, 64:128], rr[:, 64:128], 1e-8, None, ALU.max))
            step.wait()
            inc(v.reciprocal(rr[:, 0:64], rr[:, 64:128]), "qk0_rr")
            for t in range(L0.kt):
                dve.wait_ge(s["v0_hi"], 12 * b + t + 1)
                inc(v.tensor_tensor(L0.v[:, t, :, DH:P], PS[:, 5 + t % 3, 0:256].rearrange("p (h c) -> p h c", h=HG),
                                    L0.v[:, t, :, 0:DH].bitcast(F32), ALU.subtract), "v0_lo")
            dve.wait_ge(s["qk0_rr"], b + 1)

            def spread(i):
                if i >= 2:
                    dve.wait_ge(s["qk0_rb"], 8 * b + i - 1)
                c = 1792 + 512 * (i % 2)
                inc(v.tensor_copy(FB[:, c:c + 512].rearrange("p (n c) -> p n c", c=DH),
                                  rr[:, 8 * i:8 * i + 8].unsqueeze(2).to_broadcast([P, 8, DH])), "qk0_spread")

            spread(0)
            for i in range(8 + 1):
                if i + 1 < 8:
                    spread(i + 1)
                if i < 8:
                    dve.wait_ge(s["qk0_rb"], 8 * b + i + 1)
                    gain = tg[:, 7:8] if i < 2 else cst[:, q_ + 1:q_ + 2]
                    raw = FA[:, 512 * i:512 * i + 512]
                    inc(v.scalar_tensor_tensor(raw, raw, gain, PS[:, i % 4, :], ALU.mult, ALU.mult), "qk0_scaled")
                if i >= 1:
                    dve.wait_ge(s["qk0_hi"], 8 * b + i)
                    p, cols = key_block(i - 1)
                    for h, (rows, other) in enumerate(halves):
                        lo = L0.q_lo[rows, p, cols] if i <= 2 else L0.k[other, 2 * p + h, cols]
                        hi = (L0.q if i <= 2 else L0.k)[rows, 2 * p + h, cols]
                        last = v.tensor_tensor(lo, FA[rows, 512 * (i - 1):512 * i], hi.bitcast(F32), ALU.subtract)
                    inc(last, "qk0_lo")
            dve.wait_ge(s["bo_added"], b + 1)
            attention(L0, b, b)
            out_norm(L0, b)
            out_lo(L0, b)
            out_add(L0, b, b)

        dve.wait_ge(s["x_att"], 4)
        for b in range(NB):
            if b:
                dve.wait_ge(s["ln_turned"], NB + b)
            norm(2 * NB + b + 1, b, x_tiles(b))
            split_norm(NB + b + 1, b)

        def ffn_split(j, r, hi, lo):
            dve.wait_ge(s["f_act"], j + 1)
            inc(v.tensor_copy(hi, hf[:, r, :]), "f_hi")
            dve.wait_ge(s["f_hi"], j + 1)
            inc(v.tensor_tensor(lo, hf[:, r, :], hi.bitcast(F32), ALU.subtract), "f_lo")

        for j in range(2 * MT):
            m, h = j // 2, j % 2
            ffn_split(j, h, h1[0][:, m, h * 512:h * 512 + 512], h1[1][:, m, h * 512:h * 512 + 512])
        with dve.Fori(0, MT // 2) as i:
            for c in range(4):
                dve.wait_ge(s["f3_done"], AHEAD_F3 + 4 * i + c - 1)
                ffn_split(2 * MT + 4 * i + c, c % 2, fh2[:, c % 2, 0, :], fh2[:, c % 2, 1, :])
        dve.wait_ge(s["f3_done"], AHEAD_F3 + 2 * MT)

        def x_update(gate, name):
            for w in range(4):
                xt = x[:, 2 * w:2 * w + 2, :].rearrange("p t n -> p (t n)")
                last = v.scalar_tensor_tensor(xt, PS[:, 4 + w, :], tg[:, gate:gate + 1], xt, ALU.mult, ALU.add)
                if name == "out_ready":
                    last.then_inc(s[name], 2)
            return last

        inc(x_update(6, "x_ffn"), "x_ffn")
        dve.wait_ge(s["bo_in"], 32)
        inc(v.tensor_scalar(bo[:, :], bo[:, :], tg[:, 1:2], None, ALU.mult), "bo_gated")
        dve.wait_ge(s["x_ffn"], 1)
        for b in range(NB):
            dve.wait_ge(s["ln_turned"], 2 * NB + b)
            norm(3 * NB + b + 1, b, x_tiles(b))
            split_norm(2 * NB + b + 1, b)
        dve.wait_ge(s["bo_added"], 2 * NB)

        def project_lo(J0, jobs):
            for j in jobs:
                dve.wait_ge(s["pj_hi"], J0 + j + 1)
                src = PS[:, PROJ_BANKS[j % 4], :]
                if j < 6:
                    for h, (rows, other) in enumerate(halves):
                        if j < 2:
                            ins = v.scalar_tensor_tensor(L1.q_lo[rows, j, :], src[rows, :], SCALE,
                                                         L1.q[rows, 2 * j + h, :].bitcast(F32), ALU.mult, ALU.subtract)
                        else:
                            p, cols = (j - 2) // 2, slice((j - 2) % 2 * 512, (j - 2) % 2 * 512 + 512)
                            ins = v.tensor_tensor(L1.k[other, 2 * p + h, cols], src[rows, :],
                                                  L1.k[rows, 2 * p + h, cols].bitcast(F32), ALU.subtract)
                else:
                    ins = v.tensor_tensor(L1.v[:, j - 6, :, DH:P], src[:, 0:256].rearrange("p (h c) -> p h c", h=HG),
                                          L1.v[:, j - 6, :, 0:DH].bitcast(F32), ALU.subtract)
                inc(ins, "pj_lo")

        def heads(g_, more):
            for b in range(NB):
                C = 2 * g_ + b + 2
                nxt = b == 0 or more
                J1 = 28 * g_ + 14 * (b + 1)
                attention(L1, b, C)
                if nxt:
                    project_lo(J1, range(6))
                out_norm(L1, C)
                if nxt:
                    project_lo(J1, range(6, OUT_AT))
                out_lo(L1, C)
                if nxt:
                    project_lo(J1, range(OUT_AT, 14))
                out_add(L1, b, C)

        project_lo(0, range(14))
        with dve.Fori(0, NG1 - 1) as g_:
            heads(g_, True)
        heads(NG1 - 1, False)
        dve.wait_ge(s["x_att"], 4 + 4 * NG1)
        for b in range(NB):
            dve.wait_ge(s["ln_turned"], 3 * NB + b)
            norm(4 * NB + b + 1, b, x_tiles(b))
            split_norm(3 * NB + b + 1, b)

        NT = NB * TT
        dve.wait_ge(s["ln_turned"], 4 * NB)
        dve.wait_ge(s["gate_sig"], 1)
        sig = wst[:, 1728:1856].rearrange("p (t e) -> p t e", t=NT)
        biased = FA[:, 0:128].rearrange("p (t e) -> p t e", t=NT)
        expert_bias = cst[:, 20:36].unsqueeze(1).to_broadcast([P, NT, E])
        ids = cst[:, 36:52]

        def do(ins):
            step(ins)
            step.wait()

        do(v.tensor_tensor(biased, sig, expert_bias, ALU.add))
        quad = FA[:, 0:128].rearrange("p (a b c) -> p a b c", b=2, c=2)
        hi2 = FA[:, 128:192].rearrange("p (a b) -> p a b", b=2)
        lo2 = FA[:, 192:256].rearrange("p (a b) -> p a b", b=2)
        do(v.tensor_tensor(hi2, quad[:, :, :, 0], quad[:, :, :, 1], ALU.max))
        do(v.tensor_tensor(lo2, quad[:, :, :, 0], quad[:, :, :, 1], ALU.min))
        top, mid, low, grp = (FA[:, 256 + 32 * k:288 + 32 * k] for k in range(4))
        do(v.tensor_tensor(top, hi2[:, :, 0], hi2[:, :, 1], ALU.max))
        do(v.tensor_tensor(mid, hi2[:, :, 0], hi2[:, :, 1], ALU.min))
        do(v.tensor_tensor(low, lo2[:, :, 0], lo2[:, :, 1], ALU.max))
        do(v.tensor_tensor(mid, mid, low, ALU.max))
        do(v.tensor_tensor(grp, top, mid, ALU.add))
        better = FA[:, 384:512].rearrange("p (k t g) -> p k t g", k=4, t=NT)
        do(v.memset(FA[:, 384:512], 0.0))
        g4 = grp.rearrange("p (t g) -> p t g", t=NT)
        for k in range(4):
            if k:
                do(v.tensor_tensor(better[:, k, :, 0:k], g4[:, :, k:k + 1].to_broadcast([P, NT, k]), g4[:, :, 0:k],
                                   ALU.is_gt))
            if k < 3:
                do(v.tensor_tensor(better[:, k, :, k + 1:4], g4[:, :, k:k + 1].to_broadcast([P, NT, 3 - k]),
                                   g4[:, :, k + 1:4], ALU.is_ge))
        rank = FA[:, 512:544]
        do(v.tensor_reduce(rank, FA[:, 384:512].rearrange("p (k n) -> p n k", k=4), AX.X, ALU.add))
        do(v.tensor_scalar(rank, rank, 2.0, None, ALU.is_lt))
        do(v.tensor_scalar(rank, rank, BIG, -BIG, ALU.mult, ALU.add))
        masked = FA[:, 640:768]
        do(v.tensor_tensor(masked.rearrange("p (n j) -> p n j", j=4), FA[:, 0:128].rearrange("p (n j) -> p n j", j=4),
                           rank.unsqueeze(2).to_broadcast([P, 32, 4]), ALU.add))
        best = FA[:, 768:832]
        index = FA[:, 832:896]
        for t in range(NT):
            last = v.max(best[:, 8 * t:8 * t + 8], masked[:, E * t:E * t + E])
        do(last)
        for t in range(NT):
            last = v.max_index(index[:, 8 * t:8 * t + 8].bitcast(U32), best[:, 8 * t:8 * t + 8], masked[:, E * t:E * t + E])
        do(last)
        do(v.tensor_copy(best, index.bitcast(U32)))
        chosen = FA[:, 3584:4096].rearrange("p (t k e) -> p t k e", t=NT, k=4)
        for t in range(NT):
            last = v.tensor_tensor(chosen[:, t], best[:, 8 * t:8 * t + 4].unsqueeze(2).to_broadcast([P, 4, E]),
                                   ids.unsqueeze(1).to_broadcast([P, 4, E]), ALU.is_equal)
        do(last)
        pick = FA[:, 896:1024].rearrange("p (t e) -> p t e", t=NT)
        do(v.tensor_reduce(pick, chosen.rearrange("p t k e -> p t e k"), AX.X, ALU.add))
        do(v.tensor_tensor(pick, pick, sig, ALU.mult))
        den = FA[:, 544:552]
        do(v.tensor_reduce(den, pick, AX.X, ALU.add))
        do(v.tensor_scalar(den, den, 1e-20, None, ALU.add))
        do(v.reciprocal(FA[:, 552:560], den))
        do(v.tensor_scalar(FA[:, 552:560], FA[:, 552:560], 2.5, None, ALU.mult))
        inc(v.tensor_tensor(wst[:, 1600:1728].rearrange("p (t e) -> p t e", t=NT), pick,
                            FA[:, 552:560].unsqueeze(2).to_broadcast([P, NT, E]), ALU.mult), "rt_comb")
        dve.wait_ge(s["rt_turned"], 1)
        for w in range(2):
            inc(v.tensor_copy(FA[0:E, 1024 + 512 * w:1536 + 512 * w], PS[0:E, w, :]), "rt_copied")
        inc(v.memset(FA[0:2 * ET - 3 * E, 2560:3584], 1.0), "rt_copied")

        with dve.Fori(0, ET // 2) as i:
            for c in range(4):
                r, h = c // 2, c % 2
                dve.wait_ge(s["u_done"], 4 * i + c + 1)
                dve.wait_ge(s[f"comb_in{r}"], 32 * i + 32)
                inc(v.tensor_tensor(hcomb[:, h, :], PS[:, 2 * h + 1, :], comb[:, r, h * 512:h * 512 + 512], ALU.mult), "e_comb")
                dve.wait_ge(s["e_comb"], 4 * i + c + 1)
                dve.wait_ge(s["e_silu"], 4 * i + c + 1)
                inc(v.tensor_tensor(hful[:, h, :], hcomb[:, h, :], silu[:, h, :], ALU.mult), "e_full")
                dve.wait_ge(s["e_hi"], 4 * i + c + 1)
                inc(v.tensor_tensor(eh[:, h, 1, :], hful[:, h, :], eh[:, h, 0, :].bitcast(F32), ALU.subtract), "e_lo")
        dve.wait_ge(s["e_y"], AHEAD_Y + 2 * ET)
        x_update(3, "out_ready")


def kernel(**inputs):
    import numpy as np
    import concourse.bacc as bacc
    from concourse.bass_utils import run_bass_kernel_spmd

    a = {k: np.asarray(v) for k, v in inputs.items()}

    def pack(*parts):
        out = []
        for w in parts:
            rows, cols = w.shape
            tiles = -(-rows // 128)
            full = np.zeros((tiles * 128, cols), w.dtype)
            full[:rows] = w
            if rows == DC:
                full[rows:] = w[128:]
            out.append(full.reshape(tiles, 128, cols).transpose(1, 0, 2).reshape(128, tiles * cols))
        return np.concatenate(out, axis=1)

    w0 = pack(a["L0_xattn_Wq"].T, a["L0_xattn_Wlkv"].T, a["L0_xattn_Wkv"].T, a["L0_xattn_Wo"].T)
    w1 = np.stack([pack(*[a[f"L1_xattn_{n}"][:, 256 * g:256 * g + 256] for n in ("Wq", "Wk", "Wv")],
                        a["L1_xattn_Wo"][256 * g:256 * g + 256]) for g in range(4)])

    def experts(routed, shared):
        w = np.concatenate([routed.reshape(E * EI, D), shared])
        return np.concatenate([w, np.zeros((ET * 128 - len(w), D), w.dtype)]).T

    g_in, u_in = experts(a["L1_ffn_w1"], a["L1_ffn_ws1"]), experts(a["L1_ffn_w3"], a["L1_ffn_ws3"])
    y_out = experts(a["L1_ffn_w2"].transpose(0, 2, 1), a["L1_ffn_ws2"].T).T
    we = np.stack([pack(g_in[:, 128 * j:128 * j + 128], u_in[:, 128 * j:128 * j + 128], y_out[128 * j:128 * j + 128])
                   for j in range(ET)])
    k1 = np.stack([pack(a["L0_ffn_k1"][:, 128 * m:128 * m + 128]) for m in range(MT)])
    k2 = a["L0_ffn_k2"].reshape(MT, 128, D)

    def column(v):
        full = np.zeros(128, np.float32)
        full[:len(v)] = v
        return full

    def same(v):
        return np.broadcast_to(v, 128)

    cst = np.stack([column(a["L0_xattn_ln_x_g"][:128]), column(a["L0_xattn_ln_x_g"][128:]),
                    column(a["L0_xattn_ln_x_b"][:128]), column(a["L0_xattn_ln_x_b"][128:]),
                    a["L0_xattn_ln_l_g"][:128], a["L0_xattn_ln_l_g"][128:],
                    a["L0_xattn_ln_l_b"][:128], a["L0_xattn_ln_l_b"][128:],
                    np.tile(a["L0_xattn_qn_g"], 2), np.tile(a["L0_xattn_kn_g"], 2),
                    same(a["L0_ffn_s0"]), same(a["L0_ffn_s1"]), same(a["L0_ffn_s2"]),
                    same(a["g_xattn"][0]), same(a["g_xattn"][1]), same(a["g_ffn"][0]), same(a["g_ffn"][1])], axis=1)
    half_ones = np.zeros((128, 2), np.float32)
    half_ones[:DH, 0] = half_ones[DH:, 1] = 1 / DH
    arrays = {
        "x": a["x"], "ctx": a["ctx_768"], "ctxT": a["ctx_768"].reshape(NB * NCTX, DC).T,
        "mask": a["mask_BxS2_bk0"],
        "cst": cst, "bo": np.stack([a["L0_xattn_bo"], a["L1_xattn_bo"]]), "gbias": a["L1_ffn_gate_bias"],
        "w0": w0, "k0": a["L0_ffn_k0"], "k1": k1, "k2": k2,
        "w1": w1, "gw": pack(a["L1_ffn_gate_w"].T), "we": we, "eye": np.eye(128, dtype=np.float32),
        "ones": half_ones, "iota": np.arange(E, dtype=np.float32),
    }
    arrays = {f"{k}_in": np.ascontiguousarray(v) for k, v in arrays.items()}
    nc = bacc.Bacc("TRN2", target_bir_lowering=False, num_devices=1)
    args = [nc.dram_tensor(k, v.shape, mybir.dt.from_np(v.dtype), kind="ExternalInput").ap() for k, v in arrays.items()]
    out = nc.dram_tensor("out", (NB, S, D), F32, kind="ExternalOutput").ap()
    comb = nc.dram_tensor("comb", (2 * ET, NB * S), F32, kind="Internal").ap()
    build(nc, *args, out, comb)
    result = run_bass_kernel_spmd(nc, [arrays], core_ids=[0])
    return result.results[0]["out"]
```

```python
from contextlib import ExitStack

import concourse.bass as bass
from concourse import mybir
from concourse.alu_op_type import AluOpType as ALU

F32 = mybir.dt.float32
F32R = mybir.dt.float32r
U8 = mybir.dt.uint8
U32 = mybir.dt.uint32
ACT = mybir.ActivationFunctionType
AX = mybir.AxisListType

P = 128
NB, S, D = 2, 512, 256
KT = D // P
TT = S // P
NCTX, DC = 1024, 192
DC1 = DC - P
CT = NCTX // P
DH = 64
NK0 = NCTX + S
NK1 = NCTX
HG = 4
NG1 = 1024 // DH // HG
UNITS = 16
BLOCKS = UNITS // 2
FF = 1024
MT = FF // P
E, EI = 16, 192
ET = 26
LN_EPS = 1e-5
SCALE = DH ** -0.5
BIG = 3.0e38

PROJ_BANKS = [0, 1, 3, 4, 0, 1, 3, 4, 2, 5, 3, 4, 2, 5]
AHEAD_F3, AHEAD_Y, AHEAD_G = 2, 4, 4

FIRST_ORDER = [2, 3, 6, 7, 4, 5, 8, 9, 10, 11, 12, 13, 0, 1]
FIRST_BANKS = [0, 1, 2, 3, 0, 1, 2, 3, 0, 1, 2, 3, 2, 3]

SPARE_BANKS = (5, 7)

CTX_BANKS = [3, 4, 2, 5]

LN_BANKS = [(0, 1), (6, 7)]

W0 = {"q": 0, "lkv": 512, "kv": 1536, "wo": 2560}
W0_COLS = 3072
W1 = {"q": 0, "k": 512, "v": 1024, "wo": 1536}
W1_COLS = 2048
WE_COLS = 768
CHUNK = 1024

R_LN, R_W, R_XC = 0, 4096, 10240
R_AT = 2048
R_ATT0 = 14336
R_ATT1 = 18432
R_COLS = 40960

CONST = ["ln_x_g0", "ln_x_g1", "ln_x_b0", "ln_x_b1", "ln_l_g0", "ln_l_g1", "ln_l_b0", "ln_l_b1",
         "qn", "kn", "s0", "s1", "s2", "gx0", "gx1", "gf0", "gf1"]
NC_ = len(CONST)


def build(nc, x_d, ctx_d, ctxT_d, mask_d, cst_d, bo_d, gbias_d, w0_d, k0_d, k1_d, k2_d, w1_d, gw_d, we_d,
          eye_d, ones_d, iota_d, out_d, comb_d):
    with ExitStack() as stack:
        program(nc, stack, x_d, ctx_d, ctxT_d, mask_d, cst_d, bo_d, gbias_d, w0_d, k0_d, k1_d, k2_d, w1_d,
                gw_d, we_d, eye_d, ones_d, iota_d, out_d, comb_d)


def program(nc, stack, x_d, ctx_d, ctxT_d, mask_d, cst_d, bo_d, gbias_d, w0_d, k0_d, k1_d, k2_d, w1_d,
            gw_d, we_d, eye_d, ones_d, iota_d, out_d, comb_d):
    def sb(name, shape, dt=F32):
        return stack.enter_context(nc.sbuf_tensor(name, shape, dt))

    def sem(name):
        return stack.enter_context(nc.semaphore(name))

    R = sb("R", [P, R_COLS], F32R)
    x = sb("x", [P, NB * TT, D])
    eye = sb("eye", [P, P])
    cst = sb("cst", [P, 52])
    half_ones = sb("half_ones", [P, 2])
    tg = sb("tg", [P, 8])
    bo = sb("bo", [P, D])
    st6 = sb("st6", [P, 8, 6])
    mv = sb("mv", [P, 8, 2])
    rstd = sb("rstd", [P, 16])
    nmax = sb("nmax", [P, 8])
    sums = sb("sums", [P, 32])
    rr = sb("rr", [P, 128])
    FA = sb("FA", [P, 4096])
    FB = sb("FB", [P, 2816])
    wst = sb("wst", [P, 2048])
    xs = sb("xs", [P, 512])
    mvc = sb("mvc", [P, 8, 2])

    LNH0 = R[:, R_LN:R_LN + 1024].rearrange("p (k n) -> p k n", k=KT)
    LNL0 = R[:, R_LN + 1024:R_LN + 2048].rearrange("p (k n) -> p k n", k=KT)
    LNH = R[:, R_LN:R_LN + 2048].rearrange("p (k n) -> p k n", k=KT)
    LNL = R[:, R_LN + 2048:R_LN + 4096].rearrange("p (k n) -> p k n", k=KT)
    XC0 = [R[:, R_XC + 2048 * j:R_XC + 2048 * (j + 1)].rearrange("p (k n) -> p k n", k=2) for j in range(2)]
    XC1 = [R[:, R_XC + 4096 * j:R_XC + 4096 * (j + 1)].rearrange("p (k n) -> p k n", k=2) for j in range(2)]
    zero = R[:, 9728:9728 + P]
    pair1_keys = [FA[:, 2560:3072], FA[:, 3584:4096]]
    WH = R[:, R_W:R_W + W0_COLS]
    WL = R[:, R_W + W0_COLS:R_W + 2 * W0_COLS]
    xn = [FA[:, 1536 + D * t:1536 + D * (t + 1)] for t in range(TT)]
    late0 = [FA[:, 2048 + D * t:2048 + D * (t + 1)] for t in range(TT)]
    late1 = [FA[:, 2048:2304], FA[:, 2304:2560], FA[:, 3584:3840], FA[:, 3840:4096]]
    early = [wst[:, 1536:1792], wst[:, 1792:2048], xs[:, 0:256], xs[:, 256:512]]
    latent_aff = [[FA[:, 2560:3072], FA[:, 3072:3584]], [FA[:, 3584:4096], FA[:, 1024:1536]]]
    ctx_v = [buf[:, 0:CT * DC].rearrange("p (t n) -> p t n", t=CT) for buf in (FA, wst)]
    ctx_aff = [[FB[:, 1792 + 512 * kt:2304 + 512 * kt] for kt in range(2)],
               [FA[:, 1536 + 512 * kt:2048 + 512 * kt] for kt in range(2)]]

    PS = stack.enter_context(nc.psum_tensor("PS", [P, 8, 512], F32))

    class Attention:

        def __init__(self, layer):
            self.layer = layer
            nk = NK0 if layer == 0 else NK1
            self.nk, self.kt, self.ng, self.nb = nk, nk // P, nk // 512, nk // 512
            at = R_ATT0 if layer == 0 else R_ATT1

            def take(cols):
                nonlocal at
                at += cols
                return R[:, at - cols:at]

            self.q = take(HG * 512).rearrange("p (j n) -> p j n", j=HG)
            self.k = take(HG * nk).rearrange("p (j n) -> p j n", j=HG)
            self.q_lo = (take(1024) if layer == 1 else R[:, R_AT:R_AT + 1024]).rearrange("p (j n) -> p j n", j=2)
            self.v = take(self.kt * 512).rearrange("p (t h c) -> p t h c", h=HG, c=P)
            self.pt = [take(2 * self.kt * 256).rearrange("p (r t n) -> p r t n", r=2, t=self.kt) for _ in range(2)]
            if layer == 1:
                self.at = [[take(1024).rearrange("p (j n) -> p j n", j=2) for _ in range(2)]] * NB
            else:
                self.at = [[R[:, at_b + 1024 * j:at_b + 1024 * (j + 1)].rearrange("p (j n) -> p j n", j=2)
                            for j in range(2)] for at_b in (R_AT, R_XC)]
            self.probs = FA[:, 0:2 * nk].rearrange("p (r n) -> p r n", r=2)
            self.tmp = FA[:, 3072:3584].rearrange("p (r n) -> p r n", r=2)
            self.wo = (W0 if layer == 0 else W1)["wo"]
            self.score = [PS[:, 3 * r:3 * r + self.nb, :].rearrange("p b n -> p (b n)") for r in range(2)]

        def turn(self, u, g_):
            if g_ == 0:
                return PS[:, 6, :]
            return PS[:, 2, :] if self.layer == 1 else PS[:, 3 * (u % 2) + g_, :]

    L0, L1 = Attention(0), Attention(1)

    halves = [(slice(0, DH), slice(DH, P)), (slice(DH, P), slice(0, DH))]

    def key_block(i):
        return (i, slice(0, 512)) if i < 2 else ((i - 2) // 3, slice((i - 2) % 3 * 512, (i - 2) % 3 * 512 + 512))

    def key_low(eng, i, h):
        (rows, other), (p, cols) = halves[h], key_block(i)
        lo = L0.q_lo[rows, p, cols] if i < 2 else L0.k[other, 2 * p + h, cols]
        hi = (L0.q if i < 2 else L0.k)[rows, 2 * p + h, cols]
        return eng.tensor_tensor(lo, FA[rows, 512 * i:512 * i + 512], hi.bitcast(F32), ALU.subtract)

    maskbias = FB[:, 0:NCTX]
    mask8 = FB[:, NK0:NK0 + 256].bitcast(U8)
    at32 = FB[:, 1792:2816].rearrange("p (j n) -> p j n", j=2)

    h1 = [R[:, 18432 + 8192 * j:18432 + 8192 * (j + 1)].rearrange("p (k n) -> p k n", k=MT) for j in range(2)]
    fw0 = R[:, 34816:36864].rearrange("p (k n) -> p k n", k=KT)
    fw1 = R[:, 36864:38912].rearrange("p (r k n) -> p r k n", r=2, k=MT)
    fh2 = R[:, 38912:40960].rearrange("p (r j n) -> p r j n", r=2, j=2)
    fw2 = R[:, 9216:9728].rearrange("p (r n) -> p r n", r=2)
    hf = FA[:, 0:1024].rearrange("p (r n) -> p r n", r=2)
    k0b = FA[:, 2560:3584].bitcast(U8).rearrange("p (k n) -> p k n", k=4)
    k12b = FB[:, 2048:2688].bitcast(U8).rearrange("p (r n) -> p r n", r=2)

    ew = [[R[:, R_W + 1536 * r + 768 * j:R_W + 1536 * r + 768 * (j + 1)] for j in range(2)] for r in range(2)]
    eh = R[:, 18432:20480].rearrange("p (r j n) -> p r j n", r=2, j=2)
    gw = [R[:, 9856 + 32 * j:9888 + 32 * j].rearrange("p (k n) -> p k n", k=KT) for j in range(2)]
    est = wst[:, 0:1536].rearrange("p (r n) -> p r n", r=2)
    silu = FA[:, 0:1024].rearrange("p (r n) -> p r n", r=2)
    hcomb = FA[:, 1024:2048].rearrange("p (r n) -> p r n", r=2)
    hful = FA[:, 2560:3584].rearrange("p (r n) -> p r n", r=2)
    comb = FB[:, 0:2048].rearrange("p (r n) -> p r n", r=2)
    gst = wst[:, 1536:1568]
    RT = FB[:, 2048:2816]
    comb_rows = [xs[0:E, :], FA[0:E, 3584:4096]]

    names = (
        "x_in0 x_in1 ctx_in mask_in cst_in bo_in w0_in0 w0_in1 w1_in k0_in k1_in0 k1_in1 ctxT_in0 ctxT_in1 gw_in we_in0 we_in1 comb_in0 comb_in1 "
        "comb_out stores zeroed gates bo_gated bo_added w0_split maskbias_ready "
        "ln_var ln_std ln_xn ln_turned ln_aff ln_hi ln_lo cx_var cx_std cx_xn cx_turned cx_aff cx_hi cx_lo "
        "qk0_done qk0_raw qk0_sq qk0_ss qk0_norm qk0_rr qk0_spread qk0_rb qk0_scaled qk0_hi qk0_lo qk0_lo_pool v0_done v0_hi v0_lo "
        "scored_context scored maxed expd turned p_hi p_lo pv_done o_tmp o_sum rsum rspread rbc at_norm at_hi at_lo wo_done x_att "
        "q_twice k_lo cx_twice pj_done pj_hi pj_lo w1q_split w1o_split xc_lo "
        "fw0_ready fw1_ready f1_done f2_done f_act f_hi f_lo f3_done x_ffn "
        "ones_set gw_split gate_done gate_sig rt_comb rt_turned rt_copied e_split_in e_split_out g_done u_done e_comb e_silu e_full e_hi e_lo e_y "
        "out_ready dve_step pool_step pool_free").split()
    s = {n: sem(n) for n in names}

    def first(eng, name, value):
        if not isinstance(value, int) or value > 0:
            eng.wait_ge(s[name], value)

    class Steps:

        def __init__(self, eng, name):
            self.eng, self.sem, self.base, self.n = eng, s[name], 0, 0

        def __call__(self, ins):
            self.n += 1
            ins.then_inc(self.sem, 1)

        def wait(self):
            self.eng.wait_ge(self.sem, self.base + self.n)

    mm = nc.tensor.matmul
    eye_ap = eye[:, :]

    def three(pairs):
        out = []
        for (ah, al), (bh, bl) in pairs:
            out += [(ah, bh), (al, bh), (ah, bl)]
        return out

    def group(out, passes, skip=False):
        for n, (a, b) in enumerate(passes):
            last = mm(out, a, b, start=(n == 0), stop=(n == len(passes) - 1), skip_group_check=skip)
        return last

    def wcol(layer, name, kt, width, a, b):
        off = (W0 if layer == 0 else W1)[name] + kt * width
        return off + a, off + b

    def wpair(layer, name, kt, width, a, b, rows=P):
        lo, hi = wcol(layer, name, kt, width, a, b)
        return WH[0:rows, lo:hi], WL[0:rows, lo:hi]

    def context_passes(layer, name, width, a, b, xc, c, z, weights_first):
        w0, w1 = wpair(layer, name, 0, width, a, b), wpair(layer, name, 1, width, a, b)
        x0 = tuple(xc[j][:, 0, c:z] for j in range(2))
        pairs = [(w0[0], x0[0]), (w0[1], x0[0]), (w0[0], x0[1]),
                 (w1[0], xc[0][:, 1, c:z]), (w1[0][0:DC1], xc[1][0:DC1, 1, c:z])]
        return pairs if weights_first else [(x_, w) for w, x_ in pairs]


    block = stack.enter_context(nc.Block())

    @block.sync
    def _(sp):
        sp.sem_inc(s["f3_done"], AHEAD_F3)
        sp.sem_inc(s["e_y"], AHEAD_Y)
        sp.sem_inc(s["g_done"], AHEAD_G)
        sp.dma_start(x[:, 0:TT, :], x_d[0].rearrange("(t p) n -> p t n", p=P)).then_inc(s["x_in0"], 16)
        sp.dma_start(cst[:, 0:NC_], cst_d).then_inc(s["cst_in"], 16)
        sp.dma_start(eye[:, :], eye_d).then_inc(s["cst_in"], 16)
        sp.dma_start(cst[:, 20:36], gbias_d.partition_broadcast(P)).then_inc(s["cst_in"], 16)
        sp.dma_start(cst[:, 36:52], iota_d.partition_broadcast(P)).then_inc(s["cst_in"], 16)
        sp.dma_start(half_ones[:, :], ones_d).then_inc(s["cst_in"], 16)
        sp.dma_start(ctx_v[0], ctx_d[0].rearrange("(t p) n -> p t n", p=P)).then_inc(s["ctx_in"], 16)
        sp.dma_start(wst[:, 0:CHUNK], w0_d[:, 0:CHUNK]).then_inc(s["w0_in0"], 16)
        sp.dma_start(wst[:, CHUNK:2 * CHUNK], w0_d[:, CHUNK:2 * CHUNK]).then_inc(s["w0_in1"], 16)
        sp.dma_start(mask8, mask_d[0:1, :].partition_broadcast(P)).then_inc(s["mask_in"], 16)
        sp.dma_start(x[:, TT:2 * TT, :], x_d[1].rearrange("(t p) n -> p t n", p=P)).then_inc(s["x_in1"], 16)
        sp.dma_start(bo[:, :], bo_d[0:1, :].partition_broadcast(P)).then_inc(s["bo_in"], 16)
        sp.wait_ge(s["w0_split"], 1)
        sp.dma_start(wst[:, 0:CHUNK], w0_d[:, 2 * CHUNK:3 * CHUNK]).then_inc(s["w0_in0"], 16)
        sp.wait_ge(s["w0_split"], 3)
        sp.dma_start(ctx_v[1], ctx_d[1].rearrange("(t p) n -> p t n", p=P)).then_inc(s["ctx_in"], 16)
        sp.wait_ge(s["maskbias_ready"], 1)
        sp.dma_start(mask8, mask_d[1:2, :].partition_broadcast(P)).then_inc(s["mask_in"], 16)
        sp.wait_ge(s["bo_added"], NB)
        sp.dma_start(bo[:, :], bo_d[1:2, :].partition_broadcast(P)).then_inc(s["bo_in"], 16)
        sp.wait_ge(s["turned"], 2 * UNITS * L0.ng)
        sp.wait_ge(s["o_sum"], 2 * BLOCKS)
        sp.dma_start(k0b, k0_d.rearrange("(k p) n -> p k n", p=P)).then_inc(s["k0_in"], 16)
        sp.wait_ge(s["ln_turned"], NB + 1)
        sp.dma_start(wst[:, 0:W1_COLS], w1_d[0]).then_inc(s["w1_in"], 16)
        sp.wait_ge(s["x_att"], 4)
        sp.wait_ge(s["maxed"], 2 * UNITS)

        def context_load(c):
            kt, h = c // 2, c % 2
            for to in ((0,) if kt == 0 else (0, DC1)):
                rows = P if kt == 0 else DC1
                sp.dma_start(FB[to:to + rows, 1024 * h:1024 * h + 1024],
                             ctxT_d[kt * P:kt * P + rows, h * 1024:h * 1024 + 1024]).then_inc(s[f"ctxT_in{h}"], 16)

        def ffn_load(m):
            sp.dma_start(k12b[:, m % 2, 0:FF], k1_d[m]).then_inc(s[f"k1_in{m % 2}"], 16)
            sp.dma_start(k12b[:, m % 2, FF:FF + D], k2_d[m]).then_inc(s[f"k1_in{m % 2}"], 16)

        for c in range(2):
            context_load(c)
            ffn_load(c)
        for c in range(2):
            sp.wait_ge(s["xc_lo"], c + 1)
            context_load(c + 2)
        for m in range(2, MT):
            sp.wait_ge(s["fw1_ready"], m - 1)
            ffn_load(m)
        sp.wait_ge(s["w1o_split"], 1)
        sp.dma_start(wst[:, 0:W1_COLS], w1_d[1]).then_inc(s["w1_in"], 16)
        with sp.Fori(0, NG1 - 2) as g:
            sp.wait_ge(s["w1o_split"], g + 2)
            sp.dma_start(wst[:, 0:W1_COLS], w1_d[bass.ds(g + 2, 1)].rearrange("g p n -> (g p) n")).then_inc(s["w1_in"], 16)
        sp.wait_ge(s["w1o_split"], NG1)
        sp.dma_start(gst, gw_d).then_inc(s["gw_in"], 16)
        sp.dma_start(est[:, 0, :], we_d[0]).then_inc(s["we_in0"], 16)
        sp.dma_start(est[:, 1, :], we_d[1]).then_inc(s["we_in1"], 16)
        for r in range(2):
            sp.wait_ge(s["e_split_out"], r + 1)
            sp.dma_start(est[:, r, :], we_d[2 + r]).then_inc(s[f"we_in{r}"], 16)
        sp.wait_ge(s["rt_copied"], 2)
        routed = comb_d.rearrange("(e r) n -> e r n", r=3)
        for r in range(3):
            for w in range(2):
                sp.dma_start(routed[:, r, 512 * w:512 * w + 512], comb_rows[w]).then_inc(s["comb_out"], 16)
        sp.wait_ge(s["comb_out"], 96)

        def comb_load(row, r, name):
            for half in range(2):
                sp.dma_start(comb[64 * half:64 * half + 64, r, :],
                             comb_d[bass.ds(row + half, 1), :].partition_broadcast(64).rearrange("q o n -> q (o n)")
                             ).then_inc(s[name], 16)

        for r in range(2):
            sp.wait_ge(s["e_full"], 2 * r + 2)
            comb_load(2 * r, r, f"comb_in{r}")
        with sp.Fori(1, ET // 2 - 1) as i:
            for r in range(2):
                sp.wait_ge(s["e_split_out"], 2 * i + r + 1)
                sp.dma_start(est[:, r, :], we_d[bass.ds(2 * i + 2 + r, 1)].rearrange("g p n -> (g p) n")
                             ).then_inc(s[f"we_in{r}"], 16)
                sp.wait_ge(s["e_full"], 4 * i + 2 * r + 2)
                comb_load(4 * i + 2 * r, r, f"comb_in{r}")
        for t in range(NB * TT):
            sp.wait_ge(s["out_ready"], t + 1)
            sp.dma_start(out_d[t // TT, (t % TT) * P:(t % TT) * P + P, :], x[:, t, :]).then_inc(s["stores"], 16)
        sp.wait_ge(s["stores"], 16 * NB * TT)

    @block.gpsimd
    def _(pool):
        step = Steps(pool, "pool_step")
        g = nc.gpsimd

        def split(hi, lo, src):
            step(g.tensor_scalar(hi, src, 1.0, 0.0, ALU.mult, ALU.add))
            step.wait()
            return g.tensor_tensor(lo, src, hi.bitcast(F32), ALU.subtract)

        def pair1_low(C, count):
            for n in range(2):
                pool.wait_ge(s["pj_hi"], count + n)
                for h, (rows, other) in enumerate(halves):
                    cols = slice(512 * n, 512 * n + 512)
                    g.tensor_tensor(L1.k[other, 2 + h, cols], pair1_keys[n][rows, :], L1.k[rows, 2 + h, cols].bitcast(F32),
                                    ALU.subtract).then_inc(s["k_lo"], 1)
                    pool.wait_ge(s["k_lo"], 4 * (C - 2) + 2 * n + h + 1)

        def stack_low(c, n):
            return g.tensor_scalar(WH[DC1:P, c:c + n], WL[DC1:P, c:c + n].bitcast(F32), 1.0, 0.0, ALU.mult, ALU.add)

        def copy_queries(L, C, count):
            name = "qk0_hi" if L.layer == 0 else "pj_hi"
            pool.wait_ge(s[name], count)
            for slot in range(HG):
                rows, other = halves[slot % 2]
                pool.sem_inc(s["pool_free"], 1)
                g.tensor_scalar(L.q[other, slot, :], L.q[rows, slot, :].bitcast(F32), 1.0, 0.0, ALU.mult,
                                ALU.add).then_inc(s["q_twice"], 1)
                pool.wait_ge(s["q_twice"], HG * C + slot + 1)
            pool.sem_inc(s["pool_free"], 1)

        for c in range(W0_COLS // CHUNK):
            pool.wait_ge(s[f"w0_in{c % 2}"], 16 * (c // 2 + 1))
            src = wst[:, (c % 2) * CHUNK:(c % 2) * CHUNK + CHUNK]
            last = split(WH[:, c * CHUNK:(c + 1) * CHUNK], WL[:, c * CHUNK:(c + 1) * CHUNK], src)
            if c == W0["kv"] // CHUNK + 1:
                step(last)
                step.wait()
                last = stack_low(W0["kv"] + 512, 512)
            last.then_inc(s["w0_split"], 1)
            if c == W0["kv"] // CHUNK + 1:
                pool.wait_ge(s["w0_split"], c + 1)
        for b in range(NB):
            pool.wait_ge(s["ln_xn"], 2 * b + 1)
            pool.wait_ge(s["bo_gated"], 1)
            for t in range(TT):
                last = g.tensor_tensor(x[:, b * TT + t, :], x[:, b * TT + t, :], bo[:, :], ALU.add)
            last.then_inc(s["bo_added"], 1)
            pool.wait_ge(s["cx_hi"], 4 * b + 4)
            pool.wait_ge(s["bo_added"], b + 1)
            g.tensor_scalar(XC0[0][DC1:P, 1, :], XC0[0][0:DC1, 1, :].bitcast(F32), 1.0, 0.0, ALU.mult,
                            ALU.add).then_inc(s["cx_twice"], 1)
            pool.wait_ge(s["cx_twice"], b + 1)
            copy_queries(L0, b, 8 * b + 2)
            for i in range(8):
                pool.wait_ge(s["qk0_hi"], 8 * b + i + 1)
                key_low(g, i, 1).then_inc(s["qk0_lo_pool"], 1)
                pool.wait_ge(s["qk0_lo_pool"], 8 * b + i + 1)
        pool.wait_ge(s["at_lo"], 4)
        pool.wait_ge(s["wo_done"], 4)
        g.memset(zero.bitcast(F32), 0.0).then_inc(s["zeroed"], 1)
        for m in range(MT):
            pool.wait_ge(s[f"k1_in{m % 2}"], 32 * (m // 2 + 1))
            if m >= 2:
                pool.wait_ge(s["f3_done"], AHEAD_F3 + 2 * m - 2)
            step(g.tensor_scalar(fw1[:, m % 2].rearrange("p k n -> p (k n)"), k12b[:, m % 2, 0:FF], 2.0, -1.0, ALU.mult, ALU.add))
            step.wait()
            g.tensor_scalar(fw2[:, m % 2], k12b[:, m % 2, FF:FF + D], 2.0, -1.0, ALU.mult, ALU.add).then_inc(s["fw1_ready"], 1)
            if m == 1:
                for c in range(4):
                    kt, h = c // 2, c % 2
                    pool.wait_ge(s[f"ctxT_in{h}"], 16 if kt == 0 else 48)
                    cols = slice(1024 * h, 1024 * h + 1024)
                    split(XC1[0][:, kt, cols], XC1[1][:, kt, cols], FB[:, cols]).then_inc(s["xc_lo"], 1)
                pool.wait_ge(s["w1_in"], 16)
                n = W1["wo"]
                step(split(WH[:, 0:n], WL[:, 0:n], wst[:, 0:n]))
                step.wait()
                stack_low(W1["k"] + 256, 256)
                stack_low(W1["v"] + 256, 256).then_inc(s["w1q_split"], 1)
                pool.wait_ge(s["w1q_split"], 1)
                split(WH[:, n:W1_COLS], WL[:, n:W1_COLS], wst[:, n:W1_COLS]).then_inc(s["w1o_split"], 1)
        for b in range(NB):
            pool.wait_ge(s["ln_xn"], 2 * NB + NB + b + 1)
            pool.wait_ge(s["bo_gated"], 2)
            for t in range(TT):
                last = g.tensor_tensor(x[:, b * TT + t, :], x[:, b * TT + t, :], bo[:, :], ALU.add)
            last.then_inc(s["bo_added"], 1)

        pool.wait_ge(s["bo_added"], 2 * NB)
        copy_queries(L1, 2, 14)
        pair1_low(2, 5)
        with pool.Fori(1, NG1) as i:
            copy_queries(L1, 2 * i + 1, 28 * i - 14 + 2)
            pair1_low(2 * i + 1, 28 * i - 14 + 5)
            pool.wait_ge(s["w1_in"], 16 * i + 16)
            pool.wait_ge(s["pj_done"], 28 * i)
            n = W1["wo"]
            pool.sem_inc(s["pool_free"], 1)
            g.tensor_scalar(WH[:, 0:n], wst[:, 0:n], 1.0, 0.0, ALU.mult, ALU.add).then_inc(s["pool_step"], 1)
            pool.wait_ge(s["pool_step"], step.n + 3 * (i - 1) + 1)
            g.tensor_tensor(WL[:, 0:n], wst[:, 0:n], WH[:, 0:n].bitcast(F32), ALU.subtract).then_inc(s["pool_step"], 1)
            pool.wait_ge(s["pool_step"], step.n + 3 * (i - 1) + 2)
            pool.sem_inc(s["pool_free"], 1)
            stack_low(W1["k"] + 256, 256)
            stack_low(W1["v"] + 256, 256).then_inc(s["w1q_split"], 1)
            pool.wait_ge(s["w1q_split"], i + 1)
            copy_queries(L1, 2 * i + 2, 28 * i + 2)
            pair1_low(2 * i + 2, 28 * i + 5)
            pool.wait_ge(s["wo_done"], 4 + 4 * i)
            pool.sem_inc(s["pool_free"], 1)
            g.tensor_scalar(WH[:, n:W1_COLS], wst[:, n:W1_COLS], 1.0, 0.0, ALU.mult, ALU.add).then_inc(s["pool_step"], 1)
            pool.wait_ge(s["pool_step"], step.n + 3 * (i - 1) + 3)
            g.tensor_tensor(WL[:, n:W1_COLS], wst[:, n:W1_COLS], WH[:, n:W1_COLS].bitcast(F32),
                            ALU.subtract).then_inc(s["w1o_split"], 1)
            pool.wait_ge(s["w1o_split"], i + 1)
        step.n += 3 * (NG1 - 1)
        copy_queries(L1, 2 * NG1 + 1, 28 * NG1 - 14 + 2)
        pair1_low(2 * NG1 + 1, 28 * NG1 - 14 + 5)
        pool.wait_ge(s["gw_in"], 16)
        pool.wait_ge(s["pj_done"], 28 * NG1)
        split(gw[0].rearrange("p k n -> p (k n)"), gw[1].rearrange("p k n -> p (k n)"), gst).then_inc(s["gw_split"], 1)
        pool.wait_ge(s["at_lo"], 4 + 4 * NG1)
        g.memset(comb, 1.0).then_inc(s["ones_set"], 1)
        base = step.n
        with pool.Fori(0, ET // 2) as i:
            for r in range(2):
                pool.wait_ge(s[f"we_in{r}"], 16 * i + 16)
                if r == 1:
                    pool.wait_ge(s["wo_done"], 4 + 4 * NG1)
                pool.wait_ge(s["g_done"], AHEAD_G + 4 * i + 2 * r - 2)
                pool.sem_inc(s["pool_free"], 1)
                g.tensor_scalar(ew[r][0][:, 0:512], est[:, r, 0:512], 1.0, 0.0, ALU.mult, ALU.add).then_inc(s["pool_step"], 1)
                pool.wait_ge(s["pool_step"], base + 4 * i + 2 * r + 1)
                g.tensor_tensor(ew[r][1][:, 0:512], est[:, r, 0:512], ew[r][0][:, 0:512].bitcast(F32),
                                ALU.subtract).then_inc(s["e_split_in"], 1)
                pool.wait_ge(s["e_y"], AHEAD_Y + 4 * i + 2 * r - 2)
                pool.sem_inc(s["pool_free"], 1)
                g.tensor_scalar(ew[r][0][:, 512:768], est[:, r, 512:768], 1.0, 0.0, ALU.mult, ALU.add).then_inc(s["pool_step"], 1)
                pool.wait_ge(s["pool_step"], base + 4 * i + 2 * r + 2)
                g.tensor_tensor(ew[r][1][:, 512:768], est[:, r, 512:768], ew[r][0][:, 512:768].bitcast(F32),
                                ALU.subtract).then_inc(s["e_split_out"], 1)

    @block.tensor
    def _(pe):
        def ln_turn(n, banks, tokens=xn):
            pe.wait_ge(s["ln_xn"], n)
            for kt in range(KT):
                for t in range(TT):
                    last = nc.tensor.transpose(PS[:, banks[kt], t * P:t * P + P], tokens[t][:, kt * P:kt * P + P], eye_ap)
            last.then_inc(s["ln_turned"], 1)

        def scores(L, C, u, n):
            U0 = UNITS * C
            G0 = L.ng * UNITS * C if L.layer == 0 else 32 * C + 32
            p, h, qt = u // 8, (u // 2) % 2, ((u // 4) % 2) * 2 + u % 2
            rows = slice(DH * h, DH * h + DH)
            if n == 0:
                first(pe, "expd", U0 + u - 1)
            elif L.layer == 0 and u >= 2:
                pe.wait_ge(s["p_lo"], G0 + L.ng * (u - 2) + n + 1)
            tok, keys = slice(qt * P, qt * P + P), slice(n * 512, n * 512 + 512)
            last = group(L.score[u % 2][:, keys],
                         [(L.q[:, 2 * p + h, tok], L.k[:, 2 * p + h, keys]),
                          (L.q_lo[rows, p, tok], L.k[rows, 2 * p + h, keys])])
            if n == L.nb - 1:
                last.then_inc(s["scored"], 1)
            elif n == 1:
                last.then_inc(s["scored_context"], 1)

        def attention(L, b, C, filler=None):
            U0, K0 = UNITS * C, BLOCKS * C
            G0 = L.ng * UNITS * C if L.layer == 0 else 32 * C + 32

            def turn(u, g_):
                G = G0 + L.ng * u + g_
                if g_ == 0:
                    pe.wait_ge(s["expd"], U0 + u + 1)
                if L.layer == 1 or g_ == 0:
                    first(pe, "p_lo", G - L.ng + 1)
                out = L.turn(u, g_)
                for i in range(4):
                    c = (4 * g_ + i) * P
                    last = nc.tensor.transpose(out[:, i * P:i * P + P], L.probs[:, u % 2, c:c + P], eye_ap)
                last.then_inc(s["turned"], 1)

            def values(k, half):
                hd = 2 * (k // 4) + k % 2
                if half == 0:
                    pe.wait_ge(s["p_lo"], G0 + L.ng * (2 * k + 2))
                    first(pe, "o_sum", K0 + k)
                n = L.kt // 2
                for kt in range(half * n, half * n + n):
                    for j in range(2):
                        last = mm(PS[:, 7, 0:256], L.v[:, kt, hd, :], L.pt[j][:, k % 2, kt, :],
                                  start=(kt == 0 and j == 0), stop=(kt == L.kt - 1 and j == 1))
                if half == 1:
                    last.then_inc(s["pv_done"], 1)

            if L.layer == 0:
                pe.wait_ge(s["q_twice"], HG * C + HG)
                pe.wait_ge(s["qk0_lo"], 8 * b + 5)
                pe.wait_ge(s["qk0_lo_pool"], 8 * b + 5)
                pe.wait_ge(s["qk0_scaled"], 8 * b + 8)
                for u in (0, 1):
                    if u == 1:
                        pe.wait_ge(s["v0_lo"], 12 * b + 12)
                    for n in range(L.nb):
                        scores(L, C, u, n)
            first(pe, "x_att", 2 * C - 1)
            for u in range(UNITS + 2):
                if u < UNITS:
                    for g_ in range(L.ng):
                        turn(u, g_)
                if L.layer == 0 and u + 2 == UNITS // 2:
                    pe.wait_ge(s["qk0_lo"], 8 * b + 8)
                    pe.wait_ge(s["qk0_lo_pool"], 8 * b + 8)
                if L.layer == 1 and u + 2 == UNITS // 2:
                    pe.wait_ge(s["k_lo"], 4 * (C - 1))
                if u + 2 < UNITS:
                    scores(L, C, u + 2, 0)
                    if L.layer == 1:
                        scores(L, C, u + 2, 1)
                elif filler:
                    filler(u)
                if u == 2:
                    first(pe, "x_att", 2 * C)
                    if L.layer == 1:
                        pe.wait_ge(s["ln_lo"], 4 * NB + 4)
                if u >= 2:
                    values(u // 2 - 1, u % 2)
                if u + 2 < UNITS and L.layer == 0:
                    scores(L, C, u + 2, 1)
                    scores(L, C, u + 2, 2)

        def out_rows(C):
            pe.wait_ge(s["rspread"], 2 * C + 2)
            for p in range(2):
                for qt in range(TT):
                    c = 512 * p + P * qt
                    last = mm(PS[:, 2 + 3 * p, qt * P:qt * P + P], FA[:, c:c + P], eye_ap, start=True, stop=True)
                last.then_inc(s["rbc"], 1)

        def out_project(L, b, C):
            pe.wait_ge(s["at_lo"], 2 * C + 2)
            for w in range(2):
                for e in range(2):
                    tt = 2 * w + e
                    pairs = [(tuple(L.at[b][j][:, p, tt * P:tt * P + P] for j in range(2)),
                              (WH[:, L.wo + p * D:L.wo + p * D + D], WL[:, L.wo + p * D:L.wo + p * D + D]))
                             for p in range(2)]
                    last = group(PS[:, 6 + w, e * D:e * D + D], three(pairs))
                last.then_inc(s["wo_done"], 1)

        pe.wait_ge(s["cst_in"], 80)

        def context_turn(b, gg):
            pe.wait_ge(s["cx_xn"], b + 1)
            for kt in range(2):
                rows = P if kt == 0 else DC1
                for t in range(4):
                    last = nc.tensor.transpose(PS[0:rows, CTX_BANKS[2 * gg + kt], t * P:t * P + P],
                                               ctx_v[b][:, 4 * gg + t, kt * P:kt * P + rows], eye_ap)
                last.then_inc(s["cx_turned"], 1)

        ln_turn(2, LN_BANKS[0])
        context_turn(0, 0)
        context_turn(0, 1)
        for b in range(NB):
            pe.wait_ge(s["ln_lo"], 2 * b + 2)
            pe.wait_ge(s["cx_lo"], 4 * b + 4)
            pe.wait_ge(s["cx_twice"], b + 1)
            pe.wait_ge(s["w0_split"], 3)

            def square_sums(i):
                pe.wait_ge(s["qk0_sq"], 8 * b + i + 1)
                for tt in range(TT):
                    last = mm(PS[:, 4, i * 8 + tt * 2:i * 8 + tt * 2 + 2],
                              FB[:, 1792 + 512 * (i % 2) + tt * P:1792 + 512 * (i % 2) + tt * P + P],
                              half_ones[:, :], start=True, stop=True)
                last.then_inc(s["qk0_ss"], 1)

            lat = [(LNH0[:, kt, :], LNL0[:, kt, :]) for kt in range(KT)]
            for i in range(8):
                if i >= 4:
                    pe.wait_ge(s["qk0_sq"], 8 * b + i - 3)
                if i < 2:
                    passes = three([(wpair(0, "q", kt, 256, i * P, i * P + P), lat[kt]) for kt in range(KT)])
                else:
                    p, n = (i - 2) // 3, (i - 2) % 3
                    if n < 2:
                        passes = context_passes(0, "kv", 512, p * P, p * P + P, XC0, n * 512, n * 512 + 512, True)
                    else:
                        passes = three([(wpair(0, "lkv", kt, 512, p * P, p * P + P), lat[kt]) for kt in range(KT)])
                group(PS[:, i % 4, :], passes).then_inc(s["qk0_done"], 1)
                if i >= 1:
                    square_sums(i - 1)
            square_sums(7)

            def value_tile(t):
                if t >= 3:
                    pe.wait_ge(s["v0_lo"], 12 * b + t - 2)
                if t < CT:
                    passes = context_passes(0, "kv", 512, 256, 512, XC0, t * P, t * P + P, False)
                else:
                    c = (t - CT) * P
                    passes = three([((LNH0[:, kt, c:c + P], LNL0[:, kt, c:c + P]), wpair(0, "lkv", kt, 512, 256, 512))
                                    for kt in range(KT)])
                group(PS[:, 5 + t % 3, 0:256], passes).then_inc(s["v0_done"], 1)

            for t in range(3):
                value_tile(t)
            for i in range(8):
                if i >= 4:
                    pe.wait_ge(s["qk0_scaled"], 8 * b + i - 3)
                pe.wait_ge(s["qk0_spread"], 8 * b + i + 1)
                for tt in range(TT):
                    c = 1792 + 512 * (i % 2) + tt * P
                    last = mm(PS[:, i % 4, tt * P:tt * P + P], FB[:, c:c + P], eye_ap, start=True, stop=True)
                last.then_inc(s["qk0_rb"], 1)
                value_tile(3 + i)
            value_tile(11)

            def next_norm(u):
                if u == UNITS:
                    pe.wait_ge(s["p_lo"], L0.ng * (UNITS * b + UNITS - 1))
                    ln_turn(2 * NB + b, LN_BANKS[0], early)

            attention(L0, b, b, next_norm)
            pe.wait_ge(s["p_lo"], L0.ng * UNITS * (b + 1))
            if b == 0:
                context_turn(1, 0)
            out_rows(b)
            if b == 0:
                pe.wait_ge(s["at_norm"], 2)
                context_turn(1, 1)
            out_project(L0, b, b)

        pe.wait_ge(s["fw0_ready"], KT)
        for j in range(2 * MT):
            h, m = j // MT, j % MT
            if j == 4:
                pe.wait_ge(s["x_att"], 4)
                ln_turn(2 * NB + 2, LN_BANKS[1])
            if m == 0:
                pe.wait_ge(s["ln_lo"], 2 * NB + 2 * (h + 1))
            if j >= 4:
                pe.wait_ge(s["f_act"], j - 3)
            passes = [(fw0[:, kt, m * P:m * P + P], X[:, kt, h * 512:h * 512 + 512])
                      for kt in range(KT) for X in (LNH, LNL)]
            group(PS[:, j % 4, :], passes).then_inc(s["f1_done"], 1)
        pe.wait_ge(s["zeroed"], 1)
        for w in range(4):
            last = mm(PS[:, 4 + w, :], zero, LNH[:, 0, 0:512], start=True, stop=False, skip_group_check=True)
        pe.wait_ge(s["f_lo"], 2 * MT)

        def ffn2(j, m, r, h):
            if h == 0:
                pe.wait_ge(s["fw1_ready"], m + 1)
            pe.wait_ge(s["f_act"], 2 * MT + j - 3)
            passes = [(fw1[:, r, kt, :], X[:, kt, h * 512:h * 512 + 512]) for kt in range(MT) for X in h1]
            group(PS[:, (2 * r + h) % 4, :], passes).then_inc(s["f2_done"], 1)

        def ffn3(j, r, h):
            pe.wait_ge(s["f_lo"], 2 * MT + j + 1)
            for tt in range(TT):
                T = TT * h + tt
                for part in range(2):
                    last = mm(PS[:, 4 + T // 2, (T % 2) * D:(T % 2) * D + D], fh2[:, h, part, tt * P:tt * P + P],
                              fw2[:, r, :], start=False, stop=False, skip_group_check=True)
            last.then_inc(s["f3_done"], 1)

        ffn2(0, 0, 0, 0)
        with pe.Fori(0, MT // 2 - 1) as i:
            for c in range(4):
                ffn2(4 * i + c + 1, 2 * i + (c + 1) // 2, ((c + 1) // 2) % 2, (c + 1) % 2)
                ffn3(4 * i + c, c // 2, c % 2)
        base = 2 * MT - 4
        for c in range(4):
            if c < 3:
                ffn2(base + c + 1, MT - 2 + (c + 1) // 2, (c + 1) // 2, (c + 1) % 2)
            ffn3(base + c, c // 2, c % 2)

        def project(b, J0, jobs, order=range(14), banks=PROJ_BANKS):
            for n in jobs:
                j = order[n]
                if n >= 4:
                    pe.wait_ge(s["pj_lo"], J0 + n - 3)
                out = PS[:, banks[n], :]
                if j < 2:
                    passes = three([(wpair(1, "q", kt, 256, j * P, j * P + P),
                                     (LNH[:, kt, b * S:b * S + S], LNL[:, kt, b * S:b * S + S])) for kt in range(KT)])
                elif j < 6:
                    p, c = (j - 2) // 2, NCTX * b + (j - 2) % 2 * 512
                    passes = context_passes(1, "k", 256, p * P, p * P + P, XC1, c, c + 512, True)
                else:
                    c = NCTX * b + (j - 6) * P
                    passes = context_passes(1, "v", 256, 0, 256, XC1, c, c + P, False)
                    out = out[:, 0:256]
                group(out, passes).then_inc(s["pj_done"], 1)

        def router(b):
            pe.wait_ge(s["ln_lo"], 6 * NB + 2 * (b + 1))
            for t in range(TT * b, TT * b + TT):
                c = t * P
                passes = three([((LNH[:, kt, c:c + P], LNL[:, kt, c:c + P]), (gw[0][:, kt, :], gw[1][:, kt, :]))
                                for kt in range(KT)])
                last = group(PS[:, 3, t * E:t * E + E], passes)
            last.then_inc(s["gate_done"], 1)

        def heads(g_, more):
            for b in range(NB):
                C = 2 * g_ + b + 2
                nxt = b == 0 or more
                J1 = 28 * g_ + 14 * (b + 1)

                def next_projections(u):
                    if u < UNITS - 1 or u > UNITS:
                        return
                    if u == UNITS - 1 and b == 1:
                        pe.wait_ge(s["w1q_split"], g_ + 2)
                    pe.wait_ge(s["expd"], UNITS * C + u)
                    project(1 - b, J1, range(2) if u == UNITS - 1 else range(2, 4))

                attention(L1, b, C, next_projections if nxt else None)
                if nxt:
                    project(1 - b, J1, range(4, 6))
                else:
                    pe.wait_ge(s["expd"], UNITS * C + UNITS)
                    ln_turn(4 * NB + 1, LN_BANKS[0], late0)
                out_rows(C)
                if nxt:
                    project(1 - b, J1, range(6, 8))
                    first_scores(C + 1, J1, 0)
                    pe.wait_ge(s["at_norm"], 2 * C + 2)
                    project(1 - b, J1, range(8, 14))
                else:
                    pe.wait_ge(s["gw_split"], 1)
                    router(0)
                if b == 0:
                    pe.wait_ge(s["w1o_split"], g_ + 1)
                out_project(L1, b, C)
                if nxt:
                    first_scores(C + 1, J1, 1)

        def first_scores(C, J1, u):
            if u == 0:
                pe.wait_ge(s["q_twice"], HG * C + HG)
            pe.wait_ge(s["pj_lo"], J1 + (14 if u else 6))
            for n in range(L1.nb):
                scores(L1, C, u, n)

        pe.wait_ge(s["w1q_split"], 1)
        pe.wait_ge(s["xc_lo"], 4)
        pe.wait_ge(s["f_act"], 4 * MT)
        project(0, 0, range(12), FIRST_ORDER, FIRST_BANKS)
        pe.wait_ge(s["pj_lo"], 10)
        ln_turn(3 * NB + 1, LN_BANKS[0])
        pe.wait_ge(s["ln_lo"], 4 * NB + 2)
        project(0, 0, range(12, 14), FIRST_ORDER, FIRST_BANKS)
        pe.wait_ge(s["x_ffn"], NB)
        pe.wait_ge(s["pj_lo"], 14)
        first_scores(NB, 0, 0)
        first_scores(NB, 0, 1)
        ln_turn(3 * NB + 2, SPARE_BANKS)
        with pe.Fori(0, NG1 - 1) as g_:
            heads(g_, True)
        heads(NG1 - 1, False)

        def zero_banks(w):
            return mm(PS[:, w, :], zero, LNH[:, 0, 0:512], start=True, stop=False, skip_group_check=True)

        def gate_up(j, tile, r, h):
            if h == 0:
                pe.wait_ge(s["e_split_in"], tile + 1)
            first(pe, "e_full", j - 1)
            for part in (1, 0):
                c = part * 256
                pairs = [((ew[r][0][:, c + kt * P:c + kt * P + P], ew[r][1][:, c + kt * P:c + kt * P + P]),
                          (LNH[:, kt, h * 512:h * 512 + 512], LNL[:, kt, h * 512:h * 512 + 512]))
                         for kt in range(KT)]
                group(PS[:, 2 * h + part, :], three(pairs)).then_inc(s["g_done" if part == 0 else "u_done"], 1)

        def down(j, tile, r, h):
            if h == 0:
                pe.wait_ge(s["e_split_out"], tile + 1)
            pe.wait_ge(s["e_lo"], j + 1)
            for tt in range(TT):
                T = TT * h + tt
                for a, w in three([((eh[:, h, 0, tt * P:tt * P + P], eh[:, h, 1, tt * P:tt * P + P]),
                                    (ew[r][0][:, 512:768], ew[r][1][:, 512:768]))]):
                    last = mm(PS[:, 4 + T // 2, (T % 2) * D:(T % 2) * D + D], a, w,
                              start=False, stop=False, skip_group_check=True)
            last.then_inc(s["e_y"], 1)

        zero_banks(4)
        zero_banks(5)
        gate_up(0, 0, 0, 0)
        pe.wait_ge(s["x_att"], 4 + 4 * NG1)
        ln_turn(4 * NB + 2, LN_BANKS[1], late1)
        down(0, 0, 0, 0)
        router(1)
        zero_banks(6)
        zero_banks(7)
        pe.wait_ge(s["gate_sig"], 1)
        gate_up(1, 0, 0, 1)
        gate_up(2, 1, 1, 0)
        down(1, 0, 0, 1)
        gate_up(3, 1, 1, 1)
        down(2, 1, 1, 0)
        pe.wait_ge(s["e_full"], 3)
        pe.wait_ge(s["rt_comb"], 1)
        for t in range(NB * TT):
            last = nc.tensor.transpose(PS[0:E, t // TT, (t % TT) * P:(t % TT) * P + P], wst[:, 1600 + t * E:1600 + t * E + E],
                                       eye_ap)
        last.then_inc(s["rt_turned"], 1)
        down(3, 1, 1, 1)
        pe.wait_ge(s["rt_copied"], 2)
        gate_up(4, 2, 0, 0)
        gate_up(5, 2, 0, 1)
        with pe.Fori(1, ET // 2 - 1) as i:
            for c in range(4):
                gate_up(4 * i + c + 2, 2 * i + c // 2 + 1, (c // 2 + 1) % 2, c % 2)
                down(4 * i + c, 2 * i + c // 2, c // 2, c % 2)
        base = 2 * ET - 4
        for c in range(4):
            if c < 2:
                gate_up(base + c + 2, ET - 1, 1, c)
            down(base + c, ET - 2 + c // 2, c // 2, c % 2)

    @block.scalar
    def _(act):
        a_ = nc.scalar.activation
        col = {n: cst[:, i:i + 1] for i, n in enumerate(CONST)}

        def ln_root(n, cols=TT):
            act.wait_ge(s["ln_var"], n)
            a_(rstd[:, 8:8 + cols], rstd[:, 0:cols], ACT.Sqrt).then_inc(s["ln_std"], 1)

        def ln_split(n, b, dst, banks=None):
            act.wait_ge(s["ln_turned"], n)
            for kt in range(KT):
                a_(dst[:, kt, b * S:b * S + S], PS[:, (banks or LN_BANKS[b])[kt], :], ACT.Copy).then_inc(s["ln_hi"], 1)

        def exp(L, C, u):
            U0 = UNITS * C
            G0 = L.ng * UNITS * C if L.layer == 0 else 32 * C + 32
            if u == 0:
                first(act, "rsum", C)
                first(act, "rbc", 2 * C)
            act.wait_ge(s["maxed"], U0 + u + 1)
            first(act, "turned", G0 + L.ng * (u - 1))
            a_(L.probs[:, u % 2, :], L.score[u % 2], ACT.Exp, bias=nmax[:, u % 2:u % 2 + 1], scale=1.0,
               accum_out=sums[:, u:u + 1]).then_inc(s["expd"], 1)

        def attention(L, b, C, filler=None):
            U0, K0 = UNITS * C, BLOCKS * C
            G0 = L.ng * UNITS * C if L.layer == 0 else 32 * C + 32

            def out_copy(k):
                h = k % 2
                act.wait_ge(s["pv_done"], K0 + k + 1)
                first(act, "o_sum", K0 + k - 1)
                a_(L.tmp[DH * h:DH * h + DH, k % 2, :], PS[0:DH, 7, 0:256], ACT.Copy).then_inc(s["o_tmp"], 1)

            if L.layer == 0:
                exp(L, C, 0)
            for u in range(UNITS + 3):
                if u >= 4 and u % 2 == 0:
                    out_copy(u // 2 - 2)
                if u < UNITS:
                    for g_ in range(L.ng):
                        G = G0 + L.ng * u + g_
                        act.wait_ge(s["turned"], G + 1)
                        if g_ == 0:
                            first(act, "pv_done", K0 + u // 2 - 1)
                        a_(L.pt[0][:, (u // 2) % 2, 4 * g_:4 * g_ + 4, (u % 2) * P:(u % 2) * P + P],
                           L.turn(u, g_).rearrange("p (t n) -> p t n", t=4), ACT.Copy).then_inc(s["p_hi"], 1)
                if u + 1 < UNITS:
                    exp(L, C, u + 1)
                if filler:
                    filler(u)

        def out_hi(L, b, C):
            for p in range(2):
                act.wait_ge(s["at_norm"], 2 * C + p + 1)
                a_(L.at[b][0][:, p, :], at32[:, p, :], ACT.Copy).then_inc(s["at_hi"], 1)

        act.wait_ge(s["cst_in"], 80)
        a_(tg[:, 0:4], cst[:, CONST.index("gx0"):CONST.index("gx0") + 4], ACT.Tanh).then_inc(s["gates"], 1)

        def context_root(b):
            act.wait_ge(s["cx_var"], b + 1)
            a_(rr[:, CT:2 * CT], rr[:, 0:CT], ACT.Sqrt).then_inc(s["cx_std"], 1)

        def latents(b):
            act.wait_ge(s["ln_turned"], b + 1)
            for kt in range(KT):
                gain = dict(bias=col[f"ln_l_b{kt}"], scale=col[f"ln_l_g{kt}"])
                a_(latent_aff[b][kt], PS[:, kt, :], ACT.Identity, **gain).then_inc(s["ln_aff"], 1)
                a_(LNH0[:, kt, :], PS[:, kt, :], ACT.Identity, **gain).then_inc(s["ln_hi"], 1)

        def context(b, i):
            gg, kt = i // 2, i % 2
            rows = P if kt == 0 else DC1
            act.wait_ge(s["cx_turned"], 4 * b + i + 1)
            first(act, "cx_lo", 4 * b + i - 1)
            src = PS[0:rows, CTX_BANKS[i], :]
            gain = dict(bias=col[f"ln_x_b{kt}"][0:rows], scale=col[f"ln_x_g{kt}"][0:rows])
            a_(ctx_aff[b][kt][0:rows, :], src, ACT.Identity, **gain).then_inc(s["cx_aff"], 1)
            a_(XC0[0][0:rows, kt, gg * 512:gg * 512 + 512], src, ACT.Identity, **gain).then_inc(s["cx_hi"], 1)

        ln_root(1)
        context_root(0)
        ln_root(2)
        latents(0)
        for i in range(4):
            context(0, i)
        for b in range(NB):
            for i in range(8):
                act.wait_ge(s["qk0_done"], 8 * b + i + 1)
                a_(FA[:, 512 * i:512 * i + 512], PS[:, i % 4, :], ACT.Copy).then_inc(s["qk0_raw"], 1)
                first(act, "qk0_ss", 8 * b + i - 1)
                a_(FB[:, 1792 + 512 * (i % 2):2304 + 512 * (i % 2)], PS[:, i % 4, :], ACT.Square).then_inc(s["qk0_sq"], 1)
                if i == 1 and b == 0:
                    ln_root(3)
                    context_root(1)
                elif i == 5 and b == 0:
                    ln_root(4)
                elif i == 1:
                    ln_root(2 * NB + 1)
            act.wait_ge(s["qk0_ss"], 8 * b + 8)
            a_(rr[:, 64:128], PS[:, 4, 0:64], ACT.Sqrt).then_inc(s["qk0_norm"], 1)

            def value_hi(t):
                act.wait_ge(s["v0_done"], 12 * b + t + 1)
                a_(L0.v[:, t, :, 0:DH], PS[:, 5 + t % 3, 0:256].rearrange("p (h c) -> p h c", h=HG),
                   ACT.Copy).then_inc(s["v0_hi"], 1)

            for t in range(3):
                value_hi(t)
            for i in range(8):
                value_hi(3 + i)
                act.wait_ge(s["qk0_scaled"], 8 * b + i + 1)
                p, cols = key_block(i)
                for h, (rows, other) in enumerate(halves):
                    last = a_((L0.q if i < 2 else L0.k)[rows, 2 * p + h, cols], FA[rows, 512 * i:512 * i + 512], ACT.Copy)
                last.then_inc(s["qk0_hi"], 1)
            value_hi(11)
            act.wait_ge(s["qk0_lo"], 8 * b + 8)
            act.wait_ge(s["qk0_lo_pool"], 8 * b + 8)

            def next_norm(u):
                if u == UNITS + 1:
                    if b == 0:
                        latents(1)
                    else:
                        ln_split(NB + 1, 0, LNH)

            attention(L0, b, b, next_norm)
            out_hi(L0, b, b)
            if b == 0:
                for i in range(4):
                    context(1, i)

        for j in range(2 * MT):
            if j == 2:
                ln_root(2 * NB + 2)
            elif j == 6:
                ln_split(NB + 2, 1, LNH)
            act.wait_ge(s["f1_done"], j + 1)
            if j >= 2:
                act.wait_ge(s["f_lo"], j - 1)
            a_(hf[:, j % 2, :], PS[:, j % 4, :], ACT.Relu, scale=tg[:, 4:5]).then_inc(s["f_act"], 1)
        with act.Fori(0, MT // 2) as i:
            for c in range(4):
                act.wait_ge(s["f2_done"], 4 * i + c + 1)
                act.wait_ge(s["f_lo"], 2 * MT + 4 * i + c - 1)
                a_(hf[:, c % 2, :], PS[:, c, :], ACT.Relu, scale=tg[:, 5:6]).then_inc(s["f_act"], 1)

        def project_hi(C, J0, jobs, order=range(14), banks=PROJ_BANKS):
            for n in jobs:
                j = order[n]
                act.wait_ge(s["pj_done"], J0 + n + 1)
                src = PS[:, banks[n], :]
                if j < 6:
                    for h, (rows, other) in enumerate(halves):
                        if j < 2:
                            ins = a_(L1.q[rows, 2 * j + h, :], src[rows, :], ACT.Copy, scale=SCALE)
                        else:
                            p, c = (j - 2) // 2, (j - 2) % 2 * 512
                            ins = a_(L1.k[rows, 2 * p + h, c:c + 512], src[rows, :], ACT.Copy)
                else:
                    ins = a_(L1.v[:, j - 6, :, 0:DH], src[:, 0:256].rearrange("p (h c) -> p h c", h=HG), ACT.Copy)
                if j in (4, 5):
                    first(act, "k_lo", 4 * (C - 2))
                    ins = a_(pair1_keys[j - 4], src, ACT.Copy)
                ins.then_inc(s["pj_hi"], 1)

        def heads(g_, more):
            for b in range(NB):
                C = 2 * g_ + b + 2
                nxt = b == 0 or more
                J1 = 28 * g_ + 14 * (b + 1)

                def next_projections(u):
                    project_hi(C + 1, J1, {UNITS: range(2), UNITS + 1: range(2, 4)}.get(u, ()))

                def next_norm(u):
                    if u == 2:
                        ln_root(4 * NB + 1)

                attention(L1, b, C, next_projections if nxt else next_norm)
                if nxt:
                    project_hi(C + 1, J1, range(4, 10))
                    exp(L1, C + 1, 0)
                else:
                    ln_split(3 * NB + 1, 0, LNH)
                out_hi(L1, b, C)
                if nxt:
                    project_hi(C + 1, J1, range(10, 14))

        project_hi(NB, 0, range(1), FIRST_ORDER, FIRST_BANKS)
        ln_root(3 * NB + 1)
        project_hi(NB, 0, range(1, 12), FIRST_ORDER, FIRST_BANKS)
        ln_split(2 * NB + 1, 0, LNH)
        project_hi(NB, 0, range(12, 14), FIRST_ORDER, FIRST_BANKS)
        ln_root(3 * NB + 2)
        exp(L1, NB, 0)
        ln_split(2 * NB + 2, 1, LNH, SPARE_BANKS)
        with act.Fori(0, NG1 - 1) as g_:
            heads(g_, True)
        heads(NG1 - 1, False)
        def job(j, c):
            act.wait_ge(s["g_done"], AHEAD_G + j + 1)
            a_(silu[:, c % 2, :], PS[:, 2 * (c % 2), :], ACT.Silu).then_inc(s["e_silu"], 1)
            act.wait_ge(s["e_full"], j + 1)
            act.wait_ge(s["e_y"], AHEAD_Y + j - 1)
            a_(eh[:, c % 2, 0, :], hful[:, c % 2, :], ACT.Copy).then_inc(s["e_hi"], 1)

        ln_root(4 * NB + 2)
        job(0, 0)
        ln_split(3 * NB + 2, 1, LNH)
        act.wait_ge(s["gate_done"], 2)
        a_(wst[:, 1728:1856], PS[:, 3, 0:P], ACT.Sigmoid).then_inc(s["gate_sig"], 1)
        for c in range(1, 4):
            job(c, c)
        with act.Fori(1, ET // 2) as i:
            for c in range(4):
                job(4 * i + c, c)

    @block.vector
    def _(dve):
        step = Steps(dve, "dve_step")
        v = nc.vector

        def inc(ins, name):
            ins.then_inc(s[name], 1)

        def statistics(src, tiles, means, var, inv):
            for t in range(tiles):
                last = v.bn_stats(st6[:, t, :], src(t))
            step(last)
            step.wait()
            for t in range(tiles):
                last = v.bn_aggr(means[:, t, :], st6[:, t, :])
            step(last)
            step.wait()
            step(v.tensor_scalar(var, means[:, 0:tiles, 1], LN_EPS, None, ALU.add))
            step.wait()
            return v.reciprocal(inv, var)

        def norm_statistics(src):
            inc(statistics(src, TT, mv, rstd[:, 4:8], rstd[:, 0:TT]), "ln_var")

        def norm_apply(n, src, dst=xn):
            dve.wait_ge(s["ln_std"], n)
            for t in range(TT):
                last = v.tensor_scalar(dst[t], src(t), mv[:, t, 0:1], rstd[:, 8 + t:9 + t], ALU.subtract, ALU.mult)
            inc(last, "ln_xn")

        def norm(n, src, dst=xn):
            norm_statistics(src)
            norm_apply(n, src, dst)

        def context_statistics(b):
            dve.wait_ge(s["ctx_in"], 16 * (b + 1))
            inc(statistics(lambda t: ctx_v[b][:, t, :], CT, mvc, rr[:, 2 * CT:3 * CT], rr[:, 0:CT]), "cx_var")

        def context_apply(b):
            dve.wait_ge(s["cx_std"], b + 1)
            for t in range(CT):
                last = v.tensor_scalar(ctx_v[b][:, t, :], ctx_v[b][:, t, :], mvc[:, t, 0:1], rr[:, CT + t:CT + t + 1],
                                       ALU.subtract, ALU.mult)
            inc(last, "cx_xn")

        def x_tiles(b):
            return lambda t: x[:, b * TT + t, :]

        def split_norm(n, b, banks=None):
            for kt in range(KT):
                dve.wait_ge(s["ln_hi"], 2 * (n - 1) + kt + 1)
                cols = slice(b * S, b * S + S)
                inc(v.tensor_tensor(LNL[:, kt, cols], PS[:, (banks or LN_BANKS[b])[kt], :], LNH[:, kt, cols].bitcast(F32), ALU.subtract), "ln_lo")

        def maximum(L, C, u):
            U0 = UNITS * C
            r = u % 2
            if L.layer == 0:
                dve.wait_ge(s["scored_context"], U0 + u + 1)
                first(dve, "expd", U0 + u - 1)
                step(v.tensor_tensor_reduce(L.score[r][:, 0:NCTX], L.score[r][:, 0:NCTX], maskbias, 1.0, -BIG, ALU.add,
                                            ALU.max, accum_out=nmax[:, 2 + r:3 + r]))
                dve.wait_ge(s["scored"], U0 + u + 1)
                step(v.tensor_reduce(nmax[:, 4 + r:5 + r], L.score[r][:, NCTX:NK0], AX.X, ALU.max, negate=True))
                step.wait()
                inc(v.scalar_tensor_tensor(nmax[:, r:r + 1], nmax[:, 2 + r:3 + r], -1.0, nmax[:, 4 + r:5 + r], ALU.mult,
                                           ALU.min), "maxed")
            else:
                dve.wait_ge(s["scored"], U0 + u + 1)
                first(dve, "expd", U0 + u - 1)
                inc(v.tensor_reduce(nmax[:, r:r + 1], L.score[r], AX.X, ALU.max, negate=True), "maxed")

        def attention(L, b, C, filler=None):
            U0, K0 = UNITS * C, BLOCKS * C
            G0 = L.ng * UNITS * C if L.layer == 0 else 32 * C + 32

            def split(u):
                for g_ in range(L.ng):
                    dve.wait_ge(s["p_hi"], G0 + L.ng * u + g_ + 1)
                    hi, lo = (L.pt[j][:, (u // 2) % 2, 4 * g_:4 * g_ + 4, (u % 2) * P:(u % 2) * P + P] for j in range(2))
                    turned = L.turn(u, g_).rearrange("p (t n) -> p t n", t=4)
                    inc(v.tensor_tensor(lo, turned, hi.bitcast(F32), ALU.subtract), "p_lo")

            def out_sum(k):
                p, qh, h = k // 4, (k // 2) % 2, k % 2
                dve.wait_ge(s["o_tmp"], K0 + k + 1)
                if k == 0:
                    first(dve, "at_hi", 2 * C)
                rows = slice(DH * h, DH * h + DH)
                inc(v.tensor_tensor(at32[rows, p, qh * 256:qh * 256 + 256], PS[DH:P, 7, 0:256], L.tmp[rows, k % 2, :],
                                    ALU.add), "o_sum")

            def spread_sums():
                dve.wait_ge(s["expd"], U0 + UNITS)
                inc(v.reciprocal(rr[:, 0:UNITS], sums[:, 0:UNITS]), "rsum")
                dve.wait_ge(s["rsum"], C + 1)
                dve.wait_ge(s["turned"], G0 + L.ng * UNITS)
                for p in range(2):
                    for qh in range(2):
                        src = rr[:, 8 * p + 4 * qh:8 * p + 4 * qh + 4].rearrange("p (h q) -> p q h", h=2)
                        dst = FA[:, 512 * p + 256 * qh:512 * p + 256 * qh + 256].rearrange("p (q h c) -> p q h c", q=2, h=2)
                        last = v.tensor_copy(dst, src.unsqueeze(3).to_broadcast([P, 2, 2, DH]))
                    inc(last, "rspread")

            if L.layer == 0:
                maximum(L, C, 0)
            for u in range(UNITS + 3):
                if u + 1 < UNITS:
                    maximum(L, C, u + 1)
                if u >= 4 and u % 2 == 0:
                    out_sum(u // 2 - 2)
                if u < UNITS:
                    split(u)
                if u == UNITS:
                    spread_sums()
                if filler:
                    filler(u)

        def out_norm(L, C):
            dve.wait_ge(s["o_sum"], BLOCKS * C + BLOCKS)
            for p in range(2):
                dve.wait_ge(s["rbc"], 2 * C + p + 1)
                inc(v.tensor_tensor(at32[:, p, :], PS[:, 2 + 3 * p, :], at32[:, p, :], ALU.mult), "at_norm")

        def out_lo(L, b, C):
            for p in range(2):
                dve.wait_ge(s["at_hi"], 2 * C + p + 1)
                inc(v.tensor_tensor(L.at[b][1][:, p, :], at32[:, p, :], L.at[b][0][:, p, :].bitcast(F32), ALU.subtract), "at_lo")

        def out_add(L, b, C):
            first(dve, "x_att", 2 * C)
            for w in range(2):
                dve.wait_ge(s["wo_done"], 2 * C + w + 1)
                xt = x[:, b * TT + 2 * w:b * TT + 2 * w + 2, :].rearrange("p t n -> p (t n)")
                inc(v.scalar_tensor_tensor(xt, PS[:, 6 + w, :], tg[:, L.layer:L.layer + 1], xt, ALU.mult, ALU.add), "x_att")

        dve.wait_ge(s["cst_in"], 80)
        dve.wait_ge(s["gates"], 1)
        s0 = CONST.index("s0")
        step(v.tensor_scalar(tg[:, 4:5], cst[:, s0:s0 + 1], 4.0, None, ALU.mult))
        step(v.tensor_scalar(tg[:, 5:6], cst[:, s0 + 1:s0 + 2], 2.0, None, ALU.mult))
        step(v.tensor_tensor(tg[:, 6:7], cst[:, s0 + 2:s0 + 3], tg[:, 2:3], ALU.mult))
        q_ = CONST.index("qn")
        step(v.tensor_scalar(tg[:, 7:8], cst[:, q_:q_ + 1], SCALE, None, ALU.mult))

        def latents_lo(b):
            for kt in range(KT):
                dve.wait_ge(s["ln_hi"], 2 * b + kt + 1)
                inc(v.tensor_tensor(LNL0[:, kt, :], latent_aff[b][kt],
                                    LNH0[:, kt, :].bitcast(F32), ALU.subtract), "ln_lo")

        def context_lo(b, i):
            gg, kt = i // 2, i % 2
            rows = P if kt == 0 else DC1
            cols = slice(gg * 512, gg * 512 + 512)
            dve.wait_ge(s["cx_hi"], 4 * b + i + 1)
            inc(v.tensor_tensor(XC0[1][0:rows, kt, cols], ctx_aff[b][kt][0:rows, :],
                                XC0[0][0:rows, kt, cols].bitcast(F32), ALU.subtract), "cx_lo")

        def mask_bias(b):
            dve.wait_ge(s["mask_in"], 16 * (b + 1))
            inc(v.tensor_scalar(maskbias, mask8, BIG, -BIG, ALU.mult, ALU.add), "maskbias_ready")

        dve.wait_ge(s["x_in0"], 16)
        norm(1, x_tiles(0))
        context_statistics(0)
        dve.wait_ge(s["ln_xn"], 1)
        norm_statistics(lambda t: xn[t])
        norm_apply(2, lambda t: xn[t])
        context_apply(0)
        dve.wait_ge(s["bo_in"], 16)
        inc(v.tensor_scalar(bo[:, :], bo[:, :], tg[:, 0:1], None, ALU.mult), "bo_gated")
        mask_bias(0)
        latents_lo(0)
        for i in range(4):
            context_lo(0, i)
        for b in range(NB):
            if b == 0:
                dve.wait_ge(s["x_in1"], 16)
                dve.wait_ge(s["w0_split"], 3)
                norm_statistics(x_tiles(1))
                context_statistics(1)
                norm_apply(3, x_tiles(1), early)
                dve.wait_ge(s["ln_xn"], 3)
                norm_statistics(lambda t: early[t])
                context_apply(1)
                norm_apply(4, lambda t: early[t], early)
            else:
                dve.wait_ge(s["x_att"], 2)
                dve.wait_ge(s["ln_turned"], NB)
                norm(2 * NB + 1, x_tiles(0), early)
            dve.wait_ge(s["qk0_norm"], b + 1)
            step(v.tensor_scalar(rr[:, 64:128], rr[:, 64:128], 1e-8, None, ALU.max))
            step.wait()
            inc(v.reciprocal(rr[:, 0:64], rr[:, 64:128]), "qk0_rr")
            dve.wait_ge(s["qk0_rr"], b + 1)

            def value_lo(t):
                dve.wait_ge(s["v0_hi"], 12 * b + t + 1)
                inc(v.tensor_tensor(L0.v[:, t, :, DH:P], PS[:, 5 + t % 3, 0:256].rearrange("p (h c) -> p h c", h=HG),
                                    L0.v[:, t, :, 0:DH].bitcast(F32), ALU.subtract), "v0_lo")

            def spread(i):
                if i >= 2:
                    dve.wait_ge(s["qk0_rb"], 8 * b + i - 1)
                c = 1792 + 512 * (i % 2)
                inc(v.tensor_copy(FB[:, c:c + 512].rearrange("p (n c) -> p n c", c=DH),
                                  rr[:, 8 * i:8 * i + 8].unsqueeze(2).to_broadcast([P, 8, DH])), "qk0_spread")

            spread(0)
            for t in range(3):
                value_lo(t)
            for i in range(8 + 1):
                if i + 1 < 8:
                    spread(i + 1)
                if i < 8:
                    dve.wait_ge(s["qk0_rb"], 8 * b + i + 1)
                    gain = tg[:, 7:8] if i < 2 else cst[:, q_ + 1:q_ + 2]
                    raw = FA[:, 512 * i:512 * i + 512]
                    inc(v.scalar_tensor_tensor(raw, raw, gain, PS[:, i % 4, :], ALU.mult, ALU.mult), "qk0_scaled")
                if i == 8:
                    value_lo(3 + i)
                if i >= 1:
                    dve.wait_ge(s["qk0_hi"], 8 * b + i)
                    inc(key_low(v, i - 1, 0), "qk0_lo")
                if i < 8:
                    value_lo(3 + i)
            dve.wait_ge(s["bo_added"], b + 1)

            def next_norm(u):
                if u == UNITS + 1:
                    if b == 0:
                        latents_lo(1)
                    else:
                        split_norm(NB + 1, 0)

            attention(L0, b, b, next_norm)
            out_norm(L0, b)
            out_lo(L0, b, b)
            if b == 0:
                for i in range(4):
                    context_lo(1, i)
                mask_bias(1)
            else:
                dve.wait_ge(s["k0_in"], 16)
                for kt in range(KT):
                    inc(v.tensor_tensor(fw0[:, kt, :], k0b[:, kt, :], k0b[:, KT + kt, :], ALU.subtract), "fw0_ready")
            out_add(L0, b, b)

        dve.wait_ge(s["x_att"], 4)
        norm(2 * NB + 2, x_tiles(1))

        def ffn_split(j, r, hi, lo):
            dve.wait_ge(s["f_act"], j + 1)
            inc(v.tensor_copy(hi, hf[:, r, :]), "f_hi")
            dve.wait_ge(s["f_hi"], j + 1)
            inc(v.tensor_tensor(lo, hf[:, r, :], hi.bitcast(F32), ALU.subtract), "f_lo")

        for j in range(2 * MT):
            h, m = j // MT, j % MT
            if j == 6:
                split_norm(NB + 2, 1)
            ffn_split(j, j % 2, h1[0][:, m, h * 512:h * 512 + 512], h1[1][:, m, h * 512:h * 512 + 512])
        with dve.Fori(0, MT // 2) as i:
            for c in range(4):
                dve.wait_ge(s["f3_done"], AHEAD_F3 + 4 * i + c - 1)
                ffn_split(2 * MT + 4 * i + c, c % 2, fh2[:, c % 2, 0, :], fh2[:, c % 2, 1, :])
        def x_update(gate, name, banks=range(4)):
            for w in banks:
                xt = x[:, 2 * w:2 * w + 2, :].rearrange("p t n -> p (t n)")
                last = v.scalar_tensor_tensor(xt, PS[:, 4 + w, :], tg[:, gate:gate + 1], xt, ALU.mult, ALU.add)
                if name == "out_ready":
                    last.then_inc(s[name], 2)
            return last

        def project_lo(J0, jobs, order=range(14), banks=PROJ_BANKS):
            for n in jobs:
                j = order[n]
                dve.wait_ge(s["pj_hi"], J0 + n + 1)
                if j in (4, 5):
                    dve.wait_ge(s["pj_lo"], J0 + n)
                    dve.sem_inc(s["pj_lo"], 1)
                    continue
                src = PS[:, banks[n], :]
                if j < 6:
                    for h, (rows, other) in enumerate(halves):
                        if j < 2:
                            ins = v.scalar_tensor_tensor(L1.q_lo[rows, j, :], src[rows, :], SCALE,
                                                         L1.q[rows, 2 * j + h, :].bitcast(F32), ALU.mult, ALU.subtract)
                        else:
                            p, cols = (j - 2) // 2, slice((j - 2) % 2 * 512, (j - 2) % 2 * 512 + 512)
                            ins = v.tensor_tensor(L1.k[other, 2 * p + h, cols], src[rows, :],
                                                  L1.k[rows, 2 * p + h, cols].bitcast(F32), ALU.subtract)
                else:
                    ins = v.tensor_tensor(L1.v[:, j - 6, :, DH:P], src[:, 0:256].rearrange("p (h c) -> p h c", h=HG),
                                          L1.v[:, j - 6, :, 0:DH].bitcast(F32), ALU.subtract)
                inc(ins, "pj_lo")

        def heads(g_, more):
            for b in range(NB):
                C = 2 * g_ + b + 2
                nxt = b == 0 or more
                J1 = 28 * g_ + 14 * (b + 1)

                def next_projections(u):
                    project_lo(J1, {UNITS: range(2), UNITS + 1: range(2, 4)}.get(u, ()))

                def next_norm(u):
                    if u == 1:
                        dve.wait_ge(s["x_att"], 2 * C)
                        norm_statistics(x_tiles(0))
                    elif u == 4:
                        dve.wait_ge(s["k_lo"], 4 * (C - 1))
                        norm_apply(4 * NB + 1, x_tiles(0), late0)

                attention(L1, b, C, next_projections if nxt else next_norm)
                if not nxt:
                    split_norm(3 * NB + 1, 0)
                if nxt:
                    project_lo(J1, range(4, 6))
                out_norm(L1, C)
                if nxt:
                    project_lo(J1, range(6, 8))
                    maximum(L1, C + 1, 0)
                    project_lo(J1, range(8, 10))
                out_lo(L1, b, C)
                if nxt:
                    project_lo(J1, range(10, 14))
                out_add(L1, b, C)

        dve.wait_ge(s["bo_in"], 32)
        inc(v.tensor_scalar(bo[:, :], bo[:, :], tg[:, 1:2], None, ALU.mult), "bo_gated")
        def ffn_out(b):
            dve.wait_ge(s["f3_done"], AHEAD_F3 + 2 * MT - 1 + b)
            inc(x_update(6, "x_ffn", range(2 * b, 2 * b + 2)), "x_ffn")

        ffn_out(0)
        dve.wait_ge(s["x_ffn"], 1)
        dve.wait_ge(s["ln_turned"], 2 * NB)
        norm(3 * NB + 1, x_tiles(0))
        project_lo(0, range(4), FIRST_ORDER, FIRST_BANKS)
        ffn_out(1)
        project_lo(0, range(4, 12), FIRST_ORDER, FIRST_BANKS)
        split_norm(2 * NB + 1, 0)
        project_lo(0, range(12, 14), FIRST_ORDER, FIRST_BANKS)
        dve.wait_ge(s["x_ffn"], 2)
        norm_statistics(x_tiles(1))
        dve.wait_ge(s["ln_turned"], 2 * NB + 1)
        norm_apply(3 * NB + 2, x_tiles(1))
        maximum(L1, NB, 0)
        split_norm(2 * NB + 2, 1, SPARE_BANKS)
        dve.wait_ge(s["bo_added"], 2 * NB)
        with dve.Fori(0, NG1 - 1) as g_:
            heads(g_, True)
        heads(NG1 - 1, False)
        def job(j, c, comb_seen):
            r, h = c // 2, c % 2
            dve.wait_ge(s["u_done"], j + 1)
            if comb_seen is not None:
                dve.wait_ge(s[f"comb_in{r}"], comb_seen)
            inc(v.tensor_tensor(hcomb[:, h, :], PS[:, 2 * h + 1, :], comb[:, r, h * 512:h * 512 + 512], ALU.mult), "e_comb")
            dve.wait_ge(s["e_comb"], j + 1)
            dve.wait_ge(s["e_silu"], j + 1)
            inc(v.tensor_tensor(hful[:, h, :], hcomb[:, h, :], silu[:, h, :], ALU.mult), "e_full")

        def job_low(j, c):
            h = c % 2
            dve.wait_ge(s["e_hi"], j + 1)
            inc(v.tensor_tensor(eh[:, h, 1, :], hful[:, h, :], eh[:, h, 0, :].bitcast(F32), ALU.subtract), "e_lo")

        dve.wait_ge(s["x_att"], 4 + 4 * NG1)
        dve.wait_ge(s["ln_turned"], 3 * NB + 1)
        norm(4 * NB + 2, x_tiles(1), late1)
        dve.wait_ge(s["ones_set"], 1)
        job(0, 0, None)
        job_low(0, 0)
        split_norm(3 * NB + 2, 1)

        NT = NB * TT
        dve.wait_ge(s["gate_sig"], 1)
        sig = wst[:, 1728:1856].rearrange("p (t e) -> p t e", t=NT)
        biased = RT[:, 0:128].rearrange("p (t e) -> p t e", t=NT)
        expert_bias = cst[:, 20:36].unsqueeze(1).to_broadcast([P, NT, E])
        ids = cst[:, 36:52]

        def do(ins):
            step(ins)
            step.wait()

        do(v.tensor_tensor(biased, sig, expert_bias, ALU.add))
        quad = RT[:, 0:128].rearrange("p (a b c) -> p a b c", b=2, c=2)
        hi2 = RT[:, 128:192].rearrange("p (a b) -> p a b", b=2)
        lo2 = RT[:, 192:256].rearrange("p (a b) -> p a b", b=2)
        do(v.tensor_tensor(hi2, quad[:, :, :, 0], quad[:, :, :, 1], ALU.max))
        do(v.tensor_tensor(lo2, quad[:, :, :, 0], quad[:, :, :, 1], ALU.min))
        top, mid, low, grp = (RT[:, 256 + 32 * k:288 + 32 * k] for k in range(4))
        do(v.tensor_tensor(top, hi2[:, :, 0], hi2[:, :, 1], ALU.max))
        do(v.tensor_tensor(mid, hi2[:, :, 0], hi2[:, :, 1], ALU.min))
        do(v.tensor_tensor(low, lo2[:, :, 0], lo2[:, :, 1], ALU.max))
        do(v.tensor_tensor(mid, mid, low, ALU.max))
        do(v.tensor_tensor(grp, top, mid, ALU.add))
        job(1, 1, None)
        better = RT[:, 384:512].rearrange("p (k t g) -> p k t g", k=4, t=NT)
        do(v.memset(RT[:, 384:512], 0.0))
        g4 = grp.rearrange("p (t g) -> p t g", t=NT)
        for k in range(4):
            if k:
                do(v.tensor_tensor(better[:, k, :, 0:k], g4[:, :, k:k + 1].to_broadcast([P, NT, k]), g4[:, :, 0:k],
                                   ALU.is_gt))
            if k < 3:
                do(v.tensor_tensor(better[:, k, :, k + 1:4], g4[:, :, k:k + 1].to_broadcast([P, NT, 3 - k]),
                                   g4[:, :, k + 1:4], ALU.is_ge))
        rank = RT[:, 512:544]
        do(v.tensor_reduce(rank, RT[:, 384:512].rearrange("p (k n) -> p n k", k=4), AX.X, ALU.add))
        do(v.tensor_scalar(rank, rank, 2.0, None, ALU.is_lt))
        do(v.tensor_scalar(rank, rank, BIG, -BIG, ALU.mult, ALU.add))
        job_low(1, 1)
        masked = RT[:, 576:704]
        do(v.tensor_tensor(masked.rearrange("p (n j) -> p n j", j=4), RT[:, 0:128].rearrange("p (n j) -> p n j", j=4),
                           rank.unsqueeze(2).to_broadcast([P, 32, 4]), ALU.add))
        best = RT[:, 704:768]
        index = RT[:, 128:192]
        for t in range(NT):
            last = v.max(best[:, 8 * t:8 * t + 8], masked[:, E * t:E * t + E])
        do(last)
        for t in range(NT):
            last = v.max_index(index[:, 8 * t:8 * t + 8].bitcast(U32), best[:, 8 * t:8 * t + 8], masked[:, E * t:E * t + E])
        do(last)
        do(v.tensor_copy(best, index.bitcast(U32)))
        job(2, 2, None)
        chosen = FA[:, 2048:2560].rearrange("p (t k e) -> p t k e", t=NT, k=4)
        for t in range(NT):
            last = v.tensor_tensor(chosen[:, t], best[:, 8 * t:8 * t + 4].unsqueeze(2).to_broadcast([P, 4, E]),
                                   ids.unsqueeze(1).to_broadcast([P, 4, E]), ALU.is_equal)
        do(last)
        job_low(2, 2)
        pick = RT[:, 384:512].rearrange("p (t e) -> p t e", t=NT)
        do(v.tensor_reduce(pick, chosen.rearrange("p t k e -> p t e k"), AX.X, ALU.add))
        do(v.tensor_tensor(pick, pick, sig, ALU.mult))
        den = RT[:, 544:552]
        do(v.tensor_reduce(den, pick, AX.X, ALU.add))
        do(v.tensor_scalar(den, den, 1e-20, None, ALU.add))
        do(v.reciprocal(RT[:, 552:560], den))
        do(v.tensor_scalar(RT[:, 552:560], RT[:, 552:560], 2.5, None, ALU.mult))
        inc(v.tensor_tensor(wst[:, 1600:1728].rearrange("p (t e) -> p t e", t=NT), pick,
                            RT[:, 552:560].unsqueeze(2).to_broadcast([P, NT, E]), ALU.mult), "rt_comb")
        job(3, 3, None)
        dve.wait_ge(s["rt_turned"], 1)
        for w in range(2):
            inc(v.tensor_copy(comb_rows[w], PS[0:E, w, :]), "rt_copied")
        job_low(3, 3)

        with dve.Fori(1, ET // 2) as i:
            for c in range(4):
                job(4 * i + c, c, 32 * i)
                job_low(4 * i + c, c)
        for b in range(NB):
            dve.wait_ge(s["e_y"], AHEAD_Y + 2 * ET - 1 + b)
            x_update(3, "out_ready", range(2 * b, 2 * b + 2))



def kernel(**inputs):
    import numpy as np
    import concourse.bacc as bacc
    from concourse.bass_utils import run_bass_kernel_spmd

    a = {k: np.asarray(v) for k, v in inputs.items()}

    def pack(*parts):
        out = []
        for w in parts:
            rows, cols = w.shape
            tiles = -(-rows // 128)
            full = np.zeros((tiles * 128, cols), w.dtype)
            full[:rows] = w
            if rows == DC:
                full[rows:] = w[128:]
            out.append(full.reshape(tiles, 128, cols).transpose(1, 0, 2).reshape(128, tiles * cols))
        return np.concatenate(out, axis=1)

    w0 = pack(a["L0_xattn_Wq"].T, a["L0_xattn_Wlkv"].T, a["L0_xattn_Wkv"].T, a["L0_xattn_Wo"].T)
    w1 = np.stack([pack(*[a[f"L1_xattn_{n}"][:, 256 * g:256 * g + 256] for n in ("Wq", "Wk", "Wv")],
                        a["L1_xattn_Wo"][256 * g:256 * g + 256]) for g in range(4)])

    def experts(routed, shared):
        pad = np.zeros((-len(shared) % 128, D), shared.dtype)
        return np.concatenate([shared, pad, routed.reshape(E * EI, D)]).T

    g_in, u_in = experts(a["L1_ffn_w1"], a["L1_ffn_ws1"]), experts(a["L1_ffn_w3"], a["L1_ffn_ws3"])
    y_out = experts(a["L1_ffn_w2"].transpose(0, 2, 1), a["L1_ffn_ws2"].T).T
    we = np.stack([pack(g_in[:, 128 * j:128 * j + 128], u_in[:, 128 * j:128 * j + 128], y_out[128 * j:128 * j + 128])
                   for j in range(ET)])
    k1 = np.stack([pack(a["L0_ffn_k1"][:, 128 * m:128 * m + 128]) for m in range(MT)])
    k2 = a["L0_ffn_k2"].reshape(MT, 128, D)

    def column(v):
        full = np.zeros(128, np.float32)
        full[:len(v)] = v
        return full

    def same(v):
        return np.broadcast_to(v, 128)

    cst = np.stack([column(a["L0_xattn_ln_x_g"][:128]), column(a["L0_xattn_ln_x_g"][128:]),
                    column(a["L0_xattn_ln_x_b"][:128]), column(a["L0_xattn_ln_x_b"][128:]),
                    a["L0_xattn_ln_l_g"][:128], a["L0_xattn_ln_l_g"][128:],
                    a["L0_xattn_ln_l_b"][:128], a["L0_xattn_ln_l_b"][128:],
                    np.tile(a["L0_xattn_qn_g"], 2), np.tile(a["L0_xattn_kn_g"], 2),
                    same(a["L0_ffn_s0"]), same(a["L0_ffn_s1"]), same(a["L0_ffn_s2"]),
                    same(a["g_xattn"][0]), same(a["g_xattn"][1]), same(a["g_ffn"][0]), same(a["g_ffn"][1])], axis=1)
    half_ones = np.zeros((128, 2), np.float32)
    half_ones[:DH, 0] = half_ones[DH:, 1] = 1 / DH
    arrays = {
        "x": a["x"], "ctx": a["ctx_768"], "ctxT": a["ctx_768"].reshape(NB * NCTX, DC).T,
        "mask": a["mask_BxS2_bk0"],
        "cst": cst, "bo": np.stack([a["L0_xattn_bo"], a["L1_xattn_bo"]]), "gbias": a["L1_ffn_gate_bias"],
        "w0": w0, "k0": a["L0_ffn_k0"], "k1": k1, "k2": k2,
        "w1": w1, "gw": pack(a["L1_ffn_gate_w"].T), "we": we, "eye": np.eye(128, dtype=np.float32),
        "ones": half_ones, "iota": np.arange(E, dtype=np.float32),
    }
    arrays = {f"{k}_in": np.ascontiguousarray(v) for k, v in arrays.items()}
    nc = bacc.Bacc("TRN2", target_bir_lowering=False, num_devices=1)
    args = [nc.dram_tensor(k, v.shape, mybir.dt.from_np(v.dtype), kind="ExternalInput").ap() for k, v in arrays.items()]
    out = nc.dram_tensor("out", (NB, S, D), F32, kind="ExternalOutput").ap()
    comb = nc.dram_tensor("comb", (3 * E, NB * S), F32, kind="Internal").ap()
    build(nc, *args, out, comb)
    result = run_bass_kernel_spmd(nc, [arrays], core_ids=[0])
    return result.results[0]["out"]
```
